# Optimizing a Trainium2 kernel written in Bass

```python
import numpy as np
import jax
import jax.numpy as jnp

def _softmax(x, axis=-1):
    return jax.nn.softmax(x, axis=axis)

def _gelu(x):
    return jax.nn.gelu(x, approximate=True)

def _silu(x):
    return jax.nn.silu(x)

def _sigmoid(x):
    return jax.nn.sigmoid(x)

def _layernorm(x, axis=-1, eps=1e-05):
    m = jnp.mean(x, axis=axis, keepdims=True)
    v = jnp.var(x, axis=axis, keepdims=True)
    return (x - m) / jnp.sqrt(v + eps)

def _scatter_add(tgt, idx, src, axis=0):
    return tgt.at[idx].add(src)

def _segment_sum(src, seg, n):
    return jax.ops.segment_sum(src, seg, n)
kernel_name = 'mk_lm_tower_d2_tok_ids512_r4_5a3b27'

def setup_inputs(seed: int=0):
    np.random.seed(seed)
    _w = jnp.asarray

    def _rec_inputs():
        import jax
        import jax.numpy as jnp
        _rk = jax.random.key(seed)
        x = jax.random.randint(jax.random.fold_in(_rk, 1), (1, 2048), 0, 8000, jnp.int32)
        return x
    x = _rec_inputs()

    def _L0_tok_setup():
        import jax, jax.numpy as jnp
        import numpy as np
        VOCAB = 8000
        EMB = 128
        K = 3
        B, T = (8, 1024)
        key = jax.random.key(seed)
        k_ids, k_w = jax.random.split(key)
        token_ids = jax.random.randint(k_ids, (B, T), 0, VOCAB, dtype=jnp.int64)
        conv_w = jax.random.normal(k_w, (EMB, VOCAB, K), dtype=jnp.float32) * 0.02
        return {'token_ids': token_ids, 'conv_w': conv_w}
    _L0_tok_all = _L0_tok_setup()
    _L0_tok_in = {k: v for k, v in _L0_tok_all.items() if k in ('conv_w',)}
    del _L0_tok_all

    def _L0_attn_setup():
        import jax, jax.numpy as jnp
        import numpy as np
        B, S, D, MULT, K, EPS = (8, 512, 128, 4, 9, 1e-06)

        def _rglru(x, Wi, bi, Wr, br, lam):
            r = jax.nn.sigmoid(x @ Wr + br)
            i = jax.nn.sigmoid(x @ Wi + bi)
            log_a = -8.0 * jax.nn.softplus(lam) * r
            a = jnp.exp(log_a)
            b = jnp.sqrt(1.0 - jnp.exp(2.0 * log_a)) * (i * x)

            def combine(e1, e2):
                a1, b1 = e1
                a2, b2 = e2
                return (a1 * a2, a2 * b1 + b2)
            _, h = jax.lax.associative_scan(combine, (a, b), axis=1)
            return h

        def _conv1d(x_cdS, w_oik, b_o, pad):
            y = jax.lax.conv_general_dilated(x_cdS, w_oik, window_strides=(1,), padding=[pad], dimension_numbers=('NCH', 'OIH', 'NCH'))
            return y + b_o[None, :, None]
        key = jax.random.key(seed)
        ks = jax.random.split(key, 12)
        w = lambda k, shape, s=0.02: jax.random.normal(k, shape, dtype=jnp.float32) * s
        return dict(x=jax.random.normal(ks[0], (B, S, D), dtype=jnp.float32), g=jnp.ones((D,), jnp.float32), W1=w(ks[1], (D, D)), b1=jnp.zeros((D,), jnp.float32), W2=w(ks[2], (D, D)), b2=jnp.zeros((D,), jnp.float32), dw_w=w(ks[3], (D, D, K)), dw_b=jnp.zeros((D,), jnp.float32), pw_w=w(ks[4], (D, D, 1)), pw_b=jnp.zeros((D,), jnp.float32), Wi=w(ks[5], (D, D)), bi=jnp.zeros((D,), jnp.float32), Wr=w(ks[6], (D, D)), br=jnp.zeros((D,), jnp.float32), lam=jax.random.normal(ks[7], (D,), dtype=jnp.float32), Wm1=w(ks[8], (D, D * MULT)), bm1=jnp.zeros((D * MULT,), jnp.float32), Wm2=w(ks[9], (D * MULT, D)), bm2=jnp.zeros((D,), jnp.float32))
    _L0_attn_all = _L0_attn_setup()
    _L0_attn_in = {k: v for k, v in _L0_attn_all.items() if k in ('g', 'W1', 'b1', 'W2', 'b2', 'dw_w', 'dw_b', 'pw_w', 'pw_b', 'Wi', 'bi', 'Wr', 'br', 'lam', 'Wm1', 'bm1', 'Wm2', 'bm2')}
    del _L0_attn_all

    def _L0_ffn_setup():
        import jax, jax.numpy as jnp
        import numpy as np
        EPS = 1e-05
        TOP_K = 2

        def _moe_forward(x, Wg, W1, b1, W2, b2, gamma, beta):
            B, S, D = x.shape
            xf = x.reshape(-1, D)
            logits = xf @ Wg
            topv, topi = jax.lax.top_k(logits, TOP_K)
            gate_w = jax.nn.softmax(topv, axis=-1)
            h = jax.nn.relu(jnp.einsum('td,edh->teh', xf, W1) + b1[None])
            y = jnp.einsum('teh,ehd->ted', h, W2) + b2[None]
            mu = jnp.mean(y, axis=-1, keepdims=True)
            var = jnp.mean((y - mu) ** 2, axis=-1, keepdims=True)
            y = (y - mu) / jnp.sqrt(var + EPS) * gamma[None] + beta[None]
            y_sel = jnp.take_along_axis(y, topi[:, :, None], axis=1)
            out = jnp.sum(gate_w[:, :, None] * y_sel, axis=1)
            return out.reshape(B, S, D)
        key = jax.random.key(seed)
        ks = jax.random.split(key, 8)
        B, S, D, H, E = (4, 512, 128, 128, 8)
        sd = lambda fan_in: 1.0 / np.sqrt(fan_in)
        x = jax.random.normal(ks[0], (B, S, D), dtype=jnp.float32)
        Wg = jax.random.uniform(ks[1], (D, E), jnp.float32, -sd(D), sd(D))
        W1 = jax.random.uniform(ks[2], (E, D, H), jnp.float32, -sd(D), sd(D))
        b1 = jax.random.uniform(ks[3], (E, H), jnp.float32, -sd(D), sd(D))
        W2 = jax.random.uniform(ks[4], (E, H, D), jnp.float32, -sd(H), sd(H))
        b2 = jax.random.uniform(ks[5], (E, D), jnp.float32, -sd(H), sd(H))
        gamma = jnp.ones((E, D), jnp.float32)
        beta = jnp.zeros((E, D), jnp.float32)
        return {'x': x, 'Wg': Wg, 'W1': W1, 'b1': b1, 'W2': W2, 'b2': b2, 'gamma': gamma, 'beta': beta}
    _L0_ffn_all = _L0_ffn_setup()
    _L0_ffn_in = {k: v for k, v in _L0_ffn_all.items() if k in ('Wg', 'W1', 'b1', 'W2', 'b2', 'gamma', 'beta')}
    del _L0_ffn_all

    def _L1_attn_setup():
        import jax, jax.numpy as jnp
        import numpy as np
        D_MODEL = 128
        D_STATE = 64
        LN_EPS = 1e-05
        key = jax.random.key(seed)
        ks = jax.random.split(key, 8)
        B, T = (16, 1024)
        x = jax.random.normal(ks[0], (B, T, D_MODEL), dtype=jnp.float32)
        A = jax.random.normal(ks[1], (D_STATE, D_STATE), dtype=jnp.float32) * 0.01
        Bm = jax.random.normal(ks[2], (D_STATE, D_MODEL), dtype=jnp.float32) * 0.01
        Cm = jax.random.normal(ks[3], (D_MODEL, D_STATE), dtype=jnp.float32) * 0.01
        Dm = jax.random.normal(ks[4], (D_MODEL, D_MODEL), dtype=jnp.float32) * 0.01
        lim = 1.0 / np.sqrt(D_MODEL)
        Wi = jax.random.uniform(ks[5], (D_MODEL, D_MODEL), jnp.float32, -lim, lim)
        bi = jnp.zeros((D_MODEL,), jnp.float32)
        Wo = jax.random.uniform(ks[6], (D_MODEL, D_MODEL), jnp.float32, -lim, lim)
        bo = jnp.zeros((D_MODEL,), jnp.float32)
        gamma = jnp.ones((D_MODEL,), jnp.float32)
        beta = jnp.zeros((D_MODEL,), jnp.float32)
        return {'x': x, 'A': A, 'Bm': Bm, 'Cm': Cm, 'Dm': Dm, 'Wi': Wi, 'bi': bi, 'Wo': Wo, 'bo': bo, 'gamma': gamma, 'beta': beta}
    _L1_attn_all = _L1_attn_setup()
    _L1_attn_in = {k: v for k, v in _L1_attn_all.items() if k in ('A', 'Bm', 'Cm', 'Dm', 'Wi', 'bi', 'Wo', 'bo', 'gamma', 'beta')}
    del _L1_attn_all

    def _L1_ffn_setup():
        import jax, jax.numpy as jnp
        import numpy as np
        H = 128
        F = 512
        E = 16
        SHARED = 2
        TOP_K = 4
        B, S = (2, 512)

        def _mlp(x, w1, b1, w2, b2):
            return jax.nn.gelu(x @ w1 + b1, approximate=False) @ w2 + b2
        key = jax.random.key(seed)
        ks = jax.random.split(key, 10)
        sc = 0.02
        return {'hidden_states': jax.random.normal(ks[0], (B, S, H), dtype=jnp.float32), 'gate_w': jax.random.normal(ks[1], (E, H), dtype=jnp.float32) * sc, 're_w1': jax.random.normal(ks[2], (E, H, F), dtype=jnp.float32) * sc, 're_b1': jnp.zeros((E, F), dtype=jnp.float32), 're_w2': jax.random.normal(ks[3], (E, F, H), dtype=jnp.float32) * sc, 're_b2': jnp.zeros((E, H), dtype=jnp.float32), 'se_w1': jax.random.normal(ks[4], (SHARED, H, F), dtype=jnp.float32) * sc, 'se_b1': jnp.zeros((SHARED, F), dtype=jnp.float32), 'se_w2': jax.random.normal(ks[5], (SHARED, F, H), dtype=jnp.float32) * sc, 'se_b2': jnp.zeros((SHARED, H), dtype=jnp.float32)}
    _L1_ffn_all = _L1_ffn_setup()
    _L1_ffn_in = {k: v for k, v in _L1_ffn_all.items() if k in ('gate_w', 're_w1', 're_b1', 're_w2', 're_b2', 'se_w1', 'se_b1', 'se_w2', 'se_b2')}
    del _L1_ffn_all
    return {'x': x, 'L0_tok_conv_w': _L0_tok_in['conv_w'], 'L0_attn_g': _L0_attn_in['g'], 'L0_attn_W1': _L0_attn_in['W1'], 'L0_attn_b1': _L0_attn_in['b1'], 'L0_attn_W2': _L0_attn_in['W2'], 'L0_attn_b2': _L0_attn_in['b2'], 'L0_attn_dw_w': _L0_attn_in['dw_w'], 'L0_attn_dw_b': _L0_attn_in['dw_b'], 'L0_attn_pw_w': _L0_attn_in['pw_w'], 'L0_attn_pw_b': _L0_attn_in['pw_b'], 'L0_attn_Wi': _L0_attn_in['Wi'], 'L0_attn_bi': _L0_attn_in['bi'], 'L0_attn_Wr': _L0_attn_in['Wr'], 'L0_attn_br': _L0_attn_in['br'], 'L0_attn_lam': _L0_attn_in['lam'], 'L0_attn_Wm1': _L0_attn_in['Wm1'], 'L0_attn_bm1': _L0_attn_in['bm1'], 'L0_attn_Wm2': _L0_attn_in['Wm2'], 'L0_attn_bm2': _L0_attn_in['bm2'], 'L0_ffn_Wg': _L0_ffn_in['Wg'], 'L0_ffn_W1': _L0_ffn_in['W1'], 'L0_ffn_b1': _L0_ffn_in['b1'], 'L0_ffn_W2': _L0_ffn_in['W2'], 'L0_ffn_b2': _L0_ffn_in['b2'], 'L0_ffn_gamma': _L0_ffn_in['gamma'], 'L0_ffn_beta': _L0_ffn_in['beta'], 'L1_attn_A': _L1_attn_in['A'], 'L1_attn_Bm': _L1_attn_in['Bm'], 'L1_attn_Cm': _L1_attn_in['Cm'], 'L1_attn_Dm': _L1_attn_in['Dm'], 'L1_attn_Wi': _L1_attn_in['Wi'], 'L1_attn_bi': _L1_attn_in['bi'], 'L1_attn_Wo': _L1_attn_in['Wo'], 'L1_attn_bo': _L1_attn_in['bo'], 'L1_attn_gamma': _L1_attn_in['gamma'], 'L1_attn_beta': _L1_attn_in['beta'], 'L1_ffn_gate_w': _L1_ffn_in['gate_w'], 'L1_ffn_re_w1': _L1_ffn_in['re_w1'], 'L1_ffn_re_b1': _L1_ffn_in['re_b1'], 'L1_ffn_re_w2': _L1_ffn_in['re_w2'], 'L1_ffn_re_b2': _L1_ffn_in['re_b2'], 'L1_ffn_se_w1': _L1_ffn_in['se_w1'], 'L1_ffn_se_b1': _L1_ffn_in['se_b1'], 'L1_ffn_se_w2': _L1_ffn_in['se_w2'], 'L1_ffn_se_b2': _L1_ffn_in['se_b2']}

def reference(x, L0_tok_conv_w, L0_attn_g, L0_attn_W1, L0_attn_b1, L0_attn_W2, L0_attn_b2, L0_attn_dw_w, L0_attn_dw_b, L0_attn_pw_w, L0_attn_pw_b, L0_attn_Wi, L0_attn_bi, L0_attn_Wr, L0_attn_br, L0_attn_lam, L0_attn_Wm1, L0_attn_bm1, L0_attn_Wm2, L0_attn_bm2, L0_ffn_Wg, L0_ffn_W1, L0_ffn_b1, L0_ffn_W2, L0_ffn_b2, L0_ffn_gamma, L0_ffn_beta, L1_attn_A, L1_attn_Bm, L1_attn_Cm, L1_attn_Dm, L1_attn_Wi, L1_attn_bi, L1_attn_Wo, L1_attn_bo, L1_attn_gamma, L1_attn_beta, L1_ffn_gate_w, L1_ffn_re_w1, L1_ffn_re_b1, L1_ffn_re_w2, L1_ffn_re_b2, L1_ffn_se_w1, L1_ffn_se_b1, L1_ffn_se_w2, L1_ffn_se_b2):
    import jax
    import jax.numpy as jnp

    def _L0_tok_ref(token_ids, conv_w):
        import jax, jax.numpy as jnp
        import numpy as np
        VOCAB = 8000
        EMB = 128
        K = 3
        B, T = (8, 1024)
        'Equivalent to one_hot(token_ids) -> Conv1d(V->F, k=K, pad=K//2, no bias).\n\n            Because the conv input is one-hot over the vocab channel, the V-dim\n            contraction reduces to gathering one weight row per (position, tap):\n              out[b,t,f] = sum_k W[f, token[b, t+k-pad], k]   (zero outside [0,T)).\n            '
        Bn, Tn = token_ids.shape
        F_, V_, Kn = conv_w.shape
        pad = Kn // 2
        out = jnp.zeros((Bn, Tn, F_), dtype=conv_w.dtype)
        t = jnp.arange(Tn)
        for k in range(Kn):
            shift = k - pad
            src = t + shift
            valid = (src >= 0) & (src < Tn)
            src_c = jnp.clip(src, 0, Tn - 1)
            ids = token_ids[:, src_c]
            table_k = conv_w[:, :, k].T
            emb = table_k[ids]
            out = out + jnp.where(valid[None, :, None], emb, jnp.zeros((), conv_w.dtype))
        return out

    def _L0_attn_ref(x, g, W1, b1, W2, b2, dw_w, dw_b, pw_w, pw_b, Wi, bi, Wr, br, lam, Wm1, bm1, Wm2, bm2):
        import jax, jax.numpy as jnp
        import numpy as np
        B, S, D, MULT, K, EPS = (8, 512, 128, 4, 9, 1e-06)

        def _rglru(x, Wi, bi, Wr, br, lam):
            r = jax.nn.sigmoid(x @ Wr + br)
            i = jax.nn.sigmoid(x @ Wi + bi)
            log_a = -8.0 * jax.nn.softplus(lam) * r
            a = jnp.exp(log_a)
            b = jnp.sqrt(1.0 - jnp.exp(2.0 * log_a)) * (i * x)

            def combine(e1, e2):
                a1, b1 = e1
                a2, b2 = e2
                return (a1 * a2, a2 * b1 + b2)
            _, h = jax.lax.associative_scan(combine, (a, b), axis=1)
            return h

        def _conv1d(x_cdS, w_oik, b_o, pad):
            y = jax.lax.conv_general_dilated(x_cdS, w_oik, window_strides=(1,), padding=[pad], dimension_numbers=('NCH', 'OIH', 'NCH'))
            return y + b_o[None, :, None]
        scale = jnp.sqrt(jnp.float32(D))

        def rms(t):
            n = jnp.linalg.norm(t, axis=-1, keepdims=True) + EPS
            return t / n * scale * g
        skip = x
        xn = rms(x)
        l1 = xn @ W1 + b1
        l2 = xn @ W2 + b2
        c = jnp.transpose(l1, (0, 2, 1))
        c = _conv1d(c, dw_w, dw_b, (K // 2, K // 2))
        c = _conv1d(c, pw_w, pw_b, (0, 0))
        l1 = jnp.transpose(c, (0, 2, 1))
        l1 = _rglru(l1, Wi, bi, Wr, br, lam)
        x1 = l1 * jax.nn.gelu(l2, approximate=False) + skip
        skip2 = x1
        xn2 = rms(x1)
        h = xn2 @ Wm1 + bm1
        out = jax.nn.gelu(h, approximate=False) * h @ Wm2 + bm2 + skip2
        return out

    def _L0_ffn_ref(x, Wg, W1, b1, W2, b2, gamma, beta):
        import jax, jax.numpy as jnp
        import numpy as np
        EPS = 1e-05
        TOP_K = 2

        def _moe_forward(x, Wg, W1, b1, W2, b2, gamma, beta):
            B, S, D = x.shape
            xf = x.reshape(-1, D)
            logits = xf @ Wg
            topv, topi = jax.lax.top_k(logits, TOP_K)
            gate_w = jax.nn.softmax(topv, axis=-1)
            h = jax.nn.relu(jnp.einsum('td,edh->teh', xf, W1) + b1[None])
            y = jnp.einsum('teh,ehd->ted', h, W2) + b2[None]
            mu = jnp.mean(y, axis=-1, keepdims=True)
            var = jnp.mean((y - mu) ** 2, axis=-1, keepdims=True)
            y = (y - mu) / jnp.sqrt(var + EPS) * gamma[None] + beta[None]
            y_sel = jnp.take_along_axis(y, topi[:, :, None], axis=1)
            out = jnp.sum(gate_w[:, :, None] * y_sel, axis=1)
            return out.reshape(B, S, D)
        return _moe_forward(x, Wg, W1, b1, W2, b2, gamma, beta)

    def _L1_attn_ref(x, A, Bm, Cm, Dm, Wi, bi, Wo, bo, gamma, beta):
        import jax, jax.numpy as jnp
        import numpy as np
        D_MODEL = 128
        D_STATE = 64
        LN_EPS = 1e-05
        h = x @ Wi.T + bi
        mu = jnp.mean(h, axis=-1, keepdims=True)
        var = jnp.mean(jnp.square(h - mu), axis=-1, keepdims=True)
        h = (h - mu) * jax.lax.rsqrt(var + LN_EPS) * gamma + beta
        Bsz = h.shape[0]
        s0 = jnp.zeros((Bsz, D_STATE), h.dtype)

        def step(s, xt):
            s = s @ A.T + xt @ Bm.T
            out = s @ Cm.T + xt @ Dm.T
            return (s, out)
        _, outs = jax.lax.scan(step, s0, jnp.swapaxes(h, 0, 1))
        y = jnp.swapaxes(outs, 0, 1)
        return y @ Wo.T + bo

    def _L1_ffn_ref(hidden_states, gate_w, re_w1, re_b1, re_w2, re_b2, se_w1, se_b1, se_w2, se_b2):
        import jax, jax.numpy as jnp
        import numpy as np
        H = 128
        F = 512
        E = 16
        SHARED = 2
        TOP_K = 4
        B, S = (2, 512)

        def _mlp(x, w1, b1, w2, b2):
            return jax.nn.gelu(x @ w1 + b1, approximate=False) @ w2 + b2
        b, s, h = hidden_states.shape
        x = hidden_states.reshape(-1, h)
        gate_probs = jax.nn.softmax(x @ gate_w.T, axis=-1)
        top_v, top_i = jax.lax.top_k(gate_probs, TOP_K)
        top_v = jax.nn.softmax(top_v, axis=-1)
        combine = jnp.einsum('tk,tke->te', top_v, jax.nn.one_hot(top_i, E, dtype=x.dtype))
        routed = jnp.zeros_like(x)
        for e in range(E):
            routed = routed + combine[:, e:e + 1] * _mlp(x, re_w1[e], re_b1[e], re_w2[e], re_b2[e])
        shared = jnp.zeros_like(x)
        for j in range(SHARED):
            shared = shared + _mlp(x, se_w1[j], se_b1[j], se_w2[j], se_b2[j])
        shared = shared / SHARED
        return (routed + shared).reshape(b, s, h)
    h = _L0_tok_ref(x, L0_tok_conv_w)
    h = h + _L0_attn_ref(_layernorm(h, axis=-1), L0_attn_g, L0_attn_W1, L0_attn_b1, L0_attn_W2, L0_attn_b2, L0_attn_dw_w, L0_attn_dw_b, L0_attn_pw_w, L0_attn_pw_b, L0_attn_Wi, L0_attn_bi, L0_attn_Wr, L0_attn_br, L0_attn_lam, L0_attn_Wm1, L0_attn_bm1, L0_attn_Wm2, L0_attn_bm2)
    h = h + _L0_ffn_ref(_layernorm(h, axis=-1), L0_ffn_Wg, L0_ffn_W1, L0_ffn_b1, L0_ffn_W2, L0_ffn_b2, L0_ffn_gamma, L0_ffn_beta)
    h = h + _L1_attn_ref(_layernorm(h, axis=-1), L1_attn_A, L1_attn_Bm, L1_attn_Cm, L1_attn_Dm, L1_attn_Wi, L1_attn_bi, L1_attn_Wo, L1_attn_bo, L1_attn_gamma, L1_attn_beta)
    h = h + _L1_ffn_ref(_layernorm(h, axis=-1), L1_ffn_gate_w, L1_ffn_re_w1, L1_ffn_re_b1, L1_ffn_re_w2, L1_ffn_re_b2, L1_ffn_se_w1, L1_ffn_se_b1, L1_ffn_se_w2, L1_ffn_se_b2)
    return h

_drawn_inputs = setup_inputs


def setup_inputs(seed=0):
    import zlib

    import numpy as np

    out = dict(_drawn_inputs(seed))
    spreads = {'L0_attn_g': (1.0, 0.2),
     'L0_attn_b1': (0.0, 0.8),
     'L0_attn_b2': (0.0, 0.1),
     'L0_attn_dw_b': (0.0, 0.585),
     'L0_attn_pw_b': (0.0, 0.1),
     'L0_attn_bi': (0.0, 0.769),
     'L0_attn_br': (0.0, 0.773),
     'L0_attn_bm1': (0.0, 0.1),
     'L0_attn_bm2': (0.0, 0.1),
     'L0_ffn_gamma': (1.0, 0.2),
     'L0_ffn_beta': (0.0, 0.1),
     'L1_attn_bi': (0.0, 0.8),
     'L1_attn_bo': (0.0, 0.1),
     'L1_attn_gamma': (1.0, 0.6),
     'L1_attn_beta': (0.0, 0.8),
     'L1_ffn_re_b1': (0.0, 0.8),
     'L1_ffn_re_b2': (0.0, 0.1),
     'L1_ffn_se_b1': (0.0, 0.569),
     'L1_ffn_se_b2': (0.0, 0.1)}
    factors = {'L0_attn_Wi': 8.0,
     'L0_attn_Wr': 7.73,
     'L0_attn_lam': 3.44,
     'L1_attn_A': 8.0,
     'L1_attn_Bm': 8.0,
     'L1_attn_Cm': 8.0,
     'L1_ffn_re_w1': 2.761}
    for name, (base, spread) in spreads.items():
        noise = np.random.default_rng([zlib.crc32(name.encode()), seed]).standard_normal(out[name].shape)
        drawn = base * np.exp(spread * noise) if base else spread * noise
        out[name] = jnp.asarray(drawn.astype(out[name].dtype))
    for name, factor in factors.items():
        out[name] = (out[name] * factor).astype(out[name].dtype)
    return out
```

```python
from contextlib import ExitStack

import concourse.bass as bass
from concourse import mybir

F32 = mybir.dt.float32
I32 = mybir.dt.int32
U32 = mybir.dt.uint32
ALU = mybir.AluOpType
ACT = mybir.ActivationFunctionType
AX = mybir.AxisListType

P = 128
T = 2048
NT = T // P
GT = 4
NG = NT // GT
GC = GT * P
TAPS0 = 3
K = 9
HALO = K // 2
MULT = 4
E0 = 8
E1 = 16
TOP1 = 4
SHARED = 2
ES = E1 + SHARED
FC = 4
NS = 64
LN_EPS = 1e-5
RMS_EPS = 1e-6
SQD = float(P) ** 0.5
SCAN_LEVELS = 7
POW_LEVELS = 4 + SCAN_LEVELS - 1

COLS = ["g", "b1", "b2", "dw_b", "pw_b", "bi", "br", "lam", "bm1_0", "bm1_1", "bm1_2", "bm1_3",
        "gamma", "beta"] + [f"moe_b1_{e}" for e in range(E0)]
ROW_BM2, ROW_BI, ROW_BO, ROW_B2, ROW_GAMMA = 0, 1, 2, 3, 3 + E0
ROWS = 3 + 2 * E0
WSLOT = FC * P + FC * P + FC


class BankQueue:

    def __init__(self, nc, ctx, name, banks, keys):
        self.banks = banks
        self.at = {key: n for n, key in enumerate(keys)}
        assert len(self.at) == len(keys)
        self.filled = ctx.enter_context(nc.semaphore(f"{name}_filled"))
        self.emptied = ctx.enter_context(nc.semaphore(f"{name}_emptied"))
        self.issued = 0

    def fill(self, pe, key):
        n = self.at[key]
        assert n == self.issued, (key, n, self.issued)
        self.issued += 1
        if n >= 2:
            pe.wait_ge(self.emptied, n - 1)
        return self.banks[n % 2]

    def full(self, eng, key):
        n = self.at[key]
        eng.wait_ge(self.filled, n + 1)
        return self.banks[n % 2]

    def taken(self, eng, key):
        eng.wait_ge(self.emptied, self.at[key] + 1)


def lm_tower_kernel(nc, ids, table, consts, cols, rows, attn_w, dw_w, wm1, wm2, moe_wg, moe_w1, moe_w2,
                    moe_beta, ssm_a, ssm_bT, ssm_c, ssm_d, ssm_wiT, ssm_woT, gate_wT, ffn_w, ffn_b2, out):
    with ExitStack() as ctx:
        def sb(name, shape, dt=F32):
            return ctx.enter_context(nc.sbuf_tensor(f"sb_{name}", shape, dt))

        def sem(name):
            return ctx.enter_context(nc.semaphore(name))

        ident = sb("ident", [P, P])
        iota = sb("iota", [P, E1])
        col = sb("col", [P, len(COLS)])
        row = sb("row", [P, ROWS * P])
        w_attn = sb("w_attn", [P, 5, P])
        w_dw = sb("w_dw", [P, K, P])
        w_m1 = sb("w_m1", [P, MULT * P])
        w_m2 = sb("w_m2", [P, MULT, P])
        w_g0 = sb("w_g0", [P, E0])
        w_e1 = sb("w_e1", [P, E0, P])
        w_e2 = sb("w_e2", [P, E0, P])
        w_beta = sb("w_beta", [E0, P])
        w_a = sb("w_a", [NS, 2 * NS])
        w_bT = sb("w_bT", [P, NS])
        w_c = sb("w_c", [P, NS])
        w_d = sb("w_d", [P, P])
        w_iT = sb("w_iT", [P, P])
        w_oT = sb("w_oT", [P, P])
        w_g1 = sb("w_g1", [P, E1])
        w_b2 = sb("w_b2", [ES, P])
        w_exp = [sb(f"w_exp{s}", [P, WSLOT]) for s in range(2)]

        def column(name):
            n = COLS.index(name)
            return col[:, n:n + 1]

        def spread_row(at, n=1):
            return row[:, at * P:(at + n) * P]

        tok = sb("tok", [P, NT + 2], I32)
        work = sb("work", [P, 8192])
        gathered = work[:, 0:(NT + 2) * TAPS0 * P].rearrange("p (j c) -> p j c", c=TAPS0 * P)
        h = sb("h", [P, NT, P])
        skip = sb("skip", [P, NT, P])
        xn = sb("xn", [P, NT, P])
        xT = sb("xT", [P, NT * P])
        lpad = sb("lpad", [P, T + 2 * HALO])
        gl = sb("gl", [P, T])
        lx = sb("lx", [P, T])
        rg = sb("rg", [P, T])
        ig = sb("ig", [P, T])
        ra = sb("ra", [P, T])
        rb = sb("rb", [P, T])
        zc = sb("zc", [P, 2, GC])
        sq = sb("sq", [P, 2, GC])
        bn = sb("bn", [P, NT, 6])
        mv = sb("mv", [P, NT, 2])
        std = sb("std", [P, NT])
        rstd = sb("rstd", [P, NT])
        nrm = sb("nrm", [P, NT])
        qs = sb("qs", [P, NT])
        lamv = sb("lamv", [P, 12])
        lg0 = sb("lg0", [P, NT, E0])
        top = sb("top", [P, NT, 8])
        topi = sb("topi", [P, NT, 8], U32)
        topf = sb("topf", [P, NT, 8])
        hot = sb("hot", [P, NT, E1])
        comb = sb("comb", [P, NT, ES])
        combT = sb("combT", [ES, NT * P])
        lg1 = sb("lg1", [P, NT, E1])
        sm = sb("sm", [P, 4, NT])
        ss = sb("ss", [P, NT, E0])
        sc = sb("sc", [P, NT, E0])
        wmean = sb("wmean", [P, 2 * E0])
        powers = sb("powers", [NS, POW_LEVELS + 1, 2 * NS])
        woC = sb("woC", [NS, P])
        woD = sb("woD", [P, P])
        qT = sb("qT", [NS, NT, P])
        st = sb("st", [NS, NT, P])
        carry = sb("carry", [NS, P + 1])
        zero = sb("zero", [P, 1])

        pst = ctx.enter_context(nc.psum_tensor("pst", [P, 8, GC], F32))
        bank = [pst[:, b, :] for b in range(8)]

        G, I = range(NG), range(NT)
        tr = BankQueue(nc, ctx, "transposed", bank[0:2],
                       [("xT_a", g) for g in G] + [("xT_b", g) for g in G] + [("xT_c", g) for g in G]
                       + [("combT0", g) for g in G] + [("xT_d", g) for g in G] + [("uT", g) for g in G]
                       + [("xT_e", g) for g in G] + [("combT1", g) for g in G])
        ma = BankQueue(nc, ctx, "for_act", bank[2:4],
                       [("l2", g) for g in G] + [(w, c) for c in G for w in ("r", "i")]
                       + [("hid0", g, e) for g in G for e in range(E0)]
                       + [("hid1", e, g, f) for e in range(ES) for g in G for f in range(FC)])
        mv_keys = [("woC",), ("woD",)]
        for i in range(NT):
            mv_keys += [("q", i)] + ([("pow", i)] if i < POW_LEVELS else [])
        mv_keys += [("l1", g) for g in G] + [(w, c) for c in G for w in ("z", "lx")]
        mv_keys += [("wm1", g, m) for g in G for m in range(MULT)]
        mv_keys += [("state", i) for i in I] + [("carry", k) for k in range(SCAN_LEVELS)]
        mq = BankQueue(nc, ctx, "for_dve", bank[4:6], mv_keys)
        tm_keys = [("pT", g) for g in G] + [("out0", g) for g in G] + [("logit0", g) for g in G]
        tm_keys += [("beta0", g) for g in G] + [("y0", i, half) for i in I for half in range(2)]
        tm_keys += [("hm", g) for g in G] + [("y_ssm", g) for g in G] + [("logit1", g) for g in G]
        tm_keys += [("b2", g) for g in G] + [("y1", e, g) for e in range(ES) for g in G]
        tm = BankQueue(nc, ctx, "token_major", bank[6:8], tm_keys)

        ld_const = sem("ld_const")
        ld_ids = sem("ld_ids")
        ld_ssm = sem("ld_ssm")
        ld_attn = sem("ld_attn")
        ld_moe = sem("ld_moe")
        ld_rows = sem("ld_rows")
        ld_exp = [sem("ld_exp0"), sem("ld_exp1")]
        emb = [sem(f"emb{g}") for g in G]
        gate0 = sem("gate0")
        dve_step = sem("dve_step")
        pool_step = sem("pool_step")
        var_ready = sem("var_ready")
        std_ready = sem("std_ready")
        x_ready = sem("x_ready")
        lam_dve = sem("lam_dve")
        lam_act = sem("lam_act")
        ix_ready = sem("ix_ready")
        decay_ready = sem("decay_ready")
        prod_ready = sem("prod_ready")
        x1_ready = sem("x1_ready")
        ssq_ready = sem("ssq_ready")
        base_ready = sem("base_ready")
        gelu_ready = sem("gelu_ready")
        hid_ready = sem("hid_ready")
        centered = sem("centered")
        exp0_ready = sem("exp0_ready")
        gate0_dve = sem("gate0_dve")
        comb0_ready = sem("comb0_ready")
        y0_ready = sem("y0_ready")
        sq0_ready = sem("sq0_ready")
        ss0_ready = sem("ss0_ready")
        sd0_ready = sem("sd0_ready")
        v0_ready = sem("v0_ready")
        moe_ready = sem("moe_ready")
        hb_ready = sem("hb_ready")
        h2_base = sem("h2_base")
        exp1_dve = sem("exp1_dve")
        exp1_act = sem("exp1_act")
        comb1_ready = sem("comb1_ready")
        acc_ready = sem("acc_ready")
        out_done = sem("out_done")

        X_A, X_B, X_C, X_D, X_U, X_E = (NG * n for n in range(6))
        V_A, V_C, V_D, V_U, V_E = (NG * n for n in range(5))

        hid0 = work[:, 0:2 * E0 * GC].rearrange("p (s e c) -> p s e c", s=2, e=E0)
        hidm = work[:, 0:2 * MULT * GC].rearrange("p (s e c) -> p s e c", s=2, e=MULT)
        hid1 = work[:, 0:2 * FC * GC].rearrange("p (s e c) -> p s e c", s=2, e=FC)

        block = ctx.enter_context(nc.Block())

        @block.sync
        def _(sp):
            sp.dma_start(tok[:], ids).then_inc(ld_ids, 16)
            for dst, src in ((w_a, ssm_a), (w_c, ssm_c), (w_d, ssm_d), (w_oT, ssm_woT), (w_bT, ssm_bT),
                             (w_iT, ssm_wiT)):
                sp.dma_start(dst[:], src).then_inc(ld_ssm, 16)
            sp.dma_start(ident[:], consts[:, 0:P]).then_inc(ld_const, 16)
            sp.dma_start(iota[:], consts[:, P:P + E1]).then_inc(ld_const, 16)
            sp.dma_start(col[:], cols).then_inc(ld_const, 16)
            sp.dma_start(w_attn[:], attn_w).then_inc(ld_attn, 16)
            sp.dma_start(w_dw[:], dw_w).then_inc(ld_attn, 16)
            sp.dma_start(w_m1[:], wm1).then_inc(ld_attn, 16)
            sp.dma_start(w_m2[:], wm2).then_inc(ld_attn, 16)
            sp.dma_start(row[:], rows.partition_broadcast(P)).then_inc(ld_rows, 16)
            for dst, src in ((w_g0, moe_wg), (w_e1, moe_w1), (w_e2, moe_w2), (w_beta, moe_beta),
                             (w_g1, gate_wT), (w_b2, ffn_b2)):
                sp.dma_start(dst[:], src).then_inc(ld_moe, 16)
            for e in range(ES):
                if e >= 2:
                    sp.wait_ge(tm.filled, tm.at[("y1", e - 2, NG - 1)] + 1)
                sp.dma_start(w_exp[e % 2][:], ffn_w[e]).then_inc(ld_exp[e % 2], 16)
            sp.wait_ge(tm.emptied, len(tm.at))
            sp.dma_start(out[0].rearrange("(p i) d -> p i d", i=NT), h[:]).then_inc(out_done, 16)
            sp.wait_ge(out_done, 16)

        @block.gpsimd
        def _(pool):
            steps = [0]

            def link(ins):
                steps[0] += 1
                ins.then_inc(pool_step, 1)
                pool.wait_ge(pool_step, steps[0])

            link(nc.gpsimd.memset(gathered[:, NT + 1, :], 0.0))
            pool.wait_ge(ld_ids, 16)
            for j in range(NT + 2):
                n = P - 1 if j == NT + 1 else P
                g = max(0, min((j - 2) // GT, NG - 1))
                pool.indirect_dma_start(
                    out=gathered[0:n, j, :], out_offset=None, in_=table,
                    in_offset=bass.IndirectOffsetOnAxis(ap=tok[0:n, j:j + 1], axis=0)).then_inc(emb[g], 16)
            pool.wait_ge(ld_rows, 16)
            for g in G:
                s = slice(g * GT, (g + 1) * GT)
                pool.wait_ge(x1_ready, g + 1)
                link(nc.gpsimd.tensor_tensor(h[:, s, :], h[:, s, :], skip[:, s, :], ALU.add))
                nc.gpsimd.tensor_tensor(
                    h[:, s, :], h[:, s, :],
                    spread_row(ROW_BM2).unsqueeze(1).to_broadcast([P, GT, P]), ALU.add).then_inc(base_ready, 1)
            for i in I:
                for half in range(2):
                    n = 2 * i + half
                    pool.wait_ge(v0_ready, n + 1)
                    v = rb[:, (n % 4) * GC:(n % 4 + 1) * GC]
                    link(nc.gpsimd.tensor_tensor(v, v, spread_row(ROW_GAMMA + 4 * half, 4), ALU.mult))
                    link(nc.gpsimd.tensor_tensor(v[:, 0:2 * P], v[:, 0:2 * P], v[:, 2 * P:4 * P], ALU.add))
                    link(nc.gpsimd.tensor_tensor(v[:, 0:P], v[:, 0:P], v[:, P:2 * P], ALU.add))
                    if n == 0:
                        pool.wait_ge(hb_ready, NG)
                    nc.gpsimd.tensor_tensor(h[:, i, :], h[:, i, :], v[:, 0:P], ALU.add).then_inc(moe_ready, 1)
                    pool.wait_ge(moe_ready, n + 1)
            for g in G:
                s = slice(g * GT, (g + 1) * GT)
                pool.wait_ge(x_ready, X_D + g + 1)
                nc.gpsimd.tensor_tensor(
                    h[:, s, :], h[:, s, :],
                    spread_row(ROW_BO).unsqueeze(1).to_broadcast([P, GT, P]), ALU.add).then_inc(h2_base, 1)

        @block.scalar
        def _(act):
            def root(first, g):
                s = slice(g * GT, (g + 1) * GT)
                act.wait_ge(var_ready, first + g + 1)
                if first == V_A:
                    nc.scalar.activation(nrm[:, s], mv[:, s, 1], ACT.Sqrt, scale=float(P))
                nc.scalar.activation(std[:, s], mv[:, s, 1], ACT.Sqrt, bias=eps_ln).then_inc(std_ready, 1)

            def take_xT(key, g, scale=None, bias=None):
                src = tr.full(act, (key, g))
                dst = xT[:, g * GC:(g + 1) * GC]
                if scale is None:
                    nc.scalar.copy(dst, src).then_inc(tr.emptied, 1)
                elif bias is None:
                    nc.scalar.activation(dst, src, ACT.Copy, scale=scale).then_inc(tr.emptied, 1)
                else:
                    nc.scalar.activation(dst, src, ACT.Identity, scale=scale, bias=bias).then_inc(tr.emptied, 1)

            eps_ln = LN_EPS
            act.wait_ge(ld_const, 48)
            act.wait_ge(lam_dve, 1)
            nc.scalar.activation(lamv[:, 1:2], lamv[:, 0:1], ACT.Exp).then_inc(lam_act, 1)
            act.wait_ge(lam_dve, 2)
            nc.scalar.activation(lamv[:, 3:4], lamv[:, 2:3], ACT.Ln).then_inc(lam_act, 1)
            for g in G:
                root(V_A, g)
            for g in G:
                take_xT("xT_a", g, scale=column("g"))
            for g in G:
                src = ma.full(act, ("l2", g))
                nc.scalar.activation(gl[:, g * GC:(g + 1) * GC], src, ACT.Gelu,
                                     bias=column("b2")).then_inc(ma.emptied, 1)
            for c in G:
                for key, dst, b in (("r", rg, "br"), ("i", ig, "bi")):
                    src = ma.full(act, (key, c))
                    nc.scalar.activation(dst[:, c * GC:(c + 1) * GC], src, ACT.Sigmoid,
                                         bias=column(b)).then_inc(ma.emptied, 1)
            ma.taken(act, ("i", NG - 1))
            act.wait_ge(lam_dve, 4)
            nc.scalar.activation(ra[:], rg[:], ACT.Exp, scale=lamv[:, 8:9]).then_inc(decay_ready, 1)
            nc.scalar.activation(rb[:], rg[:], ACT.Exp, scale=lamv[:, 9:10]).then_inc(decay_ready, 1)
            act.wait_ge(decay_ready, 2)
            nc.scalar.activation(rb[:], rb[:], ACT.Sqrt, scale=-1.0, bias=1.0).then_inc(decay_ready, 1)
            for g in G:
                act.wait_ge(x1_ready, g + 1)
                for i in range(g * GT, (g + 1) * GT):
                    last = nc.scalar.activation(sq[:, 0, (i % GT) * P:(i % GT + 1) * P], skip[:, i, :],
                                                ACT.Square, accum_out=nrm[:, i:i + 1])
                last.then_inc(ssq_ready, 1)
                act.wait_ge(ssq_ready, 2 * g + 1)
                s = slice(g * GT, (g + 1) * GT)
                nc.scalar.activation(std[:, s], nrm[:, s], ACT.Sqrt).then_inc(ssq_ready, 1)
            for g in G:
                take_xT("xT_b", g, scale=column("g"))
            for g in G:
                for m in range(MULT):
                    n = g * MULT + m
                    src = mq.full(act, ("wm1", g, m))
                    if n >= 2:
                        act.wait_ge(hid_ready, n - 1)
                    nc.scalar.activation(zc[:, n % 2, :], src, ACT.Gelu,
                                         bias=column(f"bm1_{m}")).then_inc(gelu_ready, 1)
            for g in G:
                root(V_C, g)
            for g in G:
                take_xT("xT_c", g)
            act.wait_ge(exp0_ready, 1)
            nc.scalar.activation(sm[:, 1, :], sm[:, 0, :], ACT.Exp).then_inc(gate0, 1)
            for g in G:
                src = tr.full(act, ("combT0", g))
                nc.scalar.copy(combT[0:E0, g * GC:(g + 1) * GC], src[0:E0, :]).then_inc(tr.emptied, 1)

            def hidden0(g):
                if g >= 2:
                    act.wait_ge(tm.filled, tm.at[("y0", (g - 1) * GT - 1, 1)] + 1)
                for e in range(E0):
                    src = ma.full(act, ("hid0", g, e))
                    nc.scalar.activation(hid0[:, g % 2, e, :], src, ACT.Relu,
                                         bias=column(f"moe_b1_{e}")).then_inc(ma.emptied, 1)

            def squares(i):
                for half in range(2):
                    n = 2 * i + half
                    act.wait_ge(y0_ready, n + 1)
                    if n >= 2:
                        act.wait_ge(ss0_ready, n - 1)
                    nc.scalar.activation(sq[:, n % 2, :], ra[:, (n % 4) * GC:(n % 4 + 1) * GC],
                                         ACT.Square).then_inc(sq0_ready, 1)

            def deviation(i):
                act.wait_ge(ss0_ready, 2 * i + 2)
                nc.scalar.activation(ss[:, i, :], ss[:, i, :], ACT.Sqrt, scale=1.0 / P,
                                     bias=eps_ln).then_inc(sd0_ready, 1)

            hidden0(0)
            for g in G:
                if g + 1 < NG:
                    hidden0(g + 1)
                for i in range(g * GT, (g + 1) * GT):
                    squares(i)
                    deviation(i)
            for g in G:
                root(V_D, g)
            for g in G:
                take_xT("xT_d", g)
            for g in G:
                root(V_U, g)
            for g in G:
                take_xT("uT", g, scale=column("gamma"), bias=column("beta"))
            for g in G:
                root(V_E, g)
            for g in G:
                take_xT("xT_e", g)
            act.wait_ge(exp1_dve, 1)
            nc.scalar.activation(lg1[:], lg1[:], ACT.Exp).then_inc(exp1_act, 1)
            act.wait_ge(exp1_dve, 2)
            nc.scalar.activation(top[:, :, 0:TOP1], top[:, :, 0:TOP1], ACT.Exp).then_inc(exp1_act, 1)
            for g in G:
                src = tr.full(act, ("combT1", g))
                nc.scalar.copy(combT[:, g * GC:(g + 1) * GC], src[0:ES, :]).then_inc(tr.emptied, 1)
            for e in range(ES):
                act.wait_ge(ld_exp[e % 2], 16 * (e // 2 + 1))
                for g in G:
                    n = e * NG + g
                    if n >= 2:
                        act.wait_ge(tm.filled, tm.at[("y1", 0, 0)] + n - 1)
                    for f in range(FC):
                        src = ma.full(act, ("hid1", e, g, f))
                        nc.scalar.activation(hid1[:, n % 2, f, :], src, ACT.Gelu,
                                             bias=w_exp[e % 2][:, 2 * FC * P + f:2 * FC * P + f + 1]
                                             ).then_inc(ma.emptied, 1)

        @block.vector
        def _(dve):
            steps = [0]

            def mark(ins):
                steps[0] += 1
                ins.then_inc(dve_step, 1)

            def settle():
                dve.wait_ge(dve_step, steps[0])

            def link(ins):
                mark(ins)
                settle()

            def stats(src, g):
                for i in range(g * GT, (g + 1) * GT):
                    ins = nc.vector.bn_stats(bn[:, i, :], src[:, i, :])
                link(ins)
                for i in range(g * GT, (g + 1) * GT):
                    ins = nc.vector.bn_aggr(mv[:, i, :], bn[:, i, :])
                ins.then_inc(var_ready, 1)

            def normalise(src, dst, first, g, scale=None, signal=True):
                s = slice(g * GT, (g + 1) * GT)
                if scale is None:
                    dve.wait_ge(std_ready, first + g + 1)
                    link(nc.vector.reciprocal(rstd[:, s], std[:, s]))
                    scale = rstd
                for i in range(g * GT, (g + 1) * GT):
                    ins = nc.vector.tensor_scalar(dst[:, i, :], src[:, i, :], mv[:, i, 0:1],
                                                  scale[:, i:i + 1], ALU.subtract, ALU.mult)
                if signal:
                    ins.then_inc(x_ready, 1)
                else:
                    mark(ins)

            def copy_out(queue, key, dst, rows=P, width=GC):
                src = queue.full(dve, key)
                nc.vector.tensor_copy(dst, src[0:rows, 0:width]).then_inc(queue.emptied, 1)

            mark(nc.vector.memset(lpad[:, 0:HALO], 0.0))
            mark(nc.vector.memset(lpad[:, HALO + T:], 0.0))
            mark(nc.vector.memset(carry[:, 0:1], 0.0))
            link(nc.vector.memset(comb[:, :, E1:ES], 1.0 / SHARED))
            dve.wait_ge(ld_const, 48)
            lam = column("lam")
            link(nc.vector.tensor_scalar(lamv[:, 10:11], lam, -1.0, None, ALU.mult))
            link(nc.vector.tensor_tensor(lamv[:, 11:12], lam, lamv[:, 10:11], ALU.max))
            nc.vector.tensor_scalar(lamv[:, 0:1], lamv[:, 11:12], -1.0, None, ALU.mult).then_inc(lam_dve, 1)
            dve.wait_ge(lam_act, 1)
            nc.vector.tensor_scalar(lamv[:, 2:3], lamv[:, 1:2], 1.0, None, ALU.add).then_inc(lam_dve, 1)
            dve.wait_ge(lam_dve, 2)
            link(nc.vector.tensor_scalar(lamv[:, 4:5], lamv[:, 2:3], -1.0, None, ALU.add))
            link(nc.vector.tensor_scalar(lamv[:, 5:6], lamv[:, 4:5], 1e-30, None, ALU.max))
            link(nc.vector.reciprocal(lamv[:, 5:6], lamv[:, 5:6]))
            dve.wait_ge(lam_act, 2)
            link(nc.vector.tensor_tensor(lamv[:, 6:7], lamv[:, 3:4], lamv[:, 5:6], ALU.mult))
            link(nc.vector.scalar_tensor_tensor(out=lamv[:, 6:7], in0=lamv[:, 4:5], scalar=0.0,
                                                in1=lamv[:, 6:7], op0=ALU.is_equal, op1=ALU.add))
            link(nc.vector.tensor_tensor(lamv[:, 6:7], lamv[:, 6:7], lamv[:, 1:2], ALU.mult))
            link(nc.vector.scalar_tensor_tensor(out=lamv[:, 7:8], in0=lam, scalar=0.0,
                                                in1=lamv[:, 6:7], op0=ALU.max, op1=ALU.add))
            nc.vector.tensor_scalar(lamv[:, 8:9], lamv[:, 7:8], -8.0, None, ALU.mult).then_inc(lam_dve, 1)
            nc.vector.tensor_scalar(lamv[:, 9:10], lamv[:, 7:8], -16.0, None, ALU.mult).then_inc(lam_dve, 1)
            copy_out(mq, ("woC",), woC[:], NS, P)
            copy_out(mq, ("woD",), woD[:], P, P)
            for i in I:
                copy_out(mq, ("q", i), qT[:, i, :], NS, P)
                if i < POW_LEVELS:
                    copy_out(mq, ("pow", i), powers[:, i + 1, :], NS, 2 * NS)
            for g in G:
                s = slice(g * GT, (g + 1) * GT)
                dve.wait_ge(emb[g], 16 * ((GT + 2) if g == 0 else GT))
                if g == 0:
                    link(nc.vector.memset(gathered[0:1, 0, :], 0.0))
                link(nc.vector.tensor_tensor(h[:, s, :], gathered[:, g * GT:(g + 1) * GT, 0:P],
                                             gathered[:, g * GT + 1:(g + 1) * GT + 1, P:2 * P], ALU.add))
                link(nc.vector.tensor_tensor(h[:, s, :], h[:, s, :],
                                             gathered[:, g * GT + 2:(g + 1) * GT + 2, 2 * P:3 * P], ALU.add))
                stats(h, g)
            for g in G:
                s = slice(g * GT, (g + 1) * GT)
                dve.wait_ge(std_ready, V_A + g + 1)
                link(nc.vector.reciprocal(rstd[:, s], std[:, s]))
                link(nc.vector.tensor_tensor(qs[:, s], nrm[:, s], rstd[:, s], ALU.mult))
                link(nc.vector.tensor_scalar(qs[:, s], qs[:, s], RMS_EPS, None, ALU.add))
                link(nc.vector.reciprocal(qs[:, s], qs[:, s]))
                link(nc.vector.scalar_tensor_tensor(out=qs[:, s], in0=qs[:, s], scalar=SQD, in1=rstd[:, s],
                                                    op0=ALU.mult, op1=ALU.mult))
                normalise(h, xn, V_A, g, scale=qs)
            for g in G:
                normalise(h, skip, V_A, g, scale=rstd, signal=False)
            for g in G:
                src = mq.full(dve, ("l1", g)).rearrange("f (i p) -> f i p", i=GT)
                dst = lpad[:, HALO:HALO + T].rearrange("f (p i) -> f i p", i=NT)[:, g * GT:(g + 1) * GT, :]
                nc.vector.tensor_scalar(dst, src, column("b1"), None, ALU.add).then_inc(mq.emptied, 1)
            for c in G:
                src = mq.full(dve, ("z", c))
                nc.vector.tensor_scalar(zc[:, c % 2, :], src, column("dw_b"), None,
                                        ALU.add).then_inc(mq.emptied, 1)
                src = mq.full(dve, ("lx", c))
                nc.vector.tensor_scalar(lx[:, c * GC:(c + 1) * GC], src, column("pw_b"), None,
                                        ALU.add).then_inc(mq.emptied, 1)
            for c in G:
                s = slice(c * GC, (c + 1) * GC)
                ma.taken(dve, ("i", c))
                link(nc.vector.tensor_tensor(ig[:, s], ig[:, s], lx[:, s], ALU.mult))
            dve.wait_ge(decay_ready, 3)
            link(nc.vector.tensor_tensor(ig[:], ig[:], rb[:], ALU.mult))
            link(nc.vector.tensor_tensor_scan(lx[:], ra[:], ig[:], 0.0, ALU.mult, ALU.add))
            prod = rg
            for g in G:
                s = slice(g * GT, (g + 1) * GT)
                nc.vector.tensor_tensor(prod[:, g * GC:(g + 1) * GC].rearrange("f (i p) -> f i p", i=GT),
                                        lx[:].rearrange("f (p i) -> f i p", i=NT)[:, s, :],
                                        gl[:, g * GC:(g + 1) * GC].rearrange("f (i p) -> f i p", i=GT),
                                        ALU.mult).then_inc(prod_ready, 1)
            for g in G:
                s = slice(g * GT, (g + 1) * GT)
                src = tm.full(dve, ("pT", g)).rearrange("p (i f) -> p i f", i=GT)
                nc.vector.tensor_tensor(skip[:, s, :], src, skip[:, s, :], ALU.add).then_inc(tm.emptied, 1)
                tm.taken(dve, ("pT", g))
                link(nc.vector.tensor_copy(qs[:, s], rstd[:, s]))
                dve.sem_inc(x1_ready, 1)
            for g in G:
                s = slice(g * GT, (g + 1) * GT)
                dve.wait_ge(ssq_ready, 2 * g + 2)
                link(nc.vector.tensor_scalar(qs[:, s], std[:, s], RMS_EPS, None, ALU.add))
                link(nc.vector.reciprocal(qs[:, s], qs[:, s]))
                for i in range(g * GT, (g + 1) * GT):
                    ins = nc.vector.tensor_scalar(xn[:, i, :], skip[:, i, :], qs[:, i:i + 1], SQD,
                                                  ALU.mult, ALU.mult)
                ins.then_inc(x_ready, 1)
            for g in G:
                for m in range(MULT):
                    n = g * MULT + m
                    dve.wait_ge(gelu_ready, n + 1)
                    src = mq.full(dve, ("wm1", g, m))
                    if m == 0 and g >= 2:
                        dve.wait_ge(tm.filled, tm.at[("out0", g - 2)] + 1)
                    mark(nc.vector.scalar_tensor_tensor(
                        out=hidm[:, g % 2, m, :], in0=src, scalar=column(f"bm1_{m}"), in1=zc[:, n % 2, :],
                        op0=ALU.add, op1=ALU.mult))
                    settle()
                    dve.sem_inc(hid_ready, 1)
                    dve.sem_inc(mq.emptied, 1)
            for g in G:
                s = slice(g * GT, (g + 1) * GT)
                dve.wait_ge(base_ready, g + 1)
                src = tm.full(dve, ("out0", g)).rearrange("p (i f) -> p i f", i=GT)
                nc.vector.tensor_tensor(h[:, s, :], src, h[:, s, :], ALU.add).then_inc(tm.emptied, 1)
            dve.wait_ge(ld_moe, 96)
            link(nc.vector.tensor_reduce(wmean[:, 0:E0], w_e2[:], AX.X, ALU.add))
            link(nc.vector.tensor_reduce(wmean[:, E0:], spread_row(ROW_B2, E0).rearrange("p (e d) -> p e d", e=E0),
                                         AX.X, ALU.add))
            link(nc.vector.tensor_scalar(wmean[:], wmean[:], 1.0 / P, None, ALU.mult))
            for e in range(E0):
                mark(nc.vector.tensor_scalar(w_e2[:, e, :], w_e2[:, e, :], wmean[:, e:e + 1], None, ALU.subtract))
                b = spread_row(ROW_B2 + e)
                ins = nc.vector.tensor_scalar(b, b, wmean[:, E0 + e:E0 + e + 1], None, ALU.subtract)
            ins.then_inc(centered, 1)
            for g in G:
                tm.taken(dve, ("out0", g))
                stats(h, g)
            for g in G:
                normalise(h, xn, V_C, g)
            for g in G:
                src = tm.full(dve, ("logit0", g))[:, 0:GT * E0].rearrange("p (i e) -> p i e", i=GT)
                nc.vector.tensor_copy(lg0[:, g * GT:(g + 1) * GT, :], src).then_inc(tm.emptied, 1)
            tm.taken(dve, ("logit0", NG - 1))
            for i in I:
                mark(nc.vector.max(top[:, i, :], lg0[:, i, :]))
            settle()
            for i in I:
                mark(nc.vector.max_index(topi[:, i, :], top[:, i, :], lg0[:, i, :]))
            nc.vector.tensor_tensor(sm[:, 0, :], top[:, :, 1], top[:, :, 0], ALU.subtract).then_inc(exp0_ready, 1)
            settle()
            link(nc.vector.tensor_copy(topf[:], topi[:]))
            dve.wait_ge(gate0, 1)
            link(nc.vector.tensor_scalar(sm[:, 2, :], sm[:, 1, :], 1.0, None, ALU.add))
            link(nc.vector.reciprocal(sm[:, 2, :], sm[:, 2, :]))
            link(nc.vector.tensor_tensor(sm[:, 3, :], sm[:, 1, :], sm[:, 2, :], ALU.mult))

            def one_hot(dst, tmp, k, weight, n):
                out_ = dst if k == 0 else tmp
                io = iota[:, 0:n].unsqueeze(1).to_broadcast([P, NT, n])
                link(nc.vector.tensor_tensor(out_, io, topf[:, :, k:k + 1].to_broadcast([P, NT, n]), ALU.is_equal))
                link(nc.vector.tensor_tensor(out_, out_, weight.to_broadcast([P, NT, n]), ALU.mult))
                if k:
                    link(nc.vector.tensor_tensor(dst, dst, tmp, ALU.add))

            comb0 = comb[:, :, 0:E0]
            for k in range(2):
                one_hot(comb0, hot[:, :, 0:E0], k, sm[:, 2 + k, :].unsqueeze(2), E0)
            dve.sem_inc(comb0_ready, 1)
            for g in G:
                s = slice(g * GT, (g + 1) * GT)
                src = tm.full(dve, ("beta0", g)).rearrange("p (i f) -> p i f", i=GT)
                nc.vector.tensor_tensor(h[:, s, :], src, h[:, s, :], ALU.add).then_inc(tm.emptied, 1)
            tm.taken(dve, ("beta0", NG - 1))
            dve.sem_inc(hb_ready, NG)

            def y_of(n):
                return ra[:, (n % 4) * GC:(n % 4 + 1) * GC]

            def take_y(n):
                src = tm.full(dve, ("y0", n // 2, n % 2))
                nc.vector.tensor_tensor(y_of(n), src, spread_row(ROW_B2 + 4 * (n % 2), 4),
                                        ALU.add).then_inc(tm.emptied, 1)
                tm.taken(dve, ("y0", n // 2, n % 2))
                dve.sem_inc(y0_ready, 1)

            def sum_squares(n):
                dve.wait_ge(sq0_ready, n + 1)
                nc.vector.tensor_reduce(ss[:, n // 2, 4 * (n % 2):4 * (n % 2) + 4],
                                        sq[:, n % 2, :].rearrange("p (e d) -> p e d", e=4), AX.X,
                                        ALU.add).then_inc(ss0_ready, 1)

            def scale_tile(i):
                dve.wait_ge(sd0_ready, i + 1)
                link(nc.vector.reciprocal(sc[:, i, :], ss[:, i, :]))
                link(nc.vector.tensor_tensor(sc[:, i, :], sc[:, i, :], comb[:, i, 0:E0], ALU.mult))
                for half in range(2):
                    n = 2 * i + half
                    if n >= 4:
                        dve.wait_ge(moe_ready, n - 3)
                    nc.vector.tensor_tensor(
                        rb[:, (n % 4) * GC:(n % 4 + 1) * GC].rearrange("p (e d) -> p e d", e=4),
                        y_of(n).rearrange("p (e d) -> p e d", e=4),
                        sc[:, i, 4 * half:4 * half + 4].unsqueeze(2).to_broadcast([P, 4, P]),
                        ALU.mult).then_inc(v0_ready, 1)

            for i in range(NT + 1):
                if i < NT:
                    if i >= 2:
                        dve.wait_ge(v0_ready, 2 * (i - 1))
                    take_y(2 * i)
                    take_y(2 * i + 1)
                if i >= 1:
                    scale_tile(i - 1)
                if i < NT:
                    sum_squares(2 * i)
                    sum_squares(2 * i + 1)
            for g in G:
                dve.wait_ge(moe_ready, 2 * GT * (g + 1))
                stats(h, g)
            for g in G:
                normalise(h, xn, V_D, g)
            for g in G:
                s = slice(g * GT, (g + 1) * GT)
                src = tm.full(dve, ("hm", g)).rearrange("p (i f) -> p i f", i=GT)
                nc.vector.tensor_tensor(skip[:, s, :], src,
                                        spread_row(ROW_BI).unsqueeze(1).to_broadcast([P, GT, P]),
                                        ALU.add).then_inc(tm.emptied, 1)
                tm.taken(dve, ("hm", g))
                stats(skip, g)
            for g in G:
                normalise(skip, xn, V_U, g)
            for i in I:
                copy_out(mq, ("state", i), st[:, i, :], NS, P)
            mq.taken(dve, ("state", NT - 1))
            mark(nc.vector.tensor_copy(carry[:, 1:P + 1], st[:, NT - 1, :]))
            settle()
            dve.sem_inc(gate0_dve, 1)
            for k in range(SCAN_LEVELS):
                w = P - 2 ** k
                src = mq.full(dve, ("carry", k))
                nc.vector.tensor_tensor(carry[:, 1 + 2 ** k:P + 1], carry[:, 1 + 2 ** k:P + 1],
                                        src[0:NS, 0:w], ALU.add).then_inc(mq.emptied, 1)
                mq.taken(dve, ("carry", k))
            for g in G:
                s = slice(g * GT, (g + 1) * GT)
                dve.wait_ge(h2_base, g + 1)
                src = tm.full(dve, ("y_ssm", g)).rearrange("p (i f) -> p i f", i=GT)
                nc.vector.tensor_tensor(h[:, s, :], src, h[:, s, :], ALU.add).then_inc(tm.emptied, 1)
                tm.taken(dve, ("y_ssm", g))
                stats(h, g)
            for g in G:
                normalise(h, xn, V_E, g)
            for g in G:
                src = tm.full(dve, ("logit1", g))[:, 0:GT * E1].rearrange("p (i e) -> p i e", i=GT)
                nc.vector.tensor_copy(lg1[:, g * GT:(g + 1) * GT, :], src).then_inc(tm.emptied, 1)
            tm.taken(dve, ("logit1", NG - 1))
            link(nc.vector.tensor_reduce(sm[:, 0, :], lg1[:], AX.X, ALU.max))
            nc.vector.tensor_tensor(lg1[:], lg1[:], sm[:, 0, :].unsqueeze(2).to_broadcast([P, NT, E1]),
                                    ALU.subtract).then_inc(exp1_dve, 1)
            dve.wait_ge(exp1_act, 1)
            link(nc.vector.tensor_reduce(sm[:, 1, :], lg1[:], AX.X, ALU.add))
            link(nc.vector.reciprocal(sm[:, 1, :], sm[:, 1, :]))
            link(nc.vector.tensor_tensor(lg1[:], lg1[:], sm[:, 1, :].unsqueeze(2).to_broadcast([P, NT, E1]),
                                         ALU.mult))
            for i in I:
                mark(nc.vector.max(top[:, i, :], lg1[:, i, :]))
            settle()
            for i in I:
                mark(nc.vector.max_index(topi[:, i, :], top[:, i, :], lg1[:, i, :]))
            settle()
            link(nc.vector.tensor_copy(topf[:], topi[:]))
            link(nc.vector.tensor_copy(sm[:, 2, :], top[:, :, 0]))
            nc.vector.tensor_tensor(top[:, :, 0:TOP1], top[:, :, 0:TOP1],
                                    sm[:, 2, :].unsqueeze(2).to_broadcast([P, NT, TOP1]),
                                    ALU.subtract).then_inc(exp1_dve, 1)
            dve.wait_ge(exp1_act, 2)
            link(nc.vector.tensor_reduce(sm[:, 3, :], top[:, :, 0:TOP1], AX.X, ALU.add))
            link(nc.vector.reciprocal(sm[:, 3, :], sm[:, 3, :]))
            link(nc.vector.tensor_tensor(top[:, :, 0:TOP1], top[:, :, 0:TOP1],
                                         sm[:, 3, :].unsqueeze(2).to_broadcast([P, NT, TOP1]), ALU.mult))
            comb1 = comb[:, :, 0:E1]
            for k in range(TOP1):
                one_hot(comb1, hot[:], k, top[:, :, k:k + 1], E1)
            dve.sem_inc(comb1_ready, 1)
            for g in G:
                s = slice(g * GT, (g + 1) * GT)
                src = tm.full(dve, ("b2", g)).rearrange("p (i f) -> p i f", i=GT)
                nc.vector.tensor_tensor(h[:, s, :], src, h[:, s, :], ALU.add).then_inc(tm.emptied, 1)
            for e in range(ES):
                for g in G:
                    src = tm.full(dve, ("y1", e, g))
                    n = tm.at[("y1", e, g)]
                    dve.wait_ge(tm.emptied, n - NG + 1)
                    for j in range(GT):
                        i = g * GT + j
                        ins = nc.vector.scalar_tensor_tensor(
                            out=h[:, i, :], in0=src[:, j * P:(j + 1) * P], scalar=comb[:, i, e:e + 1],
                            in1=h[:, i, :], op0=ALU.mult, op1=ALU.add)
                    ins.then_inc(tm.emptied, 1)

        @block.tensor
        def _(pe):
            def mm(out_, lhsT, rhs, start=True, stop=True):
                return nc.tensor.matmul(out_, lhsT, rhs, start=start, stop=stop)

            def transpose_group(key, g, first):
                pe.wait_ge(x_ready, first + g + 1)
                dst = tr.fill(pe, (key, g))
                for j in range(GT):
                    ins = nc.tensor.transpose(dst[:, j * P:(j + 1) * P], xn[:, g * GT + j, :], ident[:])
                ins.then_inc(tr.filled, 1)

            pe.wait_ge(ld_ssm, 96)
            A, AT = w_a[:, 0:NS], w_a[:, NS:2 * NS]
            dst = mq.fill(pe, ("woC",))
            mm(dst[0:NS, 0:P], w_c[:], w_oT[:]).then_inc(mq.filled, 1)
            dst = mq.fill(pe, ("woD",))
            mm(dst[:, 0:P], w_d[:], w_oT[:]).then_inc(mq.filled, 1)
            for i in I:
                mq.taken(pe, ("q", i - 1) if i else ("woC",))
                dst = mq.fill(pe, ("q", i))
                mm(dst[0:NS, 0:P], A, qT[:, i - 1, :] if i else woC[:]).then_inc(mq.filled, 1)
                if i < POW_LEVELS:
                    if i:
                        mq.taken(pe, ("pow", i - 1))
                    N, NT_ = (A, AT) if i == 0 else (powers[:, i, 0:NS], powers[:, i, NS:2 * NS])
                    dst = mq.fill(pe, ("pow", i))
                    mm(dst[0:NS, 0:NS], NT_, N)
                    mm(dst[0:NS, NS:2 * NS], N, NT_).then_inc(mq.filled, 1)
            pe.wait_ge(ld_const, 48)
            for g in G:
                transpose_group("xT_a", g, X_A)
            pe.wait_ge(ld_attn, 64)
            for g in G:
                tr.taken(pe, ("xT_a", g))
                x = xT[:, g * GC:(g + 1) * GC]
                mm(mq.fill(pe, ("l1", g)), w_attn[:, 0, :], x).then_inc(mq.filled, 1)
                mm(ma.fill(pe, ("l2", g)), w_attn[:, 1, :], x).then_inc(ma.filled, 1)
            mq.taken(pe, ("l1", NG - 1))
            for c in G:
                dst = mq.fill(pe, ("z", c))
                for k in range(K):
                    ins = mm(dst, w_dw[:, k, :], lpad[:, c * GC + k:c * GC + k + GC], k == 0, k == K - 1)
                ins.then_inc(mq.filled, 1)
                mq.taken(pe, ("z", c))
                mm(mq.fill(pe, ("lx", c)), w_attn[:, 2, :], zc[:, c % 2, :]).then_inc(mq.filled, 1)
                mq.taken(pe, ("lx", c))
                x = lx[:, c * GC:(c + 1) * GC]
                mm(ma.fill(pe, ("r", c)), w_attn[:, 4, :], x).then_inc(ma.filled, 1)
                mm(ma.fill(pe, ("i", c)), w_attn[:, 3, :], x).then_inc(ma.filled, 1)
            for g in G:
                pe.wait_ge(prod_ready, g + 1)
                dst = tm.fill(pe, ("pT", g))
                for j in range(GT):
                    i = g * GT + j
                    ins = nc.tensor.transpose(dst[:, j * P:(j + 1) * P], rg[:, i * P:(i + 1) * P], ident[:])
                ins.then_inc(tm.filled, 1)
            for g in G:
                transpose_group("xT_b", g, X_B)
            for g in range(NG + 1):
                if g < NG:
                    tr.taken(pe, ("xT_b", g))
                    for m in range(MULT):
                        mm(mq.fill(pe, ("wm1", g, m)), w_m1[:, m * P:(m + 1) * P],
                           xT[:, g * GC:(g + 1) * GC]).then_inc(mq.filled, 1)
                if g >= 1:
                    pe.wait_ge(hid_ready, MULT * g)
                    dst = tm.fill(pe, ("out0", g - 1))
                    for j in range(GT):
                        for m in range(MULT):
                            ins = mm(dst[:, j * P:(j + 1) * P], hidm[:, (g - 1) % 2, m, j * P:(j + 1) * P],
                                     w_m2[:, m, :], m == 0, m == MULT - 1)
                    ins.then_inc(tm.filled, 1)
            for g in G:
                transpose_group("xT_c", g, X_C)
            pe.wait_ge(ld_moe, 96)
            for g in G:
                tr.taken(pe, ("xT_c", g))
                dst = tm.fill(pe, ("logit0", g))
                for j in range(GT):
                    i = g * GT + j
                    ins = mm(dst[:, j * E0:(j + 1) * E0], xT[:, i * P:(i + 1) * P], w_g0[:])
                ins.then_inc(tm.filled, 1)

            def combine_transposed(key, n, ready):
                pe.wait_ge(ready, 1)
                for g in G:
                    dst = tr.fill(pe, (key, g))
                    for j in range(GT):
                        ins = nc.tensor.transpose(dst[0:n, j * P:(j + 1) * P], comb[:, g * GT + j, 0:n], ident[:])
                    ins.then_inc(tr.filled, 1)

            def weighted_rows(key, ckey, n, w):
                for g in G:
                    tr.taken(pe, (ckey, g))
                    dst = tm.fill(pe, (key, g))
                    for j in range(GT):
                        i = g * GT + j
                        ins = mm(dst[:, j * P:(j + 1) * P], combT[0:n, i * P:(i + 1) * P], w[:])
                    ins.then_inc(tm.filled, 1)

            def hidden0(g):
                for e in range(E0):
                    mm(ma.fill(pe, ("hid0", g, e)), w_e1[:, e, :],
                       xT[:, g * GC:(g + 1) * GC]).then_inc(ma.filled, 1)

            combine_transposed("combT0", E0, comb0_ready)
            weighted_rows("beta0", "combT0", E0, w_beta)
            hidden0(0)
            pe.wait_ge(centered, 1)
            for g in G:
                if g + 1 < NG:
                    hidden0(g + 1)
                ma.taken(pe, ("hid0", g, E0 - 1))
                for j in range(GT):
                    for half in range(2):
                        dst = tm.fill(pe, ("y0", g * GT + j, half))
                        for q in range(4):
                            e = 4 * half + q
                            ins = mm(dst[:, q * P:(q + 1) * P], hid0[:, g % 2, e, j * P:(j + 1) * P], w_e2[:, e, :])
                        ins.then_inc(tm.filled, 1)
            for g in G:
                transpose_group("xT_d", g, X_D)
            for g in G:
                tr.taken(pe, ("xT_d", g))
                dst = tm.fill(pe, ("hm", g))
                for j in range(GT):
                    i = g * GT + j
                    ins = mm(dst[:, j * P:(j + 1) * P], xT[:, i * P:(i + 1) * P], w_iT[:])
                ins.then_inc(tm.filled, 1)
            for g in G:
                transpose_group("uT", g, X_U)
            for i in I:
                if i % GT == 0:
                    tr.taken(pe, ("uT", i // GT))
                dst = mq.fill(pe, ("state", i))[0:NS, 0:P]
                ins = mm(dst, w_bT[:], xT[:, i * P:(i + 1) * P], True, i == 0)
                if i:
                    mq.taken(pe, ("state", i - 1))
                    ins = mm(dst, AT, st[:, i - 1, :], False, True)
                ins.then_inc(mq.filled, 1)
            pe.wait_ge(gate0_dve, 1)
            for k in range(SCAN_LEVELS):
                if k:
                    mq.taken(pe, ("carry", k - 1))
                w = P - 2 ** k
                mm(mq.fill(pe, ("carry", k))[0:NS, 0:w], powers[:, 4 + k, NS:2 * NS],
                   carry[:, 1:1 + w]).then_inc(mq.filled, 1)
            mq.taken(pe, ("carry", SCAN_LEVELS - 1))
            for g in G:
                dst = tm.fill(pe, ("y_ssm", g))
                for j in range(GT):
                    i = g * GT + j
                    d = dst[:, j * P:(j + 1) * P]
                    mm(d, xT[:, i * P:(i + 1) * P], woD[:], True, False)
                    mm(d, st[:, i, :], woC[:], False, False)
                    ins = mm(d, carry[:, 0:P], qT[:, i, :], False, True)
                ins.then_inc(tm.filled, 1)
            for g in G:
                transpose_group("xT_e", g, X_E)
            for g in G:
                tr.taken(pe, ("xT_e", g))
                dst = tm.fill(pe, ("logit1", g))
                for j in range(GT):
                    i = g * GT + j
                    ins = mm(dst[:, j * E1:(j + 1) * E1], xT[:, i * P:(i + 1) * P], w_g1[:])
                ins.then_inc(tm.filled, 1)
            combine_transposed("combT1", ES, comb1_ready)
            weighted_rows("b2", "combT1", ES, w_b2)

            def hidden1(e, g):
                if g == 0:
                    pe.wait_ge(ld_exp[e % 2], 16 * (e // 2 + 1))
                for f in range(FC):
                    mm(ma.fill(pe, ("hid1", e, g, f)), w_exp[e % 2][:, f * P:(f + 1) * P],
                       xT[:, g * GC:(g + 1) * GC]).then_inc(ma.filled, 1)

            hidden1(0, 0)
            for e in range(ES):
                for g in G:
                    n = e * NG + g
                    if n + 1 < ES * NG:
                        hidden1((n + 1) // NG, (n + 1) % NG)
                    ma.taken(pe, ("hid1", e, g, FC - 1))
                    dst = tm.fill(pe, ("y1", e, g))
                    for j in range(GT):
                        for f in range(FC):
                            ins = mm(dst[:, j * P:(j + 1) * P], hid1[:, n % 2, f, j * P:(j + 1) * P],
                                     w_exp[e % 2][:, (FC + f) * P:(FC + f + 1) * P], f == 0, f == FC - 1)
                    ins.then_inc(tm.filled, 1)


def kernel(**inputs):
    import numpy as np
    import concourse.bacc as bacc
    from concourse.bass_utils import run_bass_kernel_spmd

    x = {k: np.asarray(v) for k, v in inputs.items()}
    c = np.ascontiguousarray
    consts = np.zeros((P, P + E1), np.float32)
    consts[:, :P] = np.eye(P)
    consts[:, P:] = np.arange(E1)
    vec = ["g", "b1", "b2", "dw_b", "pw_b", "bi", "br", "lam"]
    cols = [x[f"L0_attn_{v}"] for v in vec] + list(x["L0_attn_bm1"].reshape(MULT, P))
    cols += [x["L1_attn_gamma"], x["L1_attn_beta"]] + list(x["L0_ffn_b1"])
    rows = [x["L0_attn_bm2"], x["L1_attn_bi"], x["L1_attn_bo"], *x["L0_ffn_b2"], *x["L0_ffn_gamma"]]
    w1 = np.concatenate([x["L1_ffn_re_w1"], x["L1_ffn_se_w1"]])
    w2 = np.concatenate([x["L1_ffn_re_w2"], x["L1_ffn_se_w2"]])
    b1 = np.concatenate([x["L1_ffn_re_b1"], x["L1_ffn_se_b1"]])
    ffn = np.concatenate([
        w1, w2.reshape(ES, FC, P, P).transpose(0, 2, 1, 3).reshape(ES, P, FC * P),
        b1.reshape(ES, FC, P).transpose(0, 2, 1)], axis=2)
    ids = np.zeros((P, NT + 2), x["x"].dtype)
    ids[:, 1:NT + 1] = x["x"].reshape(P, NT)
    ids[1:, 0] = ids[:-1, NT]
    ids[:-1, NT + 1] = ids[1:, 1]
    arrays = {
        "ids": ids,
        "table": c(x["L0_tok_conv_w"].transpose(1, 2, 0).reshape(-1, TAPS0 * P)),
        "consts": consts,
        "cols": c(np.stack(cols, axis=1)),
        "rows": c(np.concatenate(rows)),
        "attn_w": c(np.stack([x["L0_attn_W1"], x["L0_attn_W2"], x["L0_attn_pw_w"][:, :, 0].T,
                              x["L0_attn_Wi"], x["L0_attn_Wr"]], axis=1)),
        "dw_w": c(x["L0_attn_dw_w"].transpose(1, 2, 0)),
        "wm1": x["L0_attn_Wm1"],
        "wm2": c(x["L0_attn_Wm2"].reshape(MULT, P, P).transpose(1, 0, 2)),
        "moe_wg": x["L0_ffn_Wg"],
        "moe_w1": c(x["L0_ffn_W1"].transpose(1, 0, 2)),
        "moe_w2": c(x["L0_ffn_W2"].transpose(1, 0, 2)),
        "moe_beta": x["L0_ffn_beta"],
        "ssm_a": c(np.concatenate([x["L1_attn_A"], x["L1_attn_A"].T], axis=1)),
        "ssm_bT": c(x["L1_attn_Bm"].T),
        "ssm_c": x["L1_attn_Cm"],
        "ssm_d": x["L1_attn_Dm"],
        "ssm_wiT": c(x["L1_attn_Wi"].T),
        "ssm_woT": c(x["L1_attn_Wo"].T),
        "gate_wT": c(x["L1_ffn_gate_w"].T),
        "ffn_w": c(ffn),
        "ffn_b2": c(np.concatenate([x["L1_ffn_re_b2"], x["L1_ffn_se_b2"]])),
    }
    nc = bacc.Bacc("TRN2", target_bir_lowering=False, num_devices=1)
    args = [nc.dram_tensor(f"in_{k}", a.shape, mybir.dt.from_np(a.dtype), kind="ExternalInput").ap()
            for k, a in arrays.items()]
    args.append(nc.dram_tensor("out", (1, T, P), F32, kind="ExternalOutput").ap())
    lm_tower_kernel(nc, *args)
    r = run_bass_kernel_spmd(nc, [{f"in_{k}": a for k, a in arrays.items()}], core_ids=[0])
    return r.results[0]["out"]
```

```python
from contextlib import ExitStack

import concourse.bass as bass
from concourse import mybir

F32 = mybir.dt.float32
I32 = mybir.dt.int32
BF16 = mybir.dt.bfloat16
U32 = mybir.dt.uint32
ALU = mybir.AluOpType
ACT = mybir.ActivationFunctionType
AX = mybir.AxisListType

P = 128
T = 2048
NT = T // P
GT = 4
NG = NT // GT
GC = GT * P
TAPS0 = 3
K = 9
HALO = K // 2
MULT = 4
E0 = 8
E1 = 16
TOP1 = 4
SHARED = 2
ES = E1 + SHARED
FC = 4
NS = 64
LN_EPS = 1e-5
RMS_EPS = 1e-6
SQD = float(P) ** 0.5
SCAN_LEVELS = 7
POW_LEVELS = 4 + SCAN_LEVELS - 1

COLS = ["g", "b1", "b2", "dw_b", "pw_b", "bi", "br", "lam", "bm1_0", "bm1_1", "bm1_2", "bm1_3",
        "gamma", "beta"] + [f"moe_b1_{e}" for e in range(E0)]
ROW_BM2, ROW_BI, ROW_BO, ROW_B2, ROW_GAMMA = 0, 1, 2, 3, 3 + E0
ROWS = 3 + 2 * E0
FH = FC * P

XRING = 8
NACC = 4
RT = -(-(T * TOP1 // P + E1 - 1) // XRING) * XRING
LEAD = 3
R_ID, R_COMB = P, P + 1
RW = P + 1 + E1


class BankQueue:

    def __init__(self, nc, ctx, name, banks, keys):
        self.banks = banks
        self.at = {key: n for n, key in enumerate(keys)}
        assert len(self.at) == len(keys)
        self.filled = ctx.enter_context(nc.semaphore(f"{name}_filled"))
        self.emptied = ctx.enter_context(nc.semaphore(f"{name}_emptied"))
        self.issued = 0

    def fill(self, pe, key):
        n = self.at[key]
        assert n == self.issued, (key, n, self.issued)
        self.issued += 1
        if n >= 2:
            pe.wait_ge(self.emptied, n - 1)
        return self.banks[n % 2]

    def full(self, eng, key):
        n = self.at[key]
        eng.wait_ge(self.filled, n + 1)
        return self.banks[n % 2]

    def taken(self, eng, key):
        eng.wait_ge(self.emptied, self.at[key] + 1)


def lm_tower_kernel(nc, ids, table, consts, cols, rows, attn_w, dw_w, wm1, wm2, moe_wg, moe_w1, moe_w2,
                    moe_beta, ssm_a, ssm_bT, ssm_c, ssm_d, ssm_wiT, ssm_woT, gate_wT, ffn_w1, ffn_w2, ffn_b1, ffn_b2,
                    consts_bf, consts_i, tile_ids, slots_dram, sums_dram, out):
    with ExitStack() as ctx:
        def sb(name, shape, dt=F32):
            return ctx.enter_context(nc.sbuf_tensor(f"sb_{name}", shape, dt))

        def sem(name):
            return ctx.enter_context(nc.semaphore(name))

        ident = sb("ident", [P, P])
        iota = sb("iota", [P, E1])
        col = sb("col", [P, len(COLS)])
        row = sb("row", [P, ROWS * P])
        w_attn = sb("w_attn", [P, 5, P])
        w_dw = sb("w_dw", [P, K, P])
        w_m1 = sb("w_m1", [P, MULT * P])
        w_m2 = sb("w_m2", [P, MULT, P])
        w_g0 = sb("w_g0", [P, E0])
        w_e1 = sb("w_e1", [P, E0, P])
        w_e2 = sb("w_e2", [P, E0, P])
        w_beta = sb("w_beta", [E0, P])
        w_a = sb("w_a", [NS, 2 * NS])
        w_bT = sb("w_bT", [P, NS])
        w_c = sb("w_c", [P, NS])
        w_d = sb("w_d", [P, P])
        w_iT = sb("w_iT", [P, P])
        w_oT = sb("w_oT", [P, P])
        w_g1 = sb("w_g1", [P, E1])
        w_b2 = sb("w_b2", [ES, P])
        w_sh1 = w_e1[:].rearrange("p e d -> p (e d)").rearrange("p (e f) -> p e f", e=SHARED)
        w_sh2 = w_e2[:].rearrange("p e d -> p (e d)").rearrange("p (e f) -> p e f", e=SHARED)
        b1T = sb("b1T", [P, ES * FC])
        tri = sb("tri", [P, P], BF16)
        ones = sb("ones", [P, P], BF16)
        token_id = sb("token_id", [P, NT + 1], I32)
        tile_no = sb("tile_no", [1, RT])

        def column(name):
            n = COLS.index(name)
            return col[:, n:n + 1]

        def spread_row(at, n=1):
            return row[:, at * P:(at + n) * P]

        tok = sb("tok", [P, NT + 2], I32)
        work = sb("work", [P, 8192])
        gathered = work[:, 0:(NT + 2) * TAPS0 * P].rearrange("p (j c) -> p j c", c=TAPS0 * P)
        h = sb("h", [P, NT, P])
        skip = sb("skip", [P, NT, P])
        slot_row = sb("slot_row", [P, NT, RW])
        xn = slot_row[:, :, 0:P]
        xT = sb("xT", [P, NT * P])
        lpad = sb("lpad", [P, T + 2 * HALO])
        early = sb("early", [P, 4, T])
        gl, lx, rg, ig = (early[:, n, :] for n in range(4))
        late = sb("late", [P, 2, T])
        ra, rb = (late[:, n, :] for n in range(2))
        zc = sb("zc", [P, 2, GC])
        sq = sb("sq", [P, 2, GC])
        bn = sb("bn", [P, NT, 6])
        mv = sb("mv", [P, NT, 2])
        std = sb("std", [P, NT])
        rstd = sb("rstd", [P, NT])
        nrm = sb("nrm", [P, NT])
        qs = sb("qs", [P, NT])
        lamv = sb("lamv", [P, 12])
        lg0 = sb("lg0", [P, NT, E0])
        top = sb("top", [P, NT, 8])
        topi = sb("topi", [P, NT, 8], U32)
        topf = sb("topf", [P, NT, 8])
        hot = sb("hot", [P, NT, E1])
        comb = sb("comb", [P, NT, ES])
        combT = sb("combT", [ES, NT * P])
        lg1 = sb("lg1", [P, NT, E1])
        sm = sb("sm", [P, 4, NT])
        ss = sb("ss", [P, NT, E0])
        sc = sb("sc", [P, NT, E0])
        wmean = sb("wmean", [P, 2 * E0])
        area_pow = sb("area_pow", [P, (POW_LEVELS + 1) * 2 * NS])
        area_q = sb("area_q", [P, NT * P])
        area_st = sb("area_st", [P, NT * P])
        powers = area_pow[0:NS, :].rearrange("s (k c) -> s k c", c=2 * NS)
        woC = sb("woC", [NS, P])
        woD = sb("woD", [P, P])
        qT = area_q[0:NS, :].rearrange("s (i c) -> s i c", c=P)
        st = area_st[0:NS, :].rearrange("s (i c) -> s i c", c=P)
        carry = sb("carry", [NS, P + 1])
        blank = sb("blank", [P, P + RW])
        choice = area_st[:, 0:TOP1 * NT * E1].rearrange("p (k i e) -> p k i e", k=TOP1, i=NT)
        chosen = sb("chosen", [P, NT, E1], BF16)
        rank = area_st[:, TOP1 * NT * E1:(TOP1 + 1) * NT * E1].rearrange("p (i e) -> p i e", i=NT)
        cnt = sb("cnt", [P, 6, E1])
        cnt_i = sb("cnt_i", [P, E1], I32)
        slot_f = sb("slot_f", [P, TOP1, NT])
        slot = sb("slot", [P, TOP1, NT], I32)
        past = area_pow[0:1, 0:RT * E1].rearrange("p (t e) -> p t e", e=E1)
        expert_f = sb("expert_f", [1, RT])
        expert_of = sb("expert_of", [1, RT], I32)
        xin = area_q[:, 0:XRING * RW].rearrange("p (n c) -> p n c", c=RW)
        xinT = area_q[:, XRING * RW:XRING * RW + 2 * P].rearrange("p (n c) -> p n c", c=P)
        yout = area_q[:, XRING * RW + 2 * P:XRING * RW + (2 + NACC) * P].rearrange("p (n c) -> p n c", c=P)
        hpre = zc
        hT = sq[:].rearrange("p n (f c) -> p n f c", c=P)

        pst = ctx.enter_context(nc.psum_tensor("pst", [P, 8, GC], F32))
        bank = [pst[:, b, :] for b in range(8)]

        G, I = range(NG), range(NT)
        tr = BankQueue(nc, ctx, "transposed", bank[0:2],
                       [("xT_a", g) for g in G] + [("xT_b", g) for g in G] + [("xT_c", g) for g in G]
                       + [("combT0", g) for g in G] + [("xT_d", g) for g in G] + [("uT", g) for g in G]
                       + [("xT_e", g) for g in G] + [("combT1", g) for g in G])
        ma = BankQueue(nc, ctx, "for_act", bank[2:4],
                       [("l2", g) for g in G] + [(w, c) for c in G for w in ("r", "i")]
                       + [("hid0", g, e) for g in G for e in range(E0)]
                       + [("hid1", e, g, f) for e in range(SHARED) for g in G for f in range(FC)])
        mv_keys = [("woC",), ("woD",)]
        for i in range(NT):
            mv_keys += [("q", i)] + ([("pow", i)] if i < POW_LEVELS else [])
        mv_keys += [("l1", g) for g in G] + [(w, c) for c in G for w in ("z", "lx")]
        mv_keys += [("wm1", g, m) for g in G for m in range(MULT)]
        mv_keys += [("state", i) for i in I] + [("carry", k) for k in range(SCAN_LEVELS)]
        mq = BankQueue(nc, ctx, "for_dve", bank[4:6], mv_keys)
        tm_keys = [("pT", g) for g in G] + [("out0", g) for g in G] + [("logit0", g) for g in G]
        tm_keys += [("beta0", g) for g in G] + [("y0", i, half) for i in I for half in range(2)]
        tm_keys += [("hm", g) for g in G] + [("y_ssm", g) for g in G] + [("logit1", g) for g in G]
        tm_keys += [("rank",)] + [("b2", g) for g in G]
        tm_keys += [("y1", e, g) for e in range(SHARED) for g in G]
        tm = BankQueue(nc, ctx, "token_major", bank[6:8], tm_keys)

        ld_const = sem("ld_const")
        ld_ids = sem("ld_ids")
        ld_ssm = sem("ld_ssm")
        ld_attn = sem("ld_attn")
        ld_moe = sem("ld_moe")
        ld_rows = sem("ld_rows")
        ld_shared = sem("ld_shared")
        ld_w1 = sem("ld_w1")
        ld_w2 = sem("ld_w2")
        ld_slot = [sem(f"ld_slot{n}") for n in range(XRING)]
        blank_ready = sem("blank_ready")
        blank_stored = sem("blank_stored")
        chosen_ready = sem("chosen_ready")
        slot_ready = sem("slot_ready")
        dispatched = sem("dispatched")
        rx_filled, rx_emptied = sem("rx_filled"), sem("rx_emptied")
        rh_filled, rh_emptied = sem("rh_filled"), sem("rh_emptied")
        rt_filled, rt_emptied = sem("rt_filled"), sem("rt_emptied")
        ry_filled, ry_emptied = sem("ry_filled"), sem("ry_emptied")
        summed = [sem(f"summed{a}") for a in range(NACC)]
        ld_sum = [sem(f"ld_sum{a}") for a in range(NACC)]
        add_started = sem("add_started")
        total_ready = sem("total_ready")
        emb = [sem(f"emb{g}") for g in G]
        gate0 = sem("gate0")
        dve_step = sem("dve_step")
        pool_step = sem("pool_step")
        var_ready = sem("var_ready")
        std_ready = sem("std_ready")
        x_ready = sem("x_ready")
        lam_dve = sem("lam_dve")
        lam_act = sem("lam_act")
        ix_ready = sem("ix_ready")
        decay_ready = sem("decay_ready")
        prod_ready = sem("prod_ready")
        x1_ready = sem("x1_ready")
        ssq_ready = sem("ssq_ready")
        base_ready = sem("base_ready")
        gelu_ready = sem("gelu_ready")
        hid_ready = sem("hid_ready")
        centered = sem("centered")
        exp0_ready = sem("exp0_ready")
        gate0_dve = sem("gate0_dve")
        comb0_ready = sem("comb0_ready")
        y0_ready = sem("y0_ready")
        sq0_ready = sem("sq0_ready")
        ss0_ready = sem("ss0_ready")
        sd0_ready = sem("sd0_ready")
        v0_ready = sem("v0_ready")
        moe_ready = sem("moe_ready")
        hb_ready = sem("hb_ready")
        h2_base = sem("h2_base")
        exp1_dve = sem("exp1_dve")
        exp1_act = sem("exp1_act")
        comb1_ready = sem("comb1_ready")
        acc_ready = sem("acc_ready")
        out_done = sem("out_done")

        X_A, X_B, X_C, X_D, X_U, X_E = (NG * n for n in range(6))
        V_A, V_C, V_D, V_U, V_E = (NG * n for n in range(5))

        hid0 = work[:, 0:2 * E0 * GC].rearrange("p (s e c) -> p s e c", s=2, e=E0)
        hidm = work[:, 0:2 * MULT * GC].rearrange("p (s e c) -> p s e c", s=2, e=MULT)
        hid1 = late[:].rearrange("p s (e c) -> p s e c", e=FC)
        w_e1_all = early[:].rearrange("p a c -> p (a c)")
        w_e2_all = work
        sum_in = [skip[:].rearrange("p i d -> p (i d)"), xT[:], lpad[:, 0:T], ra]

        def routed_steps(eng, step):
            full = (RT - LEAD) // XRING
            for u in range(-LEAD, XRING):
                step(u, 0)
            with eng.Fori(1, full) as k:
                for u in range(XRING):
                    step(u, k)
            for u in range(XRING * full, RT):
                step(u, 0)

        block = ctx.enter_context(nc.Block())

        @block.sync
        def _(sp):
            sp.dma_start(tok[:], ids).then_inc(ld_ids, 16)
            for dst, src in ((w_a, ssm_a), (w_c, ssm_c), (w_d, ssm_d), (w_oT, ssm_woT), (w_bT, ssm_bT),
                             (w_iT, ssm_wiT)):
                sp.dma_start(dst[:], src).then_inc(ld_ssm, 16)
            sp.dma_start(ident[:], consts[:, 0:P]).then_inc(ld_const, 16)
            sp.dma_start(iota[:], consts[:, P:P + E1]).then_inc(ld_const, 16)
            sp.dma_start(col[:], cols).then_inc(ld_const, 16)
            sp.dma_start(token_id[:], consts_i).then_inc(ld_const, 16)
            sp.dma_start(w_attn[:], attn_w).then_inc(ld_attn, 16)
            sp.dma_start(w_dw[:], dw_w).then_inc(ld_attn, 16)
            sp.dma_start(w_m1[:], wm1).then_inc(ld_attn, 16)
            sp.dma_start(w_m2[:], wm2).then_inc(ld_attn, 16)
            sp.dma_start(row[:], rows.partition_broadcast(P)).then_inc(ld_rows, 16)
            for dst, src in ((w_g0, moe_wg), (w_e1, moe_w1), (w_e2, moe_w2), (w_beta, moe_beta),
                             (w_g1, gate_wT), (w_b2, ffn_b2)):
                sp.dma_start(dst[:], src).then_inc(ld_moe, 16)
            for dst, src in ((b1T, ffn_b1), (tri, consts_bf[:, 0:P]), (ones, consts_bf[:, P:2 * P]),
                             (tile_no, tile_ids)):
                sp.dma_start(dst[:], src).then_inc(ld_shared, 16)
            sp.wait_ge(blank_ready, 2)
            sp.dma_start(slots_dram.rearrange("(n p) c -> p n c", p=P),
                         blank[:, P:].unsqueeze(1).to_broadcast([P, RT, RW])).then_inc(blank_stored, 16)
            for a in range(NACC):
                sp.dma_start(sums_dram[a].rearrange("(n p) c -> p n c", p=P),
                             blank[:, 0:P].unsqueeze(1).to_broadcast([P, NT + 1, P])).then_inc(blank_stored, 16)
            sp.wait_ge(tm.filled, tm.at[("pT", NG - 1)] + 1)
            sp.dma_start(w_e1_all, ffn_w1[:, 0:E1, :].rearrange("p e f -> p (e f)")).then_inc(ld_w1, 16)
            sp.wait_ge(tm.filled, tm.at[("y0", NT - 1, 1)] + 1)
            sp.dma_start(w_sh1[:], ffn_w1[:, E1:ES, :]).then_inc(ld_shared, 16)
            sp.dma_start(w_sh2[:], ffn_w2[:, E1:ES, :]).then_inc(ld_shared, 16)
            sp.dma_start(w_e2_all[:], ffn_w2[:, 0:E1, :].rearrange("p e f -> p (e f)")).then_inc(ld_w2, 16)
            sp.wait_ge(dispatched, 16 * NT * TOP1)

            def load(n, k):
                if n >= XRING or not isinstance(k, int):
                    sp.wait_ge(summed[n % NACC], 16 * (n // NACC - 1 + k * (XRING // NACC)))
                sp.dma_start(xin[:, n % XRING, :],
                             slots_dram[bass.ds((k * XRING + n) * P, P), :]).then_inc(ld_slot[n % XRING], 16)

            for n in range(XRING):
                load(n, 0)
            with sp.Fori(1, RT // XRING) as k:
                for n in range(XRING):
                    load(n, k)
            for a in range(NACC):
                sp.wait_ge(summed[a], 16 * (RT // NACC))
                if a == 0:
                    sp.wait_ge(ry_filled, RT)
                sp.dma_start(sum_in[a], sums_dram[a][0:T, :].rearrange("(p i) d -> p (i d)", i=NT)
                             ).then_inc(ld_sum[a], 16)
            sp.wait_ge(total_ready, 1)
            sp.dma_start(out[0].rearrange("(p i) d -> p i d", i=NT), h[:]).then_inc(out_done, 16)
            sp.wait_ge(out_done, 16)

        @block.gpsimd
        def _(pool):
            steps = [0]

            def link(ins):
                steps[0] += 1
                ins.then_inc(pool_step, 1)
                pool.wait_ge(pool_step, steps[0])

            nc.gpsimd.memset(blank[:], 0.0).then_inc(blank_ready, 1)
            link(nc.gpsimd.memset(gathered[:, NT + 1, :], 0.0))
            pool.wait_ge(ld_ids, 16)
            for j in range(NT + 2):
                n = P - 1 if j == NT + 1 else P
                g = max(0, min((j - 2) // GT, NG - 1))
                pool.indirect_dma_start(
                    out=gathered[0:n, j, :], out_offset=None, in_=table,
                    in_offset=bass.IndirectOffsetOnAxis(ap=tok[0:n, j:j + 1], axis=0)).then_inc(emb[g], 16)
            pool.wait_ge(ld_rows, 16)
            for g in G:
                s = slice(g * GT, (g + 1) * GT)
                pool.wait_ge(x1_ready, g + 1)
                link(nc.gpsimd.tensor_tensor(h[:, s, :], h[:, s, :], skip[:, s, :], ALU.add))
                nc.gpsimd.tensor_tensor(
                    h[:, s, :], h[:, s, :],
                    spread_row(ROW_BM2).unsqueeze(1).to_broadcast([P, GT, P]), ALU.add).then_inc(base_ready, 1)
            for i in I:
                for half in range(2):
                    n = 2 * i + half
                    pool.wait_ge(v0_ready, n + 1)
                    v = rb[:, (n % 4) * GC:(n % 4 + 1) * GC]
                    link(nc.gpsimd.tensor_tensor(v, v, spread_row(ROW_GAMMA + 4 * half, 4), ALU.mult))
                    link(nc.gpsimd.tensor_tensor(v[:, 0:2 * P], v[:, 0:2 * P], v[:, 2 * P:4 * P], ALU.add))
                    link(nc.gpsimd.tensor_tensor(v[:, 0:P], v[:, 0:P], v[:, P:2 * P], ALU.add))
                    if n == 0:
                        pool.wait_ge(hb_ready, NG)
                    nc.gpsimd.tensor_tensor(h[:, i, :], h[:, i, :], v[:, 0:P], ALU.add).then_inc(moe_ready, 1)
                    pool.wait_ge(moe_ready, n + 1)
            for g in G:
                s = slice(g * GT, (g + 1) * GT)
                pool.wait_ge(x_ready, X_D + g + 1)
                nc.gpsimd.tensor_tensor(
                    h[:, s, :], h[:, s, :],
                    spread_row(ROW_BO).unsqueeze(1).to_broadcast([P, GT, P]), ALU.add).then_inc(h2_base, 1)
            pool.wait_ge(blank_stored, 16 * (1 + NACC))
            pool.wait_ge(slot_ready, 1)
            for i in I:
                for k in range(TOP1):
                    pool.indirect_dma_start(
                        out=slots_dram, out_offset=bass.IndirectOffsetOnAxis(ap=slot[:, k, i:i + 1], axis=0),
                        in_=slot_row[:, i, :], in_offset=None).then_inc(dispatched, 16)

            def add_rows(n, k):
                a = n % NACC
                pool.wait_ge(ry_emptied, n + 1 + k * XRING)
                if n >= NACC or not isinstance(k, int):
                    pool.wait_ge(summed[a], 16 * (n // NACC + k * (XRING // NACC)))
                pool.sem_inc(add_started, 1)
                pool.indirect_dma_start(
                    out=sums_dram[a],
                    out_offset=bass.IndirectOffsetOnAxis(ap=xin[:, n % XRING, R_ID:R_ID + 1].bitcast(I32), axis=0),
                    in_=yout[:, a, :], in_offset=None, compute_op=ALU.add).then_inc(summed[a], 16)

            for n in range(XRING):
                add_rows(n, 0)
            with pool.Fori(1, RT // XRING) as k:
                for n in range(XRING):
                    add_rows(n, k)

        @block.scalar
        def _(act):
            def root(first, g):
                s = slice(g * GT, (g + 1) * GT)
                act.wait_ge(var_ready, first + g + 1)
                if first == V_A:
                    nc.scalar.activation(nrm[:, s], mv[:, s, 1], ACT.Sqrt, scale=float(P))
                nc.scalar.activation(std[:, s], mv[:, s, 1], ACT.Sqrt, bias=eps_ln).then_inc(std_ready, 1)

            def take_xT(key, g, scale=None, bias=None):
                src = tr.full(act, (key, g))
                dst = xT[:, g * GC:(g + 1) * GC]
                if scale is None:
                    nc.scalar.copy(dst, src).then_inc(tr.emptied, 1)
                elif bias is None:
                    nc.scalar.activation(dst, src, ACT.Copy, scale=scale).then_inc(tr.emptied, 1)
                else:
                    nc.scalar.activation(dst, src, ACT.Identity, scale=scale, bias=bias).then_inc(tr.emptied, 1)

            eps_ln = LN_EPS
            act.wait_ge(ld_const, 64)
            act.wait_ge(lam_dve, 1)
            nc.scalar.activation(lamv[:, 1:2], lamv[:, 0:1], ACT.Exp).then_inc(lam_act, 1)
            act.wait_ge(lam_dve, 2)
            nc.scalar.activation(lamv[:, 3:4], lamv[:, 2:3], ACT.Ln).then_inc(lam_act, 1)
            for g in G:
                root(V_A, g)
            for g in G:
                take_xT("xT_a", g, scale=column("g"))
            for g in G:
                src = ma.full(act, ("l2", g))
                nc.scalar.activation(gl[:, g * GC:(g + 1) * GC], src, ACT.Gelu,
                                     bias=column("b2")).then_inc(ma.emptied, 1)
            for c in G:
                for key, dst, b in (("r", rg, "br"), ("i", ig, "bi")):
                    src = ma.full(act, (key, c))
                    nc.scalar.activation(dst[:, c * GC:(c + 1) * GC], src, ACT.Sigmoid,
                                         bias=column(b)).then_inc(ma.emptied, 1)
            ma.taken(act, ("i", NG - 1))
            act.wait_ge(lam_dve, 4)
            nc.scalar.activation(ra[:], rg[:], ACT.Exp, scale=lamv[:, 8:9]).then_inc(decay_ready, 1)
            nc.scalar.activation(rb[:], rg[:], ACT.Exp, scale=lamv[:, 9:10]).then_inc(decay_ready, 1)
            act.wait_ge(decay_ready, 2)
            nc.scalar.activation(rb[:], rb[:], ACT.Sqrt, scale=-1.0, bias=1.0).then_inc(decay_ready, 1)
            for g in G:
                act.wait_ge(x1_ready, g + 1)
                for i in range(g * GT, (g + 1) * GT):
                    last = nc.scalar.activation(sq[:, 0, (i % GT) * P:(i % GT + 1) * P], skip[:, i, :],
                                                ACT.Square, accum_out=nrm[:, i:i + 1])
                last.then_inc(ssq_ready, 1)
                act.wait_ge(ssq_ready, 2 * g + 1)
                s = slice(g * GT, (g + 1) * GT)
                nc.scalar.activation(std[:, s], nrm[:, s], ACT.Sqrt).then_inc(ssq_ready, 1)
            for g in G:
                take_xT("xT_b", g, scale=column("g"))
            for g in G:
                for m in range(MULT):
                    n = g * MULT + m
                    src = mq.full(act, ("wm1", g, m))
                    if n >= 2:
                        act.wait_ge(hid_ready, n - 1)
                    nc.scalar.activation(zc[:, n % 2, :], src, ACT.Gelu,
                                         bias=column(f"bm1_{m}")).then_inc(gelu_ready, 1)
            for g in G:
                root(V_C, g)
            for g in G:
                take_xT("xT_c", g)
            act.wait_ge(exp0_ready, 1)
            nc.scalar.activation(sm[:, 1, :], sm[:, 0, :], ACT.Exp).then_inc(gate0, 1)
            for g in G:
                src = tr.full(act, ("combT0", g))
                nc.scalar.copy(combT[0:E0, g * GC:(g + 1) * GC], src[0:E0, :]).then_inc(tr.emptied, 1)

            def hidden0(g):
                if g >= 2:
                    act.wait_ge(tm.filled, tm.at[("y0", (g - 1) * GT - 1, 1)] + 1)
                for e in range(E0):
                    src = ma.full(act, ("hid0", g, e))
                    nc.scalar.activation(hid0[:, g % 2, e, :], src, ACT.Relu,
                                         bias=column(f"moe_b1_{e}")).then_inc(ma.emptied, 1)

            def squares(i):
                for half in range(2):
                    n = 2 * i + half
                    act.wait_ge(y0_ready, n + 1)
                    if n >= 2:
                        act.wait_ge(ss0_ready, n - 1)
                    nc.scalar.activation(sq[:, n % 2, :], ra[:, (n % 4) * GC:(n % 4 + 1) * GC],
                                         ACT.Square).then_inc(sq0_ready, 1)

            def deviation(i):
                act.wait_ge(ss0_ready, 2 * i + 2)
                nc.scalar.activation(ss[:, i, :], ss[:, i, :], ACT.Sqrt, scale=1.0 / P,
                                     bias=eps_ln).then_inc(sd0_ready, 1)

            hidden0(0)
            for g in G:
                if g + 1 < NG:
                    hidden0(g + 1)
                for i in range(g * GT, (g + 1) * GT):
                    squares(i)
                    deviation(i)
            for g in G:
                root(V_D, g)
            for g in G:
                take_xT("xT_d", g)
            for g in G:
                root(V_U, g)
            for g in G:
                take_xT("uT", g, scale=column("gamma"), bias=column("beta"))
            for g in G:
                root(V_E, g)
            for g in G:
                take_xT("xT_e", g)
            act.wait_ge(exp1_dve, 1)
            nc.scalar.activation(lg1[:], lg1[:], ACT.Exp).then_inc(exp1_act, 1)
            act.wait_ge(exp1_dve, 2)
            nc.scalar.activation(top[:, :, 0:TOP1], top[:, :, 0:TOP1], ACT.Exp).then_inc(exp1_act, 1)
            for g in G:
                src = tr.full(act, ("combT1", g))
                nc.scalar.copy(combT[:, g * GC:(g + 1) * GC], src[0:ES, :]).then_inc(tr.emptied, 1)
            act.wait_ge(ld_shared, 96)
            for e in range(SHARED):
                for g in G:
                    n = e * NG + g
                    if n >= 2:
                        act.wait_ge(tm.filled, tm.at[("y1", 0, 0)] + n - 1)
                    for f in range(FC):
                        b = (E1 + e) * FC + f
                        src = ma.full(act, ("hid1", e, g, f))
                        nc.scalar.activation(hid1[:, n % 2, f, :], src, ACT.Gelu,
                                             bias=b1T[:, b:b + 1]).then_inc(ma.emptied, 1)

            act.wait_ge(slot_ready, 1)

            def step(s, k):
                n = s + 1
                if n < 0 or n >= RT:
                    return
                at = k * XRING + n
                act.wait_ge(rt_filled, at + 1)
                e = act.value_load(expert_of[0:1, bass.ds(at, 1)], min_val=0, max_val=E1 - 1)
                for f in range(FC):
                    ins = nc.scalar.activation(hT[:, n % 2, f, :], bank[4 + n % 2][:, f * P:(f + 1) * P],
                                               ACT.Gelu, bias=b1T[:, bass.ds(e * FC + f, 1)])
                ins.then_inc(rt_emptied, 1)

            routed_steps(act, step)

        @block.vector
        def _(dve):
            steps = [0]

            def mark(ins):
                steps[0] += 1
                ins.then_inc(dve_step, 1)

            def settle():
                dve.wait_ge(dve_step, steps[0])

            def link(ins):
                mark(ins)
                settle()

            def stats(src, g):
                for i in range(g * GT, (g + 1) * GT):
                    ins = nc.vector.bn_stats(bn[:, i, :], src[:, i, :])
                link(ins)
                for i in range(g * GT, (g + 1) * GT):
                    ins = nc.vector.bn_aggr(mv[:, i, :], bn[:, i, :])
                ins.then_inc(var_ready, 1)

            def normalise(src, dst, first, g, scale=None, signal=True):
                s = slice(g * GT, (g + 1) * GT)
                if scale is None:
                    dve.wait_ge(std_ready, first + g + 1)
                    link(nc.vector.reciprocal(rstd[:, s], std[:, s]))
                    scale = rstd
                for i in range(g * GT, (g + 1) * GT):
                    ins = nc.vector.tensor_scalar(dst[:, i, :], src[:, i, :], mv[:, i, 0:1],
                                                  scale[:, i:i + 1], ALU.subtract, ALU.mult)
                if signal:
                    ins.then_inc(x_ready, 1)
                else:
                    mark(ins)

            def copy_out(queue, key, dst, rows=P, width=GC):
                src = queue.full(dve, key)
                nc.vector.tensor_copy(dst, src[0:rows, 0:width]).then_inc(queue.emptied, 1)

            dve.wait_ge(blank_ready, 1)
            dve.wait_ge(ld_const, 64)
            nc.vector.tensor_copy(blank[:, P + R_ID:P + R_ID + 1].bitcast(I32),
                                  token_id[:, NT:NT + 1]).then_inc(blank_ready, 1)
            mark(nc.vector.memset(lpad[:, 0:HALO], 0.0))
            mark(nc.vector.memset(lpad[:, HALO + T:], 0.0))
            mark(nc.vector.memset(carry[:, 0:1], 0.0))
            link(nc.vector.memset(comb[:, :, E1:ES], 1.0 / SHARED))
            dve.wait_ge(ld_const, 64)
            lam = column("lam")
            link(nc.vector.tensor_scalar(lamv[:, 10:11], lam, -1.0, None, ALU.mult))
            link(nc.vector.tensor_tensor(lamv[:, 11:12], lam, lamv[:, 10:11], ALU.max))
            nc.vector.tensor_scalar(lamv[:, 0:1], lamv[:, 11:12], -1.0, None, ALU.mult).then_inc(lam_dve, 1)
            dve.wait_ge(lam_act, 1)
            nc.vector.tensor_scalar(lamv[:, 2:3], lamv[:, 1:2], 1.0, None, ALU.add).then_inc(lam_dve, 1)
            dve.wait_ge(lam_dve, 2)
            link(nc.vector.tensor_scalar(lamv[:, 4:5], lamv[:, 2:3], -1.0, None, ALU.add))
            link(nc.vector.tensor_scalar(lamv[:, 5:6], lamv[:, 4:5], 1e-30, None, ALU.max))
            link(nc.vector.reciprocal(lamv[:, 5:6], lamv[:, 5:6]))
            dve.wait_ge(lam_act, 2)
            link(nc.vector.tensor_tensor(lamv[:, 6:7], lamv[:, 3:4], lamv[:, 5:6], ALU.mult))
            link(nc.vector.scalar_tensor_tensor(out=lamv[:, 6:7], in0=lamv[:, 4:5], scalar=0.0,
                                                in1=lamv[:, 6:7], op0=ALU.is_equal, op1=ALU.add))
            link(nc.vector.tensor_tensor(lamv[:, 6:7], lamv[:, 6:7], lamv[:, 1:2], ALU.mult))
            link(nc.vector.scalar_tensor_tensor(out=lamv[:, 7:8], in0=lam, scalar=0.0,
                                                in1=lamv[:, 6:7], op0=ALU.max, op1=ALU.add))
            nc.vector.tensor_scalar(lamv[:, 8:9], lamv[:, 7:8], -8.0, None, ALU.mult).then_inc(lam_dve, 1)
            nc.vector.tensor_scalar(lamv[:, 9:10], lamv[:, 7:8], -16.0, None, ALU.mult).then_inc(lam_dve, 1)
            copy_out(mq, ("woC",), woC[:], NS, P)
            copy_out(mq, ("woD",), woD[:], P, P)
            for i in I:
                copy_out(mq, ("q", i), qT[:, i, :], NS, P)
                if i < POW_LEVELS:
                    copy_out(mq, ("pow", i), powers[:, i + 1, :], NS, 2 * NS)
            for g in G:
                s = slice(g * GT, (g + 1) * GT)
                dve.wait_ge(emb[g], 16 * ((GT + 2) if g == 0 else GT))
                if g == 0:
                    link(nc.vector.memset(gathered[0:1, 0, :], 0.0))
                link(nc.vector.tensor_tensor(h[:, s, :], gathered[:, g * GT:(g + 1) * GT, 0:P],
                                             gathered[:, g * GT + 1:(g + 1) * GT + 1, P:2 * P], ALU.add))
                link(nc.vector.tensor_tensor(h[:, s, :], h[:, s, :],
                                             gathered[:, g * GT + 2:(g + 1) * GT + 2, 2 * P:3 * P], ALU.add))
                stats(h, g)
            for g in G:
                s = slice(g * GT, (g + 1) * GT)
                dve.wait_ge(std_ready, V_A + g + 1)
                link(nc.vector.reciprocal(rstd[:, s], std[:, s]))
                link(nc.vector.tensor_tensor(qs[:, s], nrm[:, s], rstd[:, s], ALU.mult))
                link(nc.vector.tensor_scalar(qs[:, s], qs[:, s], RMS_EPS, None, ALU.add))
                link(nc.vector.reciprocal(qs[:, s], qs[:, s]))
                link(nc.vector.scalar_tensor_tensor(out=qs[:, s], in0=qs[:, s], scalar=SQD, in1=rstd[:, s],
                                                    op0=ALU.mult, op1=ALU.mult))
                normalise(h, xn, V_A, g, scale=qs)
            for g in G:
                normalise(h, skip, V_A, g, scale=rstd, signal=False)
            for g in G:
                src = mq.full(dve, ("l1", g)).rearrange("f (i p) -> f i p", i=GT)
                dst = lpad[:, HALO:HALO + T].rearrange("f (p i) -> f i p", i=NT)[:, g * GT:(g + 1) * GT, :]
                nc.vector.tensor_scalar(dst, src, column("b1"), None, ALU.add).then_inc(mq.emptied, 1)
            for c in G:
                src = mq.full(dve, ("z", c))
                nc.vector.tensor_scalar(zc[:, c % 2, :], src, column("dw_b"), None,
                                        ALU.add).then_inc(mq.emptied, 1)
                src = mq.full(dve, ("lx", c))
                nc.vector.tensor_scalar(lx[:, c * GC:(c + 1) * GC], src, column("pw_b"), None,
                                        ALU.add).then_inc(mq.emptied, 1)
            for c in G:
                s = slice(c * GC, (c + 1) * GC)
                ma.taken(dve, ("i", c))
                link(nc.vector.tensor_tensor(ig[:, s], ig[:, s], lx[:, s], ALU.mult))
            dve.wait_ge(decay_ready, 3)
            link(nc.vector.tensor_tensor(ig[:], ig[:], rb[:], ALU.mult))
            link(nc.vector.tensor_tensor_scan(lx[:], ra[:], ig[:], 0.0, ALU.mult, ALU.add))
            prod = rg
            for g in G:
                s = slice(g * GT, (g + 1) * GT)
                nc.vector.tensor_tensor(prod[:, g * GC:(g + 1) * GC].rearrange("f (i p) -> f i p", i=GT),
                                        lx[:].rearrange("f (p i) -> f i p", i=NT)[:, s, :],
                                        gl[:, g * GC:(g + 1) * GC].rearrange("f (i p) -> f i p", i=GT),
                                        ALU.mult).then_inc(prod_ready, 1)
            for g in G:
                s = slice(g * GT, (g + 1) * GT)
                src = tm.full(dve, ("pT", g)).rearrange("p (i f) -> p i f", i=GT)
                nc.vector.tensor_tensor(skip[:, s, :], src, skip[:, s, :], ALU.add).then_inc(tm.emptied, 1)
                tm.taken(dve, ("pT", g))
                link(nc.vector.tensor_copy(qs[:, s], rstd[:, s]))
                dve.sem_inc(x1_ready, 1)
            for g in G:
                s = slice(g * GT, (g + 1) * GT)
                dve.wait_ge(ssq_ready, 2 * g + 2)
                link(nc.vector.tensor_scalar(qs[:, s], std[:, s], RMS_EPS, None, ALU.add))
                link(nc.vector.reciprocal(qs[:, s], qs[:, s]))
                for i in range(g * GT, (g + 1) * GT):
                    ins = nc.vector.tensor_scalar(xn[:, i, :], skip[:, i, :], qs[:, i:i + 1], SQD,
                                                  ALU.mult, ALU.mult)
                ins.then_inc(x_ready, 1)
            for g in G:
                for m in range(MULT):
                    n = g * MULT + m
                    dve.wait_ge(gelu_ready, n + 1)
                    src = mq.full(dve, ("wm1", g, m))
                    if m == 0 and g >= 2:
                        dve.wait_ge(tm.filled, tm.at[("out0", g - 2)] + 1)
                    mark(nc.vector.scalar_tensor_tensor(
                        out=hidm[:, g % 2, m, :], in0=src, scalar=column(f"bm1_{m}"), in1=zc[:, n % 2, :],
                        op0=ALU.add, op1=ALU.mult))
                    settle()
                    dve.sem_inc(hid_ready, 1)
                    dve.sem_inc(mq.emptied, 1)
            for g in G:
                s = slice(g * GT, (g + 1) * GT)
                dve.wait_ge(base_ready, g + 1)
                src = tm.full(dve, ("out0", g)).rearrange("p (i f) -> p i f", i=GT)
                nc.vector.tensor_tensor(h[:, s, :], src, h[:, s, :], ALU.add).then_inc(tm.emptied, 1)
            dve.wait_ge(ld_moe, 96)
            link(nc.vector.tensor_reduce(wmean[:, 0:E0], w_e2[:], AX.X, ALU.add))
            link(nc.vector.tensor_reduce(wmean[:, E0:], spread_row(ROW_B2, E0).rearrange("p (e d) -> p e d", e=E0),
                                         AX.X, ALU.add))
            link(nc.vector.tensor_scalar(wmean[:], wmean[:], 1.0 / P, None, ALU.mult))
            for e in range(E0):
                mark(nc.vector.tensor_scalar(w_e2[:, e, :], w_e2[:, e, :], wmean[:, e:e + 1], None, ALU.subtract))
                b = spread_row(ROW_B2 + e)
                ins = nc.vector.tensor_scalar(b, b, wmean[:, E0 + e:E0 + e + 1], None, ALU.subtract)
            ins.then_inc(centered, 1)
            for g in G:
                tm.taken(dve, ("out0", g))
                stats(h, g)
            for g in G:
                normalise(h, xn, V_C, g)
            for g in G:
                src = tm.full(dve, ("logit0", g))[:, 0:GT * E0].rearrange("p (i e) -> p i e", i=GT)
                nc.vector.tensor_copy(lg0[:, g * GT:(g + 1) * GT, :], src).then_inc(tm.emptied, 1)
            tm.taken(dve, ("logit0", NG - 1))
            for i in I:
                mark(nc.vector.max(top[:, i, :], lg0[:, i, :]))
            settle()
            for i in I:
                mark(nc.vector.max_index(topi[:, i, :], top[:, i, :], lg0[:, i, :]))
            nc.vector.tensor_tensor(sm[:, 0, :], top[:, :, 1], top[:, :, 0], ALU.subtract).then_inc(exp0_ready, 1)
            settle()
            link(nc.vector.tensor_copy(topf[:], topi[:]))
            dve.wait_ge(gate0, 1)
            link(nc.vector.tensor_scalar(sm[:, 2, :], sm[:, 1, :], 1.0, None, ALU.add))
            link(nc.vector.reciprocal(sm[:, 2, :], sm[:, 2, :]))
            link(nc.vector.tensor_tensor(sm[:, 3, :], sm[:, 1, :], sm[:, 2, :], ALU.mult))

            def one_hot(dst, tmp, k, weight, n, keep=None):
                out_ = dst if k == 0 else tmp
                io = iota[:, 0:n].unsqueeze(1).to_broadcast([P, NT, n])
                hit = out_ if keep is None else keep
                link(nc.vector.tensor_tensor(hit, io, topf[:, :, k:k + 1].to_broadcast([P, NT, n]), ALU.is_equal))
                link(nc.vector.tensor_tensor(out_, hit, weight.to_broadcast([P, NT, n]), ALU.mult))
                if k:
                    link(nc.vector.tensor_tensor(dst, dst, tmp, ALU.add))

            comb0 = comb[:, :, 0:E0]
            for k in range(2):
                one_hot(comb0, hot[:, :, 0:E0], k, sm[:, 2 + k, :].unsqueeze(2), E0)
            dve.sem_inc(comb0_ready, 1)
            for g in G:
                s = slice(g * GT, (g + 1) * GT)
                src = tm.full(dve, ("beta0", g)).rearrange("p (i f) -> p i f", i=GT)
                nc.vector.tensor_tensor(h[:, s, :], src, h[:, s, :], ALU.add).then_inc(tm.emptied, 1)
            tm.taken(dve, ("beta0", NG - 1))
            dve.sem_inc(hb_ready, NG)

            def y_of(n):
                return ra[:, (n % 4) * GC:(n % 4 + 1) * GC]

            def take_y(n):
                src = tm.full(dve, ("y0", n // 2, n % 2))
                nc.vector.tensor_tensor(y_of(n), src, spread_row(ROW_B2 + 4 * (n % 2), 4),
                                        ALU.add).then_inc(tm.emptied, 1)
                tm.taken(dve, ("y0", n // 2, n % 2))
                dve.sem_inc(y0_ready, 1)

            def sum_squares(n):
                dve.wait_ge(sq0_ready, n + 1)
                nc.vector.tensor_reduce(ss[:, n // 2, 4 * (n % 2):4 * (n % 2) + 4],
                                        sq[:, n % 2, :].rearrange("p (e d) -> p e d", e=4), AX.X,
                                        ALU.add).then_inc(ss0_ready, 1)

            def scale_tile(i):
                dve.wait_ge(sd0_ready, i + 1)
                link(nc.vector.reciprocal(sc[:, i, :], ss[:, i, :]))
                link(nc.vector.tensor_tensor(sc[:, i, :], sc[:, i, :], comb[:, i, 0:E0], ALU.mult))
                for half in range(2):
                    n = 2 * i + half
                    if n >= 4:
                        dve.wait_ge(moe_ready, n - 3)
                    nc.vector.tensor_tensor(
                        rb[:, (n % 4) * GC:(n % 4 + 1) * GC].rearrange("p (e d) -> p e d", e=4),
                        y_of(n).rearrange("p (e d) -> p e d", e=4),
                        sc[:, i, 4 * half:4 * half + 4].unsqueeze(2).to_broadcast([P, 4, P]),
                        ALU.mult).then_inc(v0_ready, 1)

            for i in range(NT + 1):
                if i < NT:
                    if i >= 2:
                        dve.wait_ge(v0_ready, 2 * (i - 1))
                    take_y(2 * i)
                    take_y(2 * i + 1)
                if i >= 1:
                    scale_tile(i - 1)
                if i < NT:
                    sum_squares(2 * i)
                    sum_squares(2 * i + 1)
            for g in G:
                dve.wait_ge(moe_ready, 2 * GT * (g + 1))
                stats(h, g)
            for g in G:
                normalise(h, xn, V_D, g)
            for g in G:
                s = slice(g * GT, (g + 1) * GT)
                src = tm.full(dve, ("hm", g)).rearrange("p (i f) -> p i f", i=GT)
                nc.vector.tensor_tensor(skip[:, s, :], src,
                                        spread_row(ROW_BI).unsqueeze(1).to_broadcast([P, GT, P]),
                                        ALU.add).then_inc(tm.emptied, 1)
                tm.taken(dve, ("hm", g))
                stats(skip, g)
            for g in G:
                normalise(skip, xn, V_U, g)
            for i in I:
                copy_out(mq, ("state", i), st[:, i, :], NS, P)
            mq.taken(dve, ("state", NT - 1))
            mark(nc.vector.tensor_copy(carry[:, 1:P + 1], st[:, NT - 1, :]))
            settle()
            dve.sem_inc(gate0_dve, 1)
            for k in range(SCAN_LEVELS):
                w = P - 2 ** k
                src = mq.full(dve, ("carry", k))
                nc.vector.tensor_tensor(carry[:, 1 + 2 ** k:P + 1], carry[:, 1 + 2 ** k:P + 1],
                                        src[0:NS, 0:w], ALU.add).then_inc(mq.emptied, 1)
                mq.taken(dve, ("carry", k))
            for g in G:
                s = slice(g * GT, (g + 1) * GT)
                dve.wait_ge(h2_base, g + 1)
                src = tm.full(dve, ("y_ssm", g)).rearrange("p (i f) -> p i f", i=GT)
                nc.vector.tensor_tensor(h[:, s, :], src, h[:, s, :], ALU.add).then_inc(tm.emptied, 1)
                tm.taken(dve, ("y_ssm", g))
                stats(h, g)
            for g in G:
                normalise(h, xn, V_E, g)
            for g in G:
                src = tm.full(dve, ("logit1", g))[:, 0:GT * E1].rearrange("p (i e) -> p i e", i=GT)
                nc.vector.tensor_copy(lg1[:, g * GT:(g + 1) * GT, :], src).then_inc(tm.emptied, 1)
            tm.taken(dve, ("logit1", NG - 1))
            link(nc.vector.tensor_reduce(sm[:, 0, :], lg1[:], AX.X, ALU.max))
            nc.vector.tensor_tensor(lg1[:], lg1[:], sm[:, 0, :].unsqueeze(2).to_broadcast([P, NT, E1]),
                                    ALU.subtract).then_inc(exp1_dve, 1)
            dve.wait_ge(exp1_act, 1)
            link(nc.vector.tensor_reduce(sm[:, 1, :], lg1[:], AX.X, ALU.add))
            link(nc.vector.reciprocal(sm[:, 1, :], sm[:, 1, :]))
            link(nc.vector.tensor_tensor(lg1[:], lg1[:], sm[:, 1, :].unsqueeze(2).to_broadcast([P, NT, E1]),
                                         ALU.mult))
            for i in I:
                mark(nc.vector.max(top[:, i, :], lg1[:, i, :]))
            settle()
            for i in I:
                mark(nc.vector.max_index(topi[:, i, :], top[:, i, :], lg1[:, i, :]))
            settle()
            link(nc.vector.tensor_copy(topf[:], topi[:]))
            link(nc.vector.tensor_copy(sm[:, 2, :], top[:, :, 0]))
            nc.vector.tensor_tensor(top[:, :, 0:TOP1], top[:, :, 0:TOP1],
                                    sm[:, 2, :].unsqueeze(2).to_broadcast([P, NT, TOP1]),
                                    ALU.subtract).then_inc(exp1_dve, 1)
            dve.wait_ge(exp1_act, 2)
            link(nc.vector.tensor_reduce(sm[:, 3, :], top[:, :, 0:TOP1], AX.X, ALU.add))
            link(nc.vector.reciprocal(sm[:, 3, :], sm[:, 3, :]))
            link(nc.vector.tensor_tensor(top[:, :, 0:TOP1], top[:, :, 0:TOP1],
                                         sm[:, 3, :].unsqueeze(2).to_broadcast([P, NT, TOP1]), ALU.mult))
            comb1 = comb[:, :, 0:E1]
            for k in range(TOP1):
                one_hot(comb1, hot[:], k, top[:, :, k:k + 1], E1, choice[:, k])
            dve.sem_inc(comb1_ready, 1)
            link(nc.vector.tensor_tensor(hot[:], choice[:, 0], choice[:, 1], ALU.add))
            link(nc.vector.tensor_tensor(hot[:], hot[:], choice[:, 2], ALU.add))
            nc.vector.tensor_tensor(chosen[:], hot[:], choice[:, 3], ALU.add).then_inc(chosen_ready, 1)
            mark(nc.vector.tensor_copy(slot_row[:, :, R_COMB:], comb[:, :, 0:E1]))
            mark(nc.vector.tensor_copy(slot_row[:, :, R_ID:R_ID + 1].bitcast(I32), token_id[:, 0:NT].unsqueeze(2)))
            mark(nc.vector.memset(cnt[:, 5, :], 1.0))
            src = tm.full(dve, ("rank",))
            mark(nc.vector.tensor_copy(rank[:], src[:, 0:NT * E1].rearrange("p (i e) -> p i e", i=NT)))
            nc.vector.tensor_scalar(cnt[:, 0, :], src[:, NT * E1:NT * E1 + E1], float(P - 1), None,
                                    ALU.add).then_inc(tm.emptied, 1)
            tm.taken(dve, ("rank",))
            link(nc.vector.tensor_copy(cnt_i[:], cnt[:, 0, :]))
            link(nc.vector.tensor_scalar(cnt_i[:], cnt_i[:], P.bit_length() - 1, None, ALU.arith_shift_right))
            link(nc.vector.tensor_copy(cnt[:, 1, :], cnt_i[:]))
            link(nc.vector.tensor_tensor_scan(cnt[:, 2, :], cnt[:, 5, :], cnt[:, 1, :], 0.0, ALU.mult, ALU.add))
            link(nc.vector.tensor_tensor(cnt[:, 3, :], cnt[:, 2, :], cnt[:, 1, :], ALU.subtract))
            link(nc.vector.tensor_scalar(cnt[:, 4, :], cnt[:, 3, :], float(P), None, ALU.mult))
            link(nc.vector.tensor_tensor(rank[:], rank[:], cnt[:, 4, :].unsqueeze(1).to_broadcast([P, NT, E1]),
                                         ALU.add))
            for k in range(TOP1):
                mark(nc.vector.tensor_tensor(choice[:, k], choice[:, k], rank[:], ALU.mult))
            settle()
            link(nc.vector.tensor_reduce(slot_f[:], choice[:], AX.X, ALU.add))
            mark(nc.vector.tensor_copy(slot[:], slot_f[:]))
            link(nc.vector.tensor_tensor(past[:], tile_no[:].unsqueeze(2).to_broadcast([1, RT, E1]),
                                         cnt[0:1, 2, :].unsqueeze(1).to_broadcast([1, RT, E1]), ALU.is_ge))
            link(nc.vector.tensor_reduce(expert_f[:], past[:], AX.X, ALU.add))
            nc.vector.tensor_scalar(expert_of[:], expert_f[:], float(E1 - 1), None,
                                    ALU.min).then_inc(slot_ready, 1)
            for g in G:
                s = slice(g * GT, (g + 1) * GT)
                src = tm.full(dve, ("b2", g)).rearrange("p (i f) -> p i f", i=GT)
                nc.vector.tensor_tensor(h[:, s, :], src, h[:, s, :], ALU.add).then_inc(tm.emptied, 1)
            for e in range(SHARED):
                for g in G:
                    src = tm.full(dve, ("y1", e, g))
                    n = tm.at[("y1", e, g)]
                    dve.wait_ge(tm.emptied, n - NG + 1)
                    for j in range(GT):
                        i = g * GT + j
                        ins = nc.vector.scalar_tensor_tensor(
                            out=h[:, i, :], in0=src[:, j * P:(j + 1) * P], scalar=1.0 / SHARED,
                            in1=h[:, i, :], op0=ALU.mult, op1=ALU.add)
                    ins.then_inc(tm.emptied, 1)

            def step(s, k):
                n = s + LEAD
                if n < RT:
                    dve.wait_ge(rx_filled, n + 1 + k * XRING)
                    nc.vector.tensor_copy(xinT[:, n % 2, :], bank[n % 2][:, 0:P]).then_inc(rx_emptied, 1)
                n = s + 2
                if 0 <= n < RT:
                    dve.wait_ge(rh_filled, n + 1 + k * XRING)
                    nc.vector.tensor_copy(hpre[:, n % 2, :], bank[2 + n % 2]).then_inc(rh_emptied, 1)
                n = s
                if n >= 0:
                    a = n % NACC
                    e = dve.value_load(expert_of[0:1, bass.ds(n + k * XRING, 1)], min_val=0, max_val=E1 - 1)
                    dve.wait_ge(ry_filled, n + 1 + k * XRING)
                    if n >= NACC or not isinstance(k, int):
                        dve.wait_ge(summed[a], 16 * (n // NACC + k * (XRING // NACC)))
                    nc.vector.tensor_scalar(yout[:, a, :], bank[6 + n % 2][:, 0:P],
                                            xin[:, n % XRING, bass.ds(e + R_COMB, 1)], None,
                                            ALU.mult).then_inc(ry_emptied, 1)

            routed_steps(dve, step)
            total = h[:].rearrange("p i d -> p (i d)")
            for a in range(NACC):
                dve.wait_ge(ld_sum[a], 16)
                ins = nc.vector.tensor_tensor(total, total, sum_in[a], ALU.add)
                if a < NACC - 1:
                    link(ins)
                else:
                    ins.then_inc(total_ready, 1)

        @block.tensor
        def _(pe):
            def mm(out_, lhsT, rhs, start=True, stop=True):
                return nc.tensor.matmul(out_, lhsT, rhs, start=start, stop=stop)

            def transpose_group(key, g, first):
                pe.wait_ge(x_ready, first + g + 1)
                dst = tr.fill(pe, (key, g))
                for j in range(GT):
                    ins = nc.tensor.transpose(dst[:, j * P:(j + 1) * P], xn[:, g * GT + j, :], ident[:])
                ins.then_inc(tr.filled, 1)

            pe.wait_ge(ld_ssm, 96)
            A, AT = w_a[:, 0:NS], w_a[:, NS:2 * NS]
            dst = mq.fill(pe, ("woC",))
            mm(dst[0:NS, 0:P], w_c[:], w_oT[:]).then_inc(mq.filled, 1)
            dst = mq.fill(pe, ("woD",))
            mm(dst[:, 0:P], w_d[:], w_oT[:]).then_inc(mq.filled, 1)
            for i in I:
                mq.taken(pe, ("q", i - 1) if i else ("woC",))
                dst = mq.fill(pe, ("q", i))
                mm(dst[0:NS, 0:P], A, qT[:, i - 1, :] if i else woC[:]).then_inc(mq.filled, 1)
                if i < POW_LEVELS:
                    if i:
                        mq.taken(pe, ("pow", i - 1))
                    N, NT_ = (A, AT) if i == 0 else (powers[:, i, 0:NS], powers[:, i, NS:2 * NS])
                    dst = mq.fill(pe, ("pow", i))
                    mm(dst[0:NS, 0:NS], NT_, N)
                    mm(dst[0:NS, NS:2 * NS], N, NT_).then_inc(mq.filled, 1)
            pe.wait_ge(ld_const, 64)
            for g in G:
                transpose_group("xT_a", g, X_A)
            pe.wait_ge(ld_attn, 64)
            for g in G:
                tr.taken(pe, ("xT_a", g))
                x = xT[:, g * GC:(g + 1) * GC]
                mm(mq.fill(pe, ("l1", g)), w_attn[:, 0, :], x).then_inc(mq.filled, 1)
                mm(ma.fill(pe, ("l2", g)), w_attn[:, 1, :], x).then_inc(ma.filled, 1)
            mq.taken(pe, ("l1", NG - 1))
            for c in G:
                dst = mq.fill(pe, ("z", c))
                for k in range(K):
                    ins = mm(dst, w_dw[:, k, :], lpad[:, c * GC + k:c * GC + k + GC], k == 0, k == K - 1)
                ins.then_inc(mq.filled, 1)
                mq.taken(pe, ("z", c))
                mm(mq.fill(pe, ("lx", c)), w_attn[:, 2, :], zc[:, c % 2, :]).then_inc(mq.filled, 1)
                mq.taken(pe, ("lx", c))
                x = lx[:, c * GC:(c + 1) * GC]
                mm(ma.fill(pe, ("r", c)), w_attn[:, 4, :], x).then_inc(ma.filled, 1)
                mm(ma.fill(pe, ("i", c)), w_attn[:, 3, :], x).then_inc(ma.filled, 1)
            for g in G:
                pe.wait_ge(prod_ready, g + 1)
                dst = tm.fill(pe, ("pT", g))
                for j in range(GT):
                    i = g * GT + j
                    ins = nc.tensor.transpose(dst[:, j * P:(j + 1) * P], rg[:, i * P:(i + 1) * P], ident[:])
                ins.then_inc(tm.filled, 1)
            for g in G:
                transpose_group("xT_b", g, X_B)
            for g in range(NG + 1):
                if g < NG:
                    tr.taken(pe, ("xT_b", g))
                    for m in range(MULT):
                        mm(mq.fill(pe, ("wm1", g, m)), w_m1[:, m * P:(m + 1) * P],
                           xT[:, g * GC:(g + 1) * GC]).then_inc(mq.filled, 1)
                if g >= 1:
                    pe.wait_ge(hid_ready, MULT * g)
                    dst = tm.fill(pe, ("out0", g - 1))
                    for j in range(GT):
                        for m in range(MULT):
                            ins = mm(dst[:, j * P:(j + 1) * P], hidm[:, (g - 1) % 2, m, j * P:(j + 1) * P],
                                     w_m2[:, m, :], m == 0, m == MULT - 1)
                    ins.then_inc(tm.filled, 1)
            for g in G:
                transpose_group("xT_c", g, X_C)
            pe.wait_ge(ld_moe, 96)
            for g in G:
                tr.taken(pe, ("xT_c", g))
                dst = tm.fill(pe, ("logit0", g))
                for j in range(GT):
                    i = g * GT + j
                    ins = mm(dst[:, j * E0:(j + 1) * E0], xT[:, i * P:(i + 1) * P], w_g0[:])
                ins.then_inc(tm.filled, 1)

            def combine_transposed(key, n, ready):
                pe.wait_ge(ready, 1)
                for g in G:
                    dst = tr.fill(pe, (key, g))
                    for j in range(GT):
                        ins = nc.tensor.transpose(dst[0:n, j * P:(j + 1) * P], comb[:, g * GT + j, 0:n], ident[:])
                    ins.then_inc(tr.filled, 1)

            def weighted_rows(key, ckey, n, w):
                for g in G:
                    tr.taken(pe, (ckey, g))
                    dst = tm.fill(pe, (key, g))
                    for j in range(GT):
                        i = g * GT + j
                        ins = mm(dst[:, j * P:(j + 1) * P], combT[0:n, i * P:(i + 1) * P], w[:])
                    ins.then_inc(tm.filled, 1)

            def hidden0(g):
                for e in range(E0):
                    mm(ma.fill(pe, ("hid0", g, e)), w_e1[:, e, :],
                       xT[:, g * GC:(g + 1) * GC]).then_inc(ma.filled, 1)

            combine_transposed("combT0", E0, comb0_ready)
            weighted_rows("beta0", "combT0", E0, w_beta)
            hidden0(0)
            pe.wait_ge(centered, 1)
            for g in G:
                if g + 1 < NG:
                    hidden0(g + 1)
                ma.taken(pe, ("hid0", g, E0 - 1))
                for j in range(GT):
                    for half in range(2):
                        dst = tm.fill(pe, ("y0", g * GT + j, half))
                        for q in range(4):
                            e = 4 * half + q
                            ins = mm(dst[:, q * P:(q + 1) * P], hid0[:, g % 2, e, j * P:(j + 1) * P], w_e2[:, e, :])
                        ins.then_inc(tm.filled, 1)
            for g in G:
                transpose_group("xT_d", g, X_D)
            for g in G:
                tr.taken(pe, ("xT_d", g))
                dst = tm.fill(pe, ("hm", g))
                for j in range(GT):
                    i = g * GT + j
                    ins = mm(dst[:, j * P:(j + 1) * P], xT[:, i * P:(i + 1) * P], w_iT[:])
                ins.then_inc(tm.filled, 1)
            for g in G:
                transpose_group("uT", g, X_U)
            for i in I:
                if i % GT == 0:
                    tr.taken(pe, ("uT", i // GT))
                dst = mq.fill(pe, ("state", i))[0:NS, 0:P]
                ins = mm(dst, w_bT[:], xT[:, i * P:(i + 1) * P], True, i == 0)
                if i:
                    mq.taken(pe, ("state", i - 1))
                    ins = mm(dst, AT, st[:, i - 1, :], False, True)
                ins.then_inc(mq.filled, 1)
            pe.wait_ge(gate0_dve, 1)
            for k in range(SCAN_LEVELS):
                if k:
                    mq.taken(pe, ("carry", k - 1))
                w = P - 2 ** k
                mm(mq.fill(pe, ("carry", k))[0:NS, 0:w], powers[:, 4 + k, NS:2 * NS],
                   carry[:, 1:1 + w]).then_inc(mq.filled, 1)
            mq.taken(pe, ("carry", SCAN_LEVELS - 1))
            for g in G:
                dst = tm.fill(pe, ("y_ssm", g))
                for j in range(GT):
                    i = g * GT + j
                    d = dst[:, j * P:(j + 1) * P]
                    mm(d, xT[:, i * P:(i + 1) * P], woD[:], True, False)
                    mm(d, st[:, i, :], woC[:], False, False)
                    ins = mm(d, carry[:, 0:P], qT[:, i, :], False, True)
                ins.then_inc(tm.filled, 1)
            for g in G:
                transpose_group("xT_e", g, X_E)
            for g in G:
                tr.taken(pe, ("xT_e", g))
                dst = tm.fill(pe, ("logit1", g))
                for j in range(GT):
                    i = g * GT + j
                    ins = mm(dst[:, j * E1:(j + 1) * E1], xT[:, i * P:(i + 1) * P], w_g1[:])
                ins.then_inc(tm.filled, 1)
            combine_transposed("combT1", ES, comb1_ready)
            pe.wait_ge(chosen_ready, 1)
            pe.wait_ge(ld_shared, 96)
            dst = tm.fill(pe, ("rank",))
            mm(dst[:, 0:NT * E1], tri[:], chosen[:].rearrange("p i e -> p (i e)"), True, False)
            for d in range(1, NT):
                mm(dst[:, d * E1:NT * E1], ones[:], chosen[:, 0:NT - d, :].rearrange("p i e -> p (i e)"),
                   False, d == NT - 1)
            for i in I:
                ins = mm(dst[:, NT * E1:(NT + 1) * E1], ones[:], chosen[:, i, :], i == 0, i == NT - 1)
            ins.then_inc(tm.filled, 1)
            weighted_rows("b2", "combT1", ES, w_b2)

            def hidden1(e, g):
                for f in range(FC):
                    mm(ma.fill(pe, ("hid1", e, g, f)), w_sh1[:, e, f * P:(f + 1) * P],
                       xT[:, g * GC:(g + 1) * GC]).then_inc(ma.filled, 1)

            hidden1(0, 0)
            for e in range(SHARED):
                for g in G:
                    n = e * NG + g
                    if n + 1 < SHARED * NG:
                        hidden1((n + 1) // NG, (n + 1) % NG)
                    ma.taken(pe, ("hid1", e, g, FC - 1))
                    dst = tm.fill(pe, ("y1", e, g))
                    for j in range(GT):
                        for f in range(FC):
                            ins = mm(dst[:, j * P:(j + 1) * P], hid1[:, n % 2, f, j * P:(j + 1) * P],
                                     w_sh2[:, e, f * P:(f + 1) * P], f == 0, f == FC - 1)
                    ins.then_inc(tm.filled, 1)
            for q in (tr, ma, mq, tm):
                pe.wait_ge(q.emptied, len(q.at))
            pe.wait_ge(ld_w1, 16)
            pe.wait_ge(ld_w2, 16)
            pe.wait_ge(slot_ready, 1)

            def expert(n, k):
                return pe.value_load(expert_of[0:1, bass.ds(n + k * XRING, 1)], min_val=0, max_val=E1 - 1)

            def free(emptied, n, k):
                if n >= 2 or not isinstance(k, int):
                    pe.wait_ge(emptied, n - 1 + k * XRING)

            def step(s, k):
                n = s + LEAD
                if n < RT:
                    pe.wait_ge(ld_slot[n % XRING], 16 * (n // XRING + 1 + k))
                    free(rx_emptied, n, k)
                    nc.tensor.transpose(bank[n % 2][:, 0:P], xin[:, n % XRING, 0:P],
                                        ident[:]).then_inc(rx_filled, 1)
                n = s + 2
                if 0 <= n < RT:
                    e = expert(n, k)
                    pe.wait_ge(rx_emptied, n + 1 + k * XRING)
                    free(rh_emptied, n, k)
                    mm(bank[2 + n % 2], xinT[:, n % 2, :], w_e1_all[:, bass.ds(e * FH, FH)]).then_inc(rh_filled, 1)
                n = s + 1
                if 0 <= n < RT:
                    pe.wait_ge(rh_emptied, n + 1 + k * XRING)
                    free(rt_emptied, n, k)
                    for f in range(FC):
                        ins = nc.tensor.transpose(bank[4 + n % 2][:, f * P:(f + 1) * P],
                                                  hpre[:, n % 2, f * P:(f + 1) * P], ident[:])
                    ins.then_inc(rt_filled, 1)
                n = s
                if n >= 0:
                    e = expert(n, k)
                    pe.wait_ge(rt_emptied, n + 1 + k * XRING)
                    free(ry_emptied, n, k)
                    for f in range(FC):
                        ins = mm(bank[6 + n % 2][:, 0:P], hT[:, n % 2, f, :],
                                 w_e2_all[:, bass.ds(e * FH + f * P, P)], f == 0, f == FC - 1)
                    ins.then_inc(ry_filled, 1)

            routed_steps(pe, step)


def kernel(**inputs):
    import ml_dtypes
    import numpy as np
    import concourse.bacc as bacc
    from concourse.bass_utils import run_bass_kernel_spmd

    x = {k: np.asarray(v) for k, v in inputs.items()}
    c = np.ascontiguousarray
    consts = np.zeros((P, P + E1), np.float32)
    consts[:, :P] = np.eye(P)
    consts[:, P:] = np.arange(E1)
    vec = ["g", "b1", "b2", "dw_b", "pw_b", "bi", "br", "lam"]
    cols = [x[f"L0_attn_{v}"] for v in vec] + list(x["L0_attn_bm1"].reshape(MULT, P))
    cols += [x["L1_attn_gamma"], x["L1_attn_beta"]] + list(x["L0_ffn_b1"])
    rows = [x["L0_attn_bm2"], x["L1_attn_bi"], x["L1_attn_bo"], *x["L0_ffn_b2"], *x["L0_ffn_gamma"]]
    w1 = np.concatenate([x["L1_ffn_re_w1"], x["L1_ffn_se_w1"]])
    w2 = np.concatenate([x["L1_ffn_re_w2"], x["L1_ffn_se_w2"]])
    b1 = np.concatenate([x["L1_ffn_re_b1"], x["L1_ffn_se_b1"]])
    token_id = np.zeros((P, NT + 1), np.int32)
    token_id[:, :NT] = np.arange(T).reshape(P, NT)
    token_id[:, NT] = T + np.arange(P)
    ids = np.zeros((P, NT + 2), x["x"].dtype)
    ids[:, 1:NT + 1] = x["x"].reshape(P, NT)
    ids[1:, 0] = ids[:-1, NT]
    ids[:-1, NT + 1] = ids[1:, 1]
    arrays = {
        "ids": ids,
        "table": c(x["L0_tok_conv_w"].transpose(1, 2, 0).reshape(-1, TAPS0 * P)),
        "consts": consts,
        "cols": c(np.stack(cols, axis=1)),
        "rows": c(np.concatenate(rows)),
        "attn_w": c(np.stack([x["L0_attn_W1"], x["L0_attn_W2"], x["L0_attn_pw_w"][:, :, 0].T,
                              x["L0_attn_Wi"], x["L0_attn_Wr"]], axis=1)),
        "dw_w": c(x["L0_attn_dw_w"].transpose(1, 2, 0)),
        "wm1": x["L0_attn_Wm1"],
        "wm2": c(x["L0_attn_Wm2"].reshape(MULT, P, P).transpose(1, 0, 2)),
        "moe_wg": x["L0_ffn_Wg"],
        "moe_w1": c(x["L0_ffn_W1"].transpose(1, 0, 2)),
        "moe_w2": c(x["L0_ffn_W2"].transpose(1, 0, 2)),
        "moe_beta": x["L0_ffn_beta"],
        "ssm_a": c(np.concatenate([x["L1_attn_A"], x["L1_attn_A"].T], axis=1)),
        "ssm_bT": c(x["L1_attn_Bm"].T),
        "ssm_c": x["L1_attn_Cm"],
        "ssm_d": x["L1_attn_Dm"],
        "ssm_wiT": c(x["L1_attn_Wi"].T),
        "ssm_woT": c(x["L1_attn_Wo"].T),
        "gate_wT": c(x["L1_ffn_gate_w"].T),
        "ffn_w1": c(w1.transpose(1, 0, 2)),
        "ffn_w2": c(w2.reshape(ES, FC, P, P).transpose(2, 0, 1, 3).reshape(P, ES, FH)),
        "ffn_b1": c(b1.reshape(ES * FC, P).T),
        "ffn_b2": c(np.concatenate([x["L1_ffn_re_b2"], x["L1_ffn_se_b2"]])),
        "consts_bf": np.concatenate([np.triu(np.ones((P, P)), 1), np.ones((P, P))], axis=1).astype(ml_dtypes.bfloat16),
        "consts_i": token_id,
        "tile_ids": np.arange(RT, dtype=np.float32)[None],
    }
    nc = bacc.Bacc("TRN2", target_bir_lowering=False, num_devices=1)
    args = [nc.dram_tensor(f"in_{k}", a.shape, mybir.dt.from_np(a.dtype), kind="ExternalInput").ap()
            for k, a in arrays.items()]
    args.append(nc.dram_tensor("slots", (RT * P, RW), F32, kind="Internal").ap())
    args.append([nc.dram_tensor(f"sums{a}", (T + P, P), F32, kind="Internal").ap() for a in range(NACC)])
    args.append(nc.dram_tensor("out", (1, T, P), F32, kind="ExternalOutput").ap())
    lm_tower_kernel(nc, *args)
    r = run_bass_kernel_spmd(nc, [{f"in_{k}": a for k, a in arrays.items()}], core_ids=[0])
    return r.results[0]["out"]
```

```python
from contextlib import ExitStack

import concourse.bass as bass
from concourse import mybir

F32 = mybir.dt.float32
I32 = mybir.dt.int32
BF16 = mybir.dt.bfloat16
F16 = mybir.dt.float16
U32 = mybir.dt.uint32
ALU = mybir.AluOpType
ACT = mybir.ActivationFunctionType
AX = mybir.AxisListType

P = 128
T = 2048
NT = T // P
GT = 4
NG = NT // GT
GC = GT * P
TAPS0 = 3
K = 9
SSM_AT = (0, 1, 3)
HALO = K // 2
MULT = 4
E0 = 8
E1 = 16
TOP1 = 4
SHARED = 2
ES = E1 + SHARED
FC = 4
NS = 64
LN_EPS = 1e-5
RMS_EPS = 1e-6
SQD = float(P) ** 0.5
SCAN_LEVELS = 7
POW_LEVELS = 4 + SCAN_LEVELS - 1

COLS = ["g", "b1", "b2", "dw_b", "pw_b", "bi", "br", "lam", "bm1_0", "bm1_1", "bm1_2", "bm1_3",
        "gamma", "beta"] + [f"moe_b1_{e}" for e in range(E0)]
ROW_BM2, ROW_BI, ROW_BO, ROW_B2, ROW_GAMMA = 0, 1, 2, 3, 3 + E0
ROWS = 3 + 2 * E0
FH = FC * P

XRING = 9
BODY = 2 * XRING
NACC = 3
RT = T * TOP1 // P + E1 - 1
LEAD = 2
GLEAD = 8
R_COMB = P
RW = P + E1


class BankQueue:

    def __init__(self, nc, ctx, name, banks, keys):
        self.banks = banks
        self.at = {key: n for n, key in enumerate(keys)}
        assert len(self.at) == len(keys)
        self.filled = ctx.enter_context(nc.semaphore(f"{name}_filled"))
        self.emptied = ctx.enter_context(nc.semaphore(f"{name}_emptied"))
        self.issued = 0

    def fill(self, pe, key):
        n = self.at[key]
        assert n == self.issued, (key, n, self.issued)
        self.issued += 1
        if n >= 2:
            pe.wait_ge(self.emptied, n - 1)
        return self.banks[n % 2]

    def full(self, eng, key):
        n = self.at[key]
        eng.wait_ge(self.filled, n + 1)
        return self.banks[n % 2]

    def taken(self, eng, key):
        eng.wait_ge(self.emptied, self.at[key] + 1)


def lm_tower_kernel(nc, ids, table, consts, cols, rows, attn_w, dw_w, wm1, wm2, moe_wg, moe_w1, moe_w2,
                    moe_beta, ssm_a, ssm_bT, ssm_c, ssm_d, ssm_wiT, ssm_woT, gate_wT, ffn_w1, ffn_w2, ffn_b1, ffn_b2,
                    consts_bf, slot_consts, rows_dram, sums_dram, out):
    with ExitStack() as ctx:
        def sb(name, shape, dt=F32):
            return ctx.enter_context(nc.sbuf_tensor(f"sb_{name}", shape, dt))

        def sem(name):
            return ctx.enter_context(nc.semaphore(name))

        ident = sb("ident", [P, P])
        iota = sb("iota", [P, E1])
        col = sb("col", [P, len(COLS)])
        row = sb("row", [P, ROWS * P])
        w_attn = sb("w_attn", [P, 5, P])
        w_conv = sb("w_conv", [P, K, P])
        b_conv = sb("b_conv", [P, 1])
        w_m1 = sb("w_m1", [P, MULT * P])
        w_m2 = sb("w_m2", [P, MULT, P])
        w_g0 = sb("w_g0", [P, E0])
        w_e1 = sb("w_e1", [P, E0, P])
        w_e2 = sb("w_e2", [P, E0, P])
        w_beta = sb("w_beta", [E0, P])
        w_a = sb("w_a", [NS, 2 * NS])
        w_bT = sb("w_bT", [P, NS])
        w_c = sb("w_c", [P, NS])
        w_d = sb("w_d", [P, P])
        w_iT = sb("w_iT", [P, P])
        w_oT = sb("w_oT", [P, P])
        w_g1 = sb("w_g1", [P, E1])
        w_b2 = sb("w_b2", [ES, P])
        w_sh1 = w_e1[:].rearrange("p e d -> p (e d)").rearrange("p (e f) -> p e f", e=SHARED)
        w_sh2 = w_e2[:].rearrange("p e d -> p (e d)").rearrange("p (e f) -> p e f", e=SHARED)
        b1T = sb("b1T", [P, ES * FC])
        tri = sb("tri", [P, P], BF16)
        ones = sb("ones", [P, P], BF16)
        numbers = sb("numbers", [P, NT + 1 + P + RT])
        id1, spare1 = numbers[:, 0:NT], numbers[:, NT:NT + 1]
        pos_no, tile_no = numbers[:, NT + 1:NT + 1 + P], numbers[:, NT + 1 + P:]

        def column(name):
            n = COLS.index(name)
            return col[:, n:n + 1]

        def spread_row(at, n=1):
            return row[:, at * P:(at + n) * P]

        tok = sb("tok", [P, NT + 2], I32)
        work = sb("work", [P, 8192])
        gathered = work[:, 0:(NT + 2) * TAPS0 * P].rearrange("p (j c) -> p j c", c=TAPS0 * P)
        h = sb("h", [P, NT, P])
        skip = sb("skip", [P, NT, P])
        x_row = sb("x_row", [P, NT, RW])
        xn = x_row[:, :, 0:P]
        xT = sb("xT", [P, NT * P])
        lpad = sb("lpad", [P, T + 2 * HALO])
        early = sb("early", [P, 4, T])
        gl, lx, rg, ig = (early[:, n, :] for n in range(4))
        late = sb("late", [P, 2, T])
        ra, rb = (late[:, n, :] for n in range(2))
        w_dw = late[:, 0, 0:K * P].rearrange("p (k c) -> p k c", c=P)
        zc = sb("zc", [P, 2, GC])
        sq = sb("sq", [P, 2, GC])
        bn = sb("bn", [P, NT, 6])
        mv = sb("mv", [P, NT, 2])
        std = sb("std", [P, NT])
        rstd = sb("rstd", [P, NT])
        nrm = sb("nrm", [P, NT])
        qs = sb("qs", [P, NT])
        lamv = sb("lamv", [P, 12])
        lg0 = sb("lg0", [P, NT, E0])
        top = sb("top", [P, NT, 8])
        topi = sb("topi", [P, NT, 8], U32)
        topf = sb("topf", [P, NT, 8])
        hot = sb("hot", [P, NT, E1])
        comb = sb("comb", [P, NT, ES])
        combT = sb("combT", [ES, NT * P])
        lg1 = sb("lg1", [P, NT, E1])
        sm = sb("sm", [P, 4, NT])
        ss = sb("ss", [P, NT, E0])
        sc = sb("sc", [P, NT, E0])
        wmean = sb("wmean", [P, 2 * E0])
        area_pow = sb("area_pow", [P, (POW_LEVELS + 1) * 2 * NS])
        area_q = sb("area_q", [P, NT * P])
        area_st = sb("area_st", [P, NT * P])
        powers = area_pow[0:NS, :].rearrange("s (k c) -> s k c", c=2 * NS)
        woC = sb("woC", [NS, P])
        woD = sb("woD", [P, P])
        qT = area_q[0:NS, :].rearrange("s (i c) -> s i c", c=P)
        st = area_st[0:NS, :].rearrange("s (i c) -> s i c", c=P)
        carry = sb("carry", [NS, P + 1])
        blank = sb("blank", [P, RW])
        choice = area_st[:, 0:TOP1 * NT * E1].rearrange("p (k i e) -> p k i e", k=TOP1, i=NT)
        chosen = sb("chosen", [P, NT, E1], BF16)
        rank = area_st[:, TOP1 * NT * E1:(TOP1 + 1) * NT * E1].rearrange("p (i e) -> p i e", i=NT)
        cnt = sb("cnt", [P, 6, E1])
        cnt_i = sb("cnt_i", [P, E1], I32)
        slot_f = sb("slot_f", [P, TOP1, NT])
        slot = sb("slot", [P, TOP1, NT], I32)
        past = area_pow[0:1, 0:RT * E1].rearrange("p (t e) -> p t e", e=E1)
        expert_f = sb("expert_f", [1, RT])
        expert_of = sb("expert_of", [1, RT], I32)
        spos = sb("spos", [P, TOP1, NT])
        stile = sb("stile", [P, TOP1, NT])
        slot_bits = sb("slot_bits", [P, TOP1, NT], I32)
        pos_hot = skip[:].rearrange("p i c -> p (i c)").bitcast(F16)[:, 0:4 * TOP1 * P].rearrange(
            "p (n k c) -> p n k c", n=4, k=TOP1)
        tile_hot = lpad[:].bitcast(F16)[:, 0:4 * TOP1 * RT].rearrange("p (n k c) -> p n k c", n=4, k=TOP1)
        list_f = sb("list_f", [P, RT])
        unused = sb("unused", [P, RT])
        slot_list = sb("slot_list", [P, RT], I32)
        ids_in = sb("ids_in", [P, BODY], I32)
        xin = area_q[:, 0:XRING * RW].rearrange("p (n c) -> p n c", c=RW)
        xinT = area_q[:, XRING * RW:XRING * RW + 2 * P].rearrange("p (n c) -> p n c", c=P)
        yout = area_q[:, XRING * RW + 2 * P:XRING * RW + (2 + NACC) * P].rearrange("p (n c) -> p n c", c=P)
        w1_in = zc
        hT = sq[:].rearrange("p n (f c) -> p n f c", c=P)

        pst = ctx.enter_context(nc.psum_tensor("pst", [P, 8, GC], F32))
        bank = [pst[:, b, :] for b in range(8)]

        G, I = range(NG), range(NT)
        tr = BankQueue(nc, ctx, "transposed", bank[0:2],
                       [("xT_a", g) for g in G] + [("xT_b", g) for g in G] + [("xT_c", g) for g in G]
                       + [("combT0", g) for g in G] + [("xT_d", g) for g in G] + [("uT", g) for g in G]
                       + [("xT_e", g) for g in G] + [("list",)] + [("combT1", g) for g in G])
        ma = BankQueue(nc, ctx, "for_act", bank[2:4],
                       [("l2", g) for g in G] + [(w, c) for c in G for w in ("r", "i")]
                       + [("hid0", g, e) for g in G for e in range(E0)]
                       + [("hid1", g, e, f) for g in G for e in range(SHARED) for f in range(FC)])
        def ssm_keys(lo, hi):
            keys = []
            for i in range(lo, hi):
                keys += [("q", i)] + ([("pow", i)] if i < POW_LEVELS else [])
            return keys

        mv_keys = [("l1", g) for g in G] + [("taps", n) for n in range(3)] + [("lx", c) for c in G]
        mv_keys += [("wm1", g, m) for g in G for m in range(MULT)]
        mv_keys += [("state", i) for i in I] + [("carry", k) for k in range(SCAN_LEVELS)]
        mq = BankQueue(nc, ctx, "for_dve", bank[4:6], mv_keys)
        tm_keys = [("woC",), ("woD",)] + ssm_keys(0, NT)
        tm_keys += [("pT", g) for g in G] + [("out0", g) for g in G] + [("logit0", g) for g in G]
        tm_keys += [("y0", i, half) for i in range(2) for half in range(2)] + [("beta0", g) for g in G]
        tm_keys += [("y0", i, half) for i in range(2, NT) for half in range(2)]
        tm_keys += [("hm", g) for g in G] + [("y_ssm", g) for g in G] + [("logit1", g) for g in G]
        tm_keys += [("y1", 0), ("rank",), ("y1", 1), ("y1", 2), ("y1", 3)]
        tm_keys += [("b2", g) for g in G]
        tm = BankQueue(nc, ctx, "token_major", bank[6:8], tm_keys)

        ld_const = sem("ld_const")
        ld_ids = sem("ld_ids")
        ld_ssm = sem("ld_ssm")
        ld_attn = sem("ld_attn")
        ld_ff = sem("ld_ff")
        ld_moe = sem("ld_moe")
        ld_rows = sem("ld_rows")
        ld_shared = sem("ld_shared")
        ld_w1 = sem("ld_w1")
        ld_w2 = sem("ld_w2")
        gathered_in = [sem(f"gathered_in{n}") for n in range(XRING)]
        blank_ready = sem("blank_ready")
        blank_stored = sem("blank_stored")
        rows_ready = sem("rows_ready")
        rows_stored = sem("rows_stored")
        pos_ready = sem("pos_ready")
        pos_hot_ready = sem("pos_hot_ready")
        tile_hot_ready = sem("tile_hot_ready")
        list_done = sem("list_done")
        ids_ready = sem("ids_ready")
        chosen_ready = sem("chosen_ready")
        slot_ready = sem("slot_ready")
        rx_filled, rx_emptied = sem("rx_filled"), sem("rx_emptied")
        rt_filled, rt_emptied = sem("rt_filled"), sem("rt_emptied")
        ry_filled, ry_emptied = sem("ry_filled"), sem("ry_emptied")
        summed = [sem(f"summed{a}") for a in range(NACC)]
        ld_sum = [[sem(f"ld_sum{a}_{n}") for n in range(2)] for a in range(NACC)]
        dma_started = sem("dma_started")
        hid1_used = sem("hid1_used")
        total_ready = sem("total_ready")
        emb = [sem(f"emb{g}") for g in G]
        exp0_act = sem("exp0_act")
        dve_step = sem("dve_step")
        pool_step = sem("pool_step")
        var_ready = sem("var_ready")
        std_ready = sem("std_ready")
        x_ready = sem("x_ready")
        lam_dve = sem("lam_dve")
        lam_act = sem("lam_act")
        decay_ready = sem("decay_ready")
        prod_ready = sem("prod_ready")
        x1_ready = sem("x1_ready")
        ssq_ready = sem("ssq_ready")
        base_ready = sem("base_ready")
        gelu_ready = sem("gelu_ready")
        centered = sem("centered")
        exp0_ready = sem("exp0_ready")
        carry_ready = sem("carry_ready")
        comb0_ready = sem("comb0_ready")
        sq0_ready = sem("sq0_ready")
        sd0_ready = sem("sd0_ready")
        v0_ready = sem("v0_ready")
        moe_ready = sem("moe_ready")
        h2_base = sem("h2_base")
        exp1_dve = sem("exp1_dve")
        exp1_act = sem("exp1_act")
        comb1_ready = sem("comb1_ready")
        out_done = sem("out_done")

        X_A, X_B, X_C, X_D, X_U, X_E = (NG * n for n in range(6))
        V_A, V_C, V_D, V_U, V_E = (NG * n for n in range(5))

        hid0 = work[:, 0:2 * E0 * GC].rearrange("p (s e c) -> p s e c", s=2, e=E0)
        hidm = work[:, 0:2 * MULT * GC].rearrange("p (s e c) -> p s e c", s=2, e=MULT)
        hid1 = late[:].rearrange("p s (e c) -> p s e c", e=FC)
        YR = 8

        def y_of(n):
            return early[:, 0:2, :].rearrange("p a (n c) -> p (a n) c", c=GC)[:, n % YR, :]

        def z_of(n):
            return early[:, 2:4, :].rearrange("p a (n c) -> p (a n) c", c=GC)[:, n % YR, :]

        w_e1_all = early[:].rearrange("p a c -> p (a c)")
        w_e2_all = work
        sum_in = [skip[:].rearrange("p i d -> p (i d)"), xT[:], lpad[:, 0:T]]
        sums_order = [n % NACC for n in range(RT - NACC, RT)]
        halves = [slice(0, T // 2), slice(T // 2, T)]

        def routed_steps(eng, step, lead=LEAD):
            full = (RT - GLEAD - 1) // BODY
            for u in range(-lead, BODY):
                step(u, 0)
            with eng.Fori(1, full) as body:
                k = body * (BODY // XRING)
                for u in range(BODY):
                    step(u, k)
            for u in range(BODY * full, RT):
                step(u, 0)

        block = ctx.enter_context(nc.Block())

        @block.sync
        def _(sp):
            sp.dma_start(tok[:], ids).then_inc(ld_ids, 16)
            for dst, src in ((w_a, ssm_a), (w_c, ssm_c), (w_d, ssm_d), (w_oT, ssm_woT), (w_bT, ssm_bT),
                             (w_iT, ssm_wiT)):
                sp.dma_start(dst[:], src).then_inc(ld_ssm, 16)
            sp.dma_start(ident[:], consts[:, 0:P]).then_inc(ld_const, 16)
            sp.dma_start(iota[:], consts[:, P:P + E1]).then_inc(ld_const, 16)
            sp.dma_start(col[:], cols).then_inc(ld_const, 16)
            sp.dma_start(numbers[:], slot_consts).then_inc(ld_const, 16)
            sp.dma_start(w_attn[:], attn_w).then_inc(ld_attn, 16)
            sp.dma_start(w_dw, dw_w).then_inc(ld_attn, 16)
            sp.wait_ge(emb[NG - 1], 16 * GT)
            sp.dma_start(w_m1[:], wm1).then_inc(ld_ff, 16)
            sp.dma_start(w_m2[:], wm2).then_inc(ld_ff, 16)
            sp.dma_start(row[:], rows.partition_broadcast(P)).then_inc(ld_rows, 16)
            for dst, src in ((w_g0, moe_wg), (w_e1, moe_w1), (w_e2, moe_w2), (w_beta, moe_beta),
                             (w_g1, gate_wT), (w_b2, ffn_b2)):
                sp.dma_start(dst[:], src).then_inc(ld_moe, 16)
            for dst, src in ((b1T, ffn_b1), (tri, consts_bf[:, 0:P]), (ones, consts_bf[:, P:2 * P])):
                sp.dma_start(dst[:], src).then_inc(ld_shared, 16)
            sp.wait_ge(blank_ready, 1)
            sp.wait_ge(x_ready, NG)
            sp.dma_start(rows_dram[T:T + P, :], blank[:]).then_inc(blank_stored, 16)
            for a in range(NACC):
                sp.dma_start(sums_dram[a].rearrange("(n p) c -> p n c", p=P),
                             blank[:, 0:P].unsqueeze(1).to_broadcast([P, NT + 1, P])).then_inc(blank_stored, 16)
            sp.wait_ge(tm.filled, tm.at[("y0", NT - 1, 1)] + 1)
            sp.dma_start(w_sh1[:], ffn_w1[:, E1:ES, :]).then_inc(ld_shared, 16)
            sp.dma_start(w_sh2[:], ffn_w2[:, E1:ES, :]).then_inc(ld_shared, 16)
            sp.dma_start(w_e2_all[:], ffn_w2[:, 0:E1, :].rearrange("p e f -> p (e f)")).then_inc(ld_w2, 16)
            sp.wait_ge(moe_ready, NT)
            sp.dma_start(w_e1_all, ffn_w1[:, 0:E1, :].rearrange("p e f -> p (e f)")).then_inc(ld_w1, 16)
            sp.wait_ge(rows_ready, 1)
            sp.dma_start(rows_dram[0:T, :].rearrange("(p i) c -> p (i c)", i=NT),
                         x_row[:].rearrange("p i c -> p (i c)")).then_inc(rows_stored, 16)
            for a in sums_order:
                sp.wait_ge(summed[a], 16 * len(range(a, RT, NACC)))
                for n, half in enumerate(halves):
                    sp.dma_start(sum_in[a][:, half],
                                 sums_dram[a][0:T, :].rearrange("(p i) d -> p (i d)", i=NT)[:, half]
                                 ).then_inc(ld_sum[a][n], 16)
            for n, half in enumerate(halves):
                sp.wait_ge(total_ready, n + 1)
                sp.dma_start(out[0].rearrange("(p i) d -> p (i d)", i=NT)[:, half],
                             h[:].rearrange("p i d -> p (i d)")[:, half]).then_inc(out_done, 16)
            sp.wait_ge(out_done, 32)

        @block.gpsimd
        def _(pool):
            steps = [0]

            def link(ins):
                steps[0] += 1
                ins.then_inc(pool_step, 1)
                pool.wait_ge(pool_step, steps[0])

            nc.gpsimd.memset(blank[:], 0.0).then_inc(blank_ready, 1)
            link(nc.gpsimd.memset(gathered[:, NT + 1, :], 0.0))
            pool.wait_ge(ld_ids, 16)
            for j in range(NT + 2):
                n = P - 1 if j == NT + 1 else P
                g = max(0, min((j - 2) // GT, NG - 1))
                pool.indirect_dma_start(
                    out=gathered[0:n, j, :], out_offset=None, in_=table,
                    in_offset=bass.IndirectOffsetOnAxis(ap=tok[0:n, j:j + 1], axis=0)).then_inc(emb[g], 16)
            pool.wait_ge(ld_rows, 16)
            for g in G:
                s = slice(g * GT, (g + 1) * GT)
                pool.wait_ge(x1_ready, g + 1)
                link(nc.gpsimd.tensor_tensor(h[:, s, :], h[:, s, :], skip[:, s, :], ALU.add))
                nc.gpsimd.tensor_tensor(
                    h[:, s, :], h[:, s, :],
                    spread_row(ROW_BM2).unsqueeze(1).to_broadcast([P, GT, P]), ALU.add).then_inc(base_ready, 1)
            for n in range(2 * NT):
                tm.taken(pool, ("y0", n // 2, n % 2))
                if n >= YR:
                    pool.wait_ge(moe_ready, (n - YR) // 2 + 1)
                nc.gpsimd.tensor_tensor(z_of(n), y_of(n), spread_row(ROW_GAMMA + 4 * (n % 2), 4),
                                        ALU.mult).then_inc(v0_ready, 1)
            for g in G:
                s = slice(g * GT, (g + 1) * GT)
                pool.wait_ge(x_ready, X_D + g + 1)
                nc.gpsimd.tensor_tensor(
                    h[:, s, :], h[:, s, :],
                    spread_row(ROW_BO).unsqueeze(1).to_broadcast([P, GT, P]), ALU.add).then_inc(h2_base, 1)
            pool.wait_ge(pos_ready, 1)
            for i in I:
                if i >= 4:
                    pool.wait_ge(list_done, i - 3)
                for k in range(TOP1 // 2):
                    ins = nc.gpsimd.tensor_scalar(tile_hot[:, i % 4, k, :], tile_no, stile[:, k, i:i + 1],
                                                  id1[:, i:i + 1], ALU.is_equal, ALU.mult)
                ins.then_inc(tile_hot_ready, 1)
            pool.wait_ge(rows_stored, 16)
            pool.wait_ge(blank_stored, 16 * (1 + NACC))

            def gather_rows(n, k):
                pool.wait_ge(ids_ready, n + 1 + k * XRING)
                if n >= XRING or not isinstance(k, int):
                    pool.wait_ge(ry_emptied, n + 1 - XRING + k * XRING)
                pool.sem_inc(dma_started, 1)
                pool.indirect_dma_start(
                    out=xin[:, n % XRING, :], out_offset=None, in_=rows_dram,
                    in_offset=bass.IndirectOffsetOnAxis(ap=ids_in[:, n % BODY:n % BODY + 1], axis=0)
                    ).then_inc(gathered_in[n % XRING], 16)

            def add_rows(n, k):
                a = n % NACC
                pool.wait_ge(ry_emptied, n + 1 + k * XRING)
                if n >= NACC or not isinstance(k, int):
                    pool.wait_ge(summed[a], 16 * (n // NACC + k * (XRING // NACC)))
                pool.sem_inc(dma_started, 1)
                pool.indirect_dma_start(
                    out=sums_dram[a],
                    out_offset=bass.IndirectOffsetOnAxis(ap=ids_in[:, n % BODY:n % BODY + 1], axis=0),
                    in_=yout[:, a, :], in_offset=None, compute_op=ALU.add).then_inc(summed[a], 16)

            def step(s, k):
                if s + GLEAD < RT and s + GLEAD >= 0:
                    gather_rows(s + GLEAD, k)
                if s >= 0:
                    add_rows(s, k)

            routed_steps(pool, step, GLEAD)

        @block.scalar
        def _(act):
            def root(first, g):
                s = slice(g * GT, (g + 1) * GT)
                act.wait_ge(var_ready, first + g + 1)
                if first == V_A:
                    nc.scalar.activation(nrm[:, s], mv[:, s, 1], ACT.Sqrt, scale=float(P))
                nc.scalar.activation(std[:, s], mv[:, s, 1], ACT.Sqrt, bias=eps_ln).then_inc(std_ready, 1)

            def take_xT(key, g, scale=None, bias=None):
                src = tr.full(act, (key, g))
                dst = xT[:, g * GC:(g + 1) * GC]
                if scale is None:
                    nc.scalar.copy(dst, src).then_inc(tr.emptied, 1)
                elif bias is None:
                    nc.scalar.activation(dst, src, ACT.Copy, scale=scale).then_inc(tr.emptied, 1)
                else:
                    nc.scalar.activation(dst, src, ACT.Identity, scale=scale, bias=bias).then_inc(tr.emptied, 1)

            eps_ln = LN_EPS
            act.wait_ge(ld_const, 64)
            act.wait_ge(lam_dve, 1)
            nc.scalar.activation(lamv[:, 1:2], lamv[:, 0:1], ACT.Exp).then_inc(lam_act, 1)
            act.wait_ge(lam_dve, 2)
            nc.scalar.activation(lamv[:, 3:4], lamv[:, 2:3], ACT.Ln).then_inc(lam_act, 1)
            for g in G:
                root(V_A, g)
            for g in G:
                take_xT("xT_a", g, scale=column("g"))
            for g in G:
                src = ma.full(act, ("l2", g))
                nc.scalar.activation(gl[:, g * GC:(g + 1) * GC], src, ACT.Gelu,
                                     bias=column("b2")).then_inc(ma.emptied, 1)
            act.wait_ge(lam_dve, 4)
            for c in G:
                s = slice(c * GC, (c + 1) * GC)
                for key, dst, b in (("r", rg, "br"), ("i", ig, "bi")):
                    src = ma.full(act, (key, c))
                    nc.scalar.activation(dst[:, s], src, ACT.Sigmoid, bias=column(b)).then_inc(ma.emptied, 1)
                ma.taken(act, ("r", c))
                nc.scalar.activation(ra[:, s], rg[:, s], ACT.Exp, scale=lamv[:, 8:9]).then_inc(decay_ready, 1)
                nc.scalar.activation(rb[:, s], rg[:, s], ACT.Exp, scale=lamv[:, 9:10]).then_inc(decay_ready, 1)
                act.wait_ge(decay_ready, 3 * c + 2)
                nc.scalar.activation(rb[:, s], rb[:, s], ACT.Sqrt, scale=-1.0, bias=1.0).then_inc(decay_ready, 1)
            for g in G:
                act.wait_ge(x1_ready, g + 1)
                for i in range(g * GT, (g + 1) * GT):
                    last = nc.scalar.activation(sq[:, 0, (i % GT) * P:(i % GT + 1) * P], skip[:, i, :],
                                                ACT.Square, accum_out=nrm[:, i:i + 1])
                last.then_inc(ssq_ready, 1)
                act.wait_ge(ssq_ready, 2 * g + 1)
                s = slice(g * GT, (g + 1) * GT)
                nc.scalar.activation(std[:, s], nrm[:, s], ACT.Sqrt).then_inc(ssq_ready, 1)
            for g in G:
                take_xT("xT_b", g, scale=column("g"))
            for g in G:
                for m in range(MULT):
                    n = g * MULT + m
                    src = mq.full(act, ("wm1", g, m))
                    if n >= 2:
                        act.wait_ge(mq.emptied, mq.at[("wm1", g, m)] - 1)
                    nc.scalar.activation(zc[:, n % 2, :], src, ACT.Gelu,
                                         bias=column(f"bm1_{m}")).then_inc(gelu_ready, 1)
            for g in G:
                root(V_C, g)
            for g in G:
                take_xT("xT_c", g)
            def hidden0(g, e):
                if g >= 2 and e == 0:
                    act.wait_ge(tm.filled, tm.at[("y0", (g - 1) * GT - 1, 1)] + 1)
                src = ma.full(act, ("hid0", g, e))
                nc.scalar.activation(hid0[:, g % 2, e, :], src, ACT.Relu,
                                     bias=column(f"moe_b1_{e}")).then_inc(ma.emptied, 1)

            def squares(i):
                for half in range(2):
                    tm.taken(act, ("y0", i, half))
                    y = y_of(2 * i + half)
                    for q in range(4):
                        e = 4 * half + q
                        ins = nc.scalar.activation(sq[:, half, q * P:(q + 1) * P], y[:, q * P:(q + 1) * P],
                                                   ACT.Square, accum_out=ss[:, i, e:e + 1])
                ins.then_inc(sq0_ready, 1)
                act.wait_ge(sq0_ready, i + 1)
                nc.scalar.activation(ss[:, i, :], ss[:, i, :], ACT.Sqrt, scale=1.0 / P,
                                     bias=eps_ln).then_inc(sd0_ready, 1)

            for e in range(E0 // 4):
                hidden0(0, e)
            act.wait_ge(exp0_ready, 1)
            nc.scalar.activation(sm[:, 1, :], sm[:, 0, :], ACT.Exp).then_inc(exp0_act, 1)
            for e in range(E0 // 4, E0):
                hidden0(0, e)
            for i in I:
                g, j = i // GT, i % GT
                if i == 1:
                    for c in G:
                        src = tr.full(act, ("combT0", c))
                        nc.scalar.copy(combT[0:E0, c * GC:(c + 1) * GC], src[0:E0, :]).then_inc(tr.emptied, 1)
                squares(i)
                if g + 1 < NG:
                    hidden0(g + 1, 2 * j)
                    hidden0(g + 1, 2 * j + 1)
                if i > GT and j == 1:
                    root(V_D, g - 1)
            for g in range(NG - 1):
                take_xT("xT_d", g)
            root(V_D, NG - 1)
            root(V_U, 0)
            take_xT("xT_d", NG - 1)
            for g in range(1, NG):
                root(V_U, g)
                if g == NG - 2:
                    take_xT("uT", 0, scale=column("gamma"), bias=column("beta"))
            for g in range(1, NG + 1):
                if g < NG:
                    take_xT("uT", g, scale=column("gamma"), bias=column("beta"))
                for i in range((g - 1) * GT, g * GT):
                    src = mq.full(act, ("state", i))
                    nc.scalar.copy(st[:, i, :], src[0:NS, 0:P]).then_inc(mq.emptied, 1)
            for g in range(NG + 1):
                if g < NG:
                    root(V_E, g)
                if g >= 1:
                    take_xT("xT_e", g - 1)

            def hidden1(g, e):
                n = g * SHARED + e
                if g and e < SHARED - 1:
                    act.wait_ge(hid1_used, g)
                elif g:
                    act.wait_ge(tm.filled, tm.at[("y1", g - 1)] + 1)
                for f in range(FC):
                    b = (E1 + e) * FC + f
                    src = ma.full(act, ("hid1", g, e, f))
                    nc.scalar.activation(hid1[:, n % 2, f, :], src, ACT.Gelu,
                                         bias=b1T[:, b:b + 1]).then_inc(ma.emptied, 1)

            act.wait_ge(ld_shared, 80)
            act.wait_ge(exp1_dve, 1)
            nc.scalar.activation(lg1[:], lg1[:], ACT.Exp).then_inc(exp1_act, 1)
            hidden1(0, 0)
            act.wait_ge(exp1_dve, 2)
            nc.scalar.activation(top[:, :, 0:TOP1], top[:, :, 0:TOP1], ACT.Exp).then_inc(exp1_act, 1)
            hidden1(0, 1)
            for g in range(1, NG):
                for e in range(SHARED):
                    hidden1(g, e)
            src = tr.full(act, ("list",))
            nc.scalar.copy(list_f[:], src[:, 0:RT]).then_inc(tr.emptied, 1)
            for g in G:
                src = tr.full(act, ("combT1", g))
                nc.scalar.copy(combT[:, g * GC:(g + 1) * GC], src[0:ES, :]).then_inc(tr.emptied, 1)

            act.wait_ge(slot_ready, 1)

            def step(s, k):
                n = s + 1
                if n < 0 or n >= RT:
                    return
                at = k * XRING + n
                act.wait_ge(rt_filled, at + 1)
                e = act.value_load(expert_of[0:1, bass.ds(at, 1)], min_val=0, max_val=E1 - 1)
                for f in range(FC):
                    ins = nc.scalar.activation(hT[:, n % 2, f, :], bank[4 + n % 2][:, f * P:(f + 1) * P],
                                               ACT.Gelu, bias=b1T[:, bass.ds(e * FC + f, 1)])
                ins.then_inc(rt_emptied, 1)

            routed_steps(act, step)

        @block.vector
        def _(dve):
            steps = [0]

            def mark(ins):
                steps[0] += 1
                ins.then_inc(dve_step, 1)

            def settle():
                dve.wait_ge(dve_step, steps[0])

            def link(ins):
                mark(ins)
                settle()

            def stats(src, g):
                for i in range(g * GT, (g + 1) * GT):
                    ins = nc.vector.bn_stats(bn[:, i, :], src[:, i, :])
                link(ins)
                for i in range(g * GT, (g + 1) * GT):
                    ins = nc.vector.bn_aggr(mv[:, i, :], bn[:, i, :])
                ins.then_inc(var_ready, 1)

            def normalise(src, dst, first, g, scale=None, signal=True):
                s = slice(g * GT, (g + 1) * GT)
                if scale is None:
                    dve.wait_ge(std_ready, first + g + 1)
                    link(nc.vector.reciprocal(rstd[:, s], std[:, s]))
                    scale = rstd
                for i in range(g * GT, (g + 1) * GT):
                    ins = nc.vector.tensor_scalar(dst[:, i, :], src[:, i, :], mv[:, i, 0:1],
                                                  scale[:, i:i + 1], ALU.subtract, ALU.mult)
                if signal:
                    ins.then_inc(x_ready, 1)
                else:
                    mark(ins)

            def copy_out(queue, key, dst, rows=P, width=GC):
                src = queue.full(dve, key)
                nc.vector.tensor_copy(dst, src[0:rows, 0:width]).then_inc(queue.emptied, 1)

            dve.wait_ge(ld_const, 64)
            mark(nc.vector.memset(lpad[:, 0:HALO], 0.0))
            mark(nc.vector.memset(lpad[:, HALO + T:], 0.0))
            mark(nc.vector.memset(carry[:, 0:1], 0.0))
            link(nc.vector.memset(comb[:, :, E1:ES], 1.0 / SHARED))
            dve.wait_ge(ld_const, 64)
            lam = column("lam")
            link(nc.vector.tensor_scalar(lamv[:, 10:11], lam, -1.0, None, ALU.mult))
            link(nc.vector.tensor_tensor(lamv[:, 11:12], lam, lamv[:, 10:11], ALU.max))
            nc.vector.tensor_scalar(lamv[:, 0:1], lamv[:, 11:12], -1.0, None, ALU.mult).then_inc(lam_dve, 1)
            dve.wait_ge(lam_act, 1)
            nc.vector.tensor_scalar(lamv[:, 2:3], lamv[:, 1:2], 1.0, None, ALU.add).then_inc(lam_dve, 1)
            dve.wait_ge(lam_dve, 2)
            link(nc.vector.tensor_scalar(lamv[:, 4:5], lamv[:, 2:3], -1.0, None, ALU.add))
            link(nc.vector.tensor_scalar(lamv[:, 5:6], lamv[:, 4:5], 1e-30, None, ALU.max))
            link(nc.vector.reciprocal(lamv[:, 5:6], lamv[:, 5:6]))
            dve.wait_ge(lam_act, 2)
            link(nc.vector.tensor_tensor(lamv[:, 6:7], lamv[:, 3:4], lamv[:, 5:6], ALU.mult))
            link(nc.vector.scalar_tensor_tensor(out=lamv[:, 6:7], in0=lamv[:, 4:5], scalar=0.0,
                                                in1=lamv[:, 6:7], op0=ALU.is_equal, op1=ALU.add))
            link(nc.vector.tensor_tensor(lamv[:, 6:7], lamv[:, 6:7], lamv[:, 1:2], ALU.mult))
            link(nc.vector.scalar_tensor_tensor(out=lamv[:, 7:8], in0=lam, scalar=0.0,
                                                in1=lamv[:, 6:7], op0=ALU.max, op1=ALU.add))
            nc.vector.tensor_scalar(lamv[:, 8:9], lamv[:, 7:8], -8.0, None, ALU.mult).then_inc(lam_dve, 1)
            nc.vector.tensor_scalar(lamv[:, 9:10], lamv[:, 7:8], -16.0, None, ALU.mult).then_inc(lam_dve, 1)
            def ssm_copies(lo, hi):
                for i in range(lo, hi):
                    copy_out(tm, ("q", i), qT[:, i, :], NS, P)
                    if i < POW_LEVELS:
                        copy_out(tm, ("pow", i), powers[:, i + 1, :], NS, 2 * NS)

            def embed(g):
                s = slice(g * GT, (g + 1) * GT)
                dve.wait_ge(emb[g], 16 * ((GT + 2) if g == 0 else GT))
                if g == 0:
                    link(nc.vector.memset(gathered[0:1, 0, :], 0.0))
                link(nc.vector.tensor_tensor(h[:, s, :], gathered[:, g * GT:(g + 1) * GT, 0:P],
                                             gathered[:, g * GT + 1:(g + 1) * GT + 1, P:2 * P], ALU.add))
                link(nc.vector.tensor_tensor(h[:, s, :], h[:, s, :],
                                             gathered[:, g * GT + 2:(g + 1) * GT + 2, 2 * P:3 * P], ALU.add))
                stats(h, g)

            def norms_a(g):
                s = slice(g * GT, (g + 1) * GT)
                dve.wait_ge(std_ready, V_A + g + 1)
                link(nc.vector.reciprocal(rstd[:, s], std[:, s]))
                link(nc.vector.tensor_tensor(qs[:, s], nrm[:, s], rstd[:, s], ALU.mult))
                link(nc.vector.tensor_scalar(qs[:, s], qs[:, s], RMS_EPS, None, ALU.add))
                link(nc.vector.reciprocal(qs[:, s], qs[:, s]))
                link(nc.vector.scalar_tensor_tensor(out=qs[:, s], in0=qs[:, s], scalar=SQD, in1=rstd[:, s],
                                                    op0=ALU.mult, op1=ALU.mult))
                normalise(h, xn, V_A, g, scale=qs)

            embed(0)
            embed(1)
            norms_a(0)
            embed(2)
            norms_a(1)
            embed(3)
            norms_a(2)
            norms_a(3)
            def centre_experts():
                dve.wait_ge(ld_moe, 96)
                link(nc.vector.tensor_reduce(wmean[:, 0:E0], w_e2[:], AX.X, ALU.add))
                link(nc.vector.tensor_reduce(wmean[:, E0:], spread_row(ROW_B2, E0).rearrange("p (e d) -> p e d", e=E0),
                                             AX.X, ALU.add))
                link(nc.vector.tensor_scalar(wmean[:], wmean[:], 1.0 / P, None, ALU.mult))
                for e in range(E0):
                    mark(nc.vector.tensor_scalar(w_e2[:, e, :], w_e2[:, e, :], wmean[:, e:e + 1], None, ALU.subtract))
                    b = spread_row(ROW_B2 + e)
                    ins = nc.vector.tensor_scalar(b, b, wmean[:, E0 + e:E0 + e + 1], None, ALU.subtract)
                ins.then_inc(centered, 1)

            for g in G:
                src = mq.full(dve, ("l1", g)).rearrange("f (i p) -> f i p", i=GT)
                dst = lpad[:, HALO:HALO + T].rearrange("f (p i) -> f i p", i=NT)[:, g * GT:(g + 1) * GT, :]
                nc.vector.tensor_scalar(dst, src, column("b1"), None, ALU.add).then_inc(mq.emptied, 1)
            def recur(c):
                s = slice(c * GC, (c + 1) * GC)
                ma.taken(dve, ("i", c))
                link(nc.vector.tensor_tensor(ig[:, s], ig[:, s], lx[:, s], ALU.mult))
                dve.wait_ge(decay_ready, 3 * (c + 1))
                link(nc.vector.tensor_tensor(ig[:, s], ig[:, s], rb[:, s], ALU.mult))
                before = lx[:, c * GC - 1:c * GC] if c else 0.0
                link(nc.vector.tensor_tensor_scan(lx[:, s], ra[:, s], ig[:, s], before, ALU.mult, ALU.add))

            for n in range(3):
                k = slice(4 * n, min(4 * n + 4, K))
                src = mq.full(dve, ("taps", n))[:, 0:(k.stop - k.start) * P]
                if n == 2:
                    nc.vector.tensor_tensor(b_conv[:], mq.banks[mq.at[("taps", n)] % 2][:, P:P + 1],
                                            column("pw_b"), ALU.add)
                nc.vector.tensor_copy(w_conv[:, k, :], src.rearrange("p (k c) -> p k c", c=P)
                                      ).then_inc(mq.emptied, 1)
            def take_lx(c):
                src = mq.full(dve, ("lx", c))
                nc.vector.tensor_scalar(lx[:, c * GC:(c + 1) * GC], src, b_conv[:], None,
                                        ALU.add).then_inc(mq.emptied, 1)

            copy_out(tm, ("woC",), woC[:], NS, P)
            copy_out(tm, ("woD",), woD[:], P, P)
            ssm_copies(0, 4)
            normalise(h, skip, V_A, 0, scale=rstd, signal=False)
            normalise(h, skip, V_A, 1, scale=rstd, signal=False)
            take_lx(0)
            ssm_copies(4, 8)
            normalise(h, skip, V_A, 2, scale=rstd, signal=False)
            normalise(h, skip, V_A, 3, scale=rstd, signal=False)
            take_lx(1)
            centre_experts()
            recur(0)
            take_lx(2)
            ssm_copies(8, 12)
            recur(1)
            take_lx(3)
            recur(2)
            ssm_copies(12, NT)
            recur(3)
            prod = rg
            for g in G:
                s = slice(g * GT, (g + 1) * GT)
                nc.vector.tensor_tensor(prod[:, g * GC:(g + 1) * GC].rearrange("f (i p) -> f i p", i=GT),
                                        lx[:].rearrange("f (p i) -> f i p", i=NT)[:, s, :],
                                        gl[:, g * GC:(g + 1) * GC].rearrange("f (i p) -> f i p", i=GT),
                                        ALU.mult).then_inc(prod_ready, 1)
            for g in G:
                s = slice(g * GT, (g + 1) * GT)
                src = tm.full(dve, ("pT", g)).rearrange("p (i f) -> p i f", i=GT)
                nc.vector.tensor_tensor(skip[:, s, :], src, skip[:, s, :], ALU.add).then_inc(tm.emptied, 1)
                tm.taken(dve, ("pT", g))
                link(nc.vector.tensor_copy(qs[:, s], rstd[:, s]))
                dve.sem_inc(x1_ready, 1)
            for g in G:
                s = slice(g * GT, (g + 1) * GT)
                dve.wait_ge(ssq_ready, 2 * g + 2)
                link(nc.vector.tensor_scalar(qs[:, s], std[:, s], RMS_EPS, None, ALU.add))
                link(nc.vector.reciprocal(qs[:, s], qs[:, s]))
                for i in range(g * GT, (g + 1) * GT):
                    ins = nc.vector.tensor_scalar(xn[:, i, :], skip[:, i, :], qs[:, i:i + 1], SQD,
                                                  ALU.mult, ALU.mult)
                ins.then_inc(x_ready, 1)

            def take_out0(g):
                s = slice(g * GT, (g + 1) * GT)
                dve.wait_ge(base_ready, g + 1)
                src = tm.full(dve, ("out0", g)).rearrange("p (i f) -> p i f", i=GT)
                nc.vector.tensor_tensor(h[:, s, :], src, h[:, s, :], ALU.add).then_inc(tm.emptied, 1)
                tm.taken(dve, ("out0", g))
                stats(h, g)

            for g in G:
                for m in range(MULT):
                    n = g * MULT + m
                    dve.wait_ge(gelu_ready, n + 1)
                    src = mq.full(dve, ("wm1", g, m))
                    if m == 0 and g >= 2:
                        dve.wait_ge(tm.filled, tm.at[("out0", g - 2)] + 1)
                    nc.vector.scalar_tensor_tensor(
                        out=hidm[:, g % 2, m, :], in0=src, scalar=column(f"bm1_{m}"), in1=zc[:, n % 2, :],
                        op0=ALU.add, op1=ALU.mult).then_inc(mq.emptied, 1)
                if g >= 1:
                    take_out0(g - 1)
            take_out0(NG - 1)
            for g in G:
                normalise(h, xn, V_C, g)
            for g in G:
                src = tm.full(dve, ("logit0", g))[:, 0:GT * E0].rearrange("p (i e) -> p i e", i=GT)
                nc.vector.tensor_copy(lg0[:, g * GT:(g + 1) * GT, :], src).then_inc(tm.emptied, 1)
            tm.taken(dve, ("logit0", NG - 1))
            for i in I:
                mark(nc.vector.max(top[:, i, :], lg0[:, i, :]))
            settle()
            for i in I:
                mark(nc.vector.max_index(topi[:, i, :], top[:, i, :], lg0[:, i, :]))
            nc.vector.tensor_tensor(sm[:, 0, :], top[:, :, 1], top[:, :, 0], ALU.subtract).then_inc(exp0_ready, 1)
            settle()
            link(nc.vector.tensor_copy(topf[:], topi[:]))
            dve.wait_ge(exp0_act, 1)
            link(nc.vector.tensor_scalar(sm[:, 2, :], sm[:, 1, :], 1.0, None, ALU.add))
            link(nc.vector.reciprocal(sm[:, 2, :], sm[:, 2, :]))
            link(nc.vector.tensor_tensor(sm[:, 3, :], sm[:, 1, :], sm[:, 2, :], ALU.mult))

            def one_hot(dst, tmp, k, weight, n, keep=None):
                out_ = dst if k == 0 else tmp
                io = iota[:, 0:n].unsqueeze(1).to_broadcast([P, NT, n])
                hit = out_ if keep is None else keep
                link(nc.vector.tensor_tensor(hit, io, topf[:, :, k:k + 1].to_broadcast([P, NT, n]), ALU.is_equal))
                link(nc.vector.tensor_tensor(out_, hit, weight.to_broadcast([P, NT, n]), ALU.mult))
                if k:
                    link(nc.vector.tensor_tensor(dst, dst, tmp, ALU.add))

            comb0 = comb[:, :, 0:E0]
            for k in range(2):
                one_hot(comb0, hot[:, :, 0:E0], k, sm[:, 2 + k, :].unsqueeze(2), E0)
            dve.sem_inc(comb0_ready, 1)
            def take_y(n):
                if n >= YR:
                    dve.wait_ge(sd0_ready, (n - YR) // 2 + 1)
                    dve.wait_ge(v0_ready, n - YR + 1)
                src = tm.full(dve, ("y0", n // 2, n % 2))
                nc.vector.tensor_tensor(y_of(n), src, spread_row(ROW_B2 + 4 * (n % 2), 4),
                                        ALU.add).then_inc(tm.emptied, 1)

            take_after = (0, 2, 4, 5)

            def add_tiles(i):
                dve.wait_ge(sd0_ready, i + 2)
                dve.wait_ge(v0_ready, 2 * (i + 2))
                link(nc.vector.reciprocal(sc[:, i:i + 2, :], ss[:, i:i + 2, :]))
                link(nc.vector.tensor_tensor(sc[:, i:i + 2, :], sc[:, i:i + 2, :], comb[:, i:i + 2, 0:E0], ALU.mult))
                for e in range(E0):
                    for t in (i, i + 1):
                        z = z_of(2 * t + e // 4)[:, (e % 4) * P:(e % 4 + 1) * P]
                        if e:
                            dve.wait_ge(dve_step, steps[0] - 1)
                        mark(nc.vector.scalar_tensor_tensor(out=h[:, t, :], in0=z, scalar=sc[:, t, e:e + 1],
                                                            in1=h[:, t, :], op0=ALU.mult, op1=ALU.add))
                    if e in take_after and i + 2 < NT:
                        take_y(2 * (i + 2) + take_after.index(e))
                settle()
                dve.sem_inc(moe_ready, 2)

            for n in range(4):
                take_y(n)
            for g in G:
                s = slice(g * GT, (g + 1) * GT)
                src = tm.full(dve, ("beta0", g)).rearrange("p (i f) -> p i f", i=GT)
                nc.vector.tensor_tensor(h[:, s, :], src, h[:, s, :], ALU.add).then_inc(tm.emptied, 1)
            tm.taken(dve, ("beta0", NG - 1))
            for i in range(0, NT, 2):
                add_tiles(i)
                if i % GT:
                    stats(h, i // GT)
                elif i:
                    normalise(h, xn, V_D, i // GT - 1)
            def take_hm(g):
                s = slice(g * GT, (g + 1) * GT)
                src = tm.full(dve, ("hm", g)).rearrange("p (i f) -> p i f", i=GT)
                nc.vector.tensor_tensor(skip[:, s, :], src,
                                        spread_row(ROW_BI).unsqueeze(1).to_broadcast([P, GT, P]),
                                        ALU.add).then_inc(tm.emptied, 1)
                tm.taken(dve, ("hm", g))
                stats(skip, g)

            take_hm(0)
            normalise(h, xn, V_D, NG - 1)
            take_hm(1)
            take_hm(2)
            normalise(skip, xn, V_U, 0)
            take_hm(3)
            normalise(skip, xn, V_U, 1)
            normalise(skip, xn, V_U, 2)
            normalise(skip, xn, V_U, 3)
            mq.taken(dve, ("state", NT - 1))
            mark(nc.vector.tensor_copy(carry[:, 1:P + 1], st[:, NT - 1, :]))
            settle()
            dve.sem_inc(carry_ready, 1)
            for k in range(SCAN_LEVELS):
                w = P - 2 ** k
                src = mq.full(dve, ("carry", k))
                nc.vector.tensor_tensor(carry[:, 1 + 2 ** k:P + 1], carry[:, 1 + 2 ** k:P + 1],
                                        src[0:NS, 0:w], ALU.add).then_inc(mq.emptied, 1)
                mq.taken(dve, ("carry", k))
            for g in G:
                s = slice(g * GT, (g + 1) * GT)
                dve.wait_ge(h2_base, g + 1)
                src = tm.full(dve, ("y_ssm", g)).rearrange("p (i f) -> p i f", i=GT)
                nc.vector.tensor_tensor(h[:, s, :], src, h[:, s, :], ALU.add).then_inc(tm.emptied, 1)
                tm.taken(dve, ("y_ssm", g))
                stats(h, g)
                if g >= 1:
                    normalise(h, xn, V_E, g - 1)
            def take_shared(g):
                s = slice(g * GT, (g + 1) * GT)
                src = tm.full(dve, ("y1", g)).rearrange("p (i f) -> p i f", i=GT)
                nc.vector.scalar_tensor_tensor(out=h[:, s, :], in0=src, scalar=1.0 / SHARED, in1=h[:, s, :],
                                               op0=ALU.mult, op1=ALU.add).then_inc(tm.emptied, 1)

            normalise(h, xn, V_E, NG - 1)
            for g in G:
                src = tm.full(dve, ("logit1", g))[:, 0:GT * E1].rearrange("p (i e) -> p i e", i=GT)
                nc.vector.tensor_copy(lg1[:, g * GT:(g + 1) * GT, :], src).then_inc(tm.emptied, 1)
            tm.taken(dve, ("logit1", NG - 1))
            link(nc.vector.tensor_reduce(sm[:, 0, :], lg1[:], AX.X, ALU.max))
            nc.vector.tensor_tensor(lg1[:], lg1[:], sm[:, 0, :].unsqueeze(2).to_broadcast([P, NT, E1]),
                                    ALU.subtract).then_inc(exp1_dve, 1)
            dve.wait_ge(exp1_act, 1)
            link(nc.vector.tensor_reduce(sm[:, 1, :], lg1[:], AX.X, ALU.add))
            link(nc.vector.reciprocal(sm[:, 1, :], sm[:, 1, :]))
            link(nc.vector.tensor_tensor(lg1[:], lg1[:], sm[:, 1, :].unsqueeze(2).to_broadcast([P, NT, E1]),
                                         ALU.mult))
            for i in I:
                mark(nc.vector.max(top[:, i, :], lg1[:, i, :]))
            settle()
            for i in I:
                mark(nc.vector.max_index(topi[:, i, :], top[:, i, :], lg1[:, i, :]))
            settle()
            link(nc.vector.tensor_copy(topf[:], topi[:]))
            link(nc.vector.tensor_copy(sm[:, 2, :], top[:, :, 0]))
            nc.vector.tensor_tensor(top[:, :, 0:TOP1], top[:, :, 0:TOP1],
                                    sm[:, 2, :].unsqueeze(2).to_broadcast([P, NT, TOP1]),
                                    ALU.subtract).then_inc(exp1_dve, 1)
            dve.wait_ge(exp1_act, 2)
            link(nc.vector.tensor_reduce(sm[:, 3, :], top[:, :, 0:TOP1], AX.X, ALU.add))
            link(nc.vector.reciprocal(sm[:, 3, :], sm[:, 3, :]))
            link(nc.vector.tensor_tensor(top[:, :, 0:TOP1], top[:, :, 0:TOP1],
                                         sm[:, 3, :].unsqueeze(2).to_broadcast([P, NT, TOP1]), ALU.mult))
            comb1 = comb[:, :, 0:E1]
            for k in range(TOP1):
                one_hot(comb1, hot[:], k, top[:, :, k:k + 1], E1, choice[:, k])
            dve.sem_inc(comb1_ready, 1)
            link(nc.vector.tensor_tensor(hot[:], choice[:, 0], choice[:, 1], ALU.add))
            link(nc.vector.tensor_tensor(hot[:], hot[:], choice[:, 2], ALU.add))
            nc.vector.tensor_tensor(chosen[:], hot[:], choice[:, 3], ALU.add).then_inc(chosen_ready, 1)
            nc.vector.tensor_copy(x_row[:, :, R_COMB:], comb[:, :, 0:E1]).then_inc(rows_ready, 1)
            mark(nc.vector.memset(cnt[:, 5, :], 1.0))
            take_shared(0)
            src = tm.full(dve, ("rank",))
            mark(nc.vector.tensor_copy(rank[:], src[:, 0:NT * E1].rearrange("p (i e) -> p i e", i=NT)))
            nc.vector.tensor_scalar(cnt[:, 0, :], src[:, NT * E1:NT * E1 + E1], float(P - 1), None,
                                    ALU.add).then_inc(tm.emptied, 1)
            tm.taken(dve, ("rank",))
            link(nc.vector.tensor_copy(cnt_i[:], cnt[:, 0, :]))
            link(nc.vector.tensor_scalar(cnt_i[:], cnt_i[:], P.bit_length() - 1, None, ALU.arith_shift_right))
            link(nc.vector.tensor_copy(cnt[:, 1, :], cnt_i[:]))
            link(nc.vector.tensor_tensor_scan(cnt[:, 2, :], cnt[:, 5, :], cnt[:, 1, :], 0.0, ALU.mult, ALU.add))
            link(nc.vector.tensor_tensor(cnt[:, 3, :], cnt[:, 2, :], cnt[:, 1, :], ALU.subtract))
            link(nc.vector.tensor_scalar(cnt[:, 4, :], cnt[:, 3, :], float(P), None, ALU.mult))
            link(nc.vector.tensor_tensor(rank[:], rank[:], cnt[:, 4, :].unsqueeze(1).to_broadcast([P, NT, E1]),
                                         ALU.add))
            for k in range(TOP1):
                mark(nc.vector.tensor_tensor(choice[:, k], choice[:, k], rank[:], ALU.mult))
            settle()
            link(nc.vector.tensor_reduce(slot_f[:], choice[:], AX.X, ALU.add))
            link(nc.vector.tensor_copy(slot[:], slot_f[:]))
            link(nc.vector.tensor_scalar(slot_bits[:], slot[:], P.bit_length() - 1, None, ALU.arith_shift_right))
            mark(nc.vector.tensor_copy(stile[:], slot_bits[:]))
            settle()
            nc.vector.scalar_tensor_tensor(out=spos[:], in0=stile[:], scalar=-float(P), in1=slot_f[:],
                                           op0=ALU.mult, op1=ALU.add).then_inc(pos_ready, 1)
            dve.wait_ge(pos_ready, 1)
            for i in I:
                if i >= 4:
                    dve.wait_ge(list_done, i - 3)
                for k in range(TOP1 // 2, TOP1):
                    nc.vector.tensor_scalar(tile_hot[:, i % 4, k, :], tile_no, stile[:, k, i:i + 1],
                                            id1[:, i:i + 1], ALU.is_equal, ALU.mult)
                for k in range(TOP1):
                    ins = nc.vector.tensor_scalar(pos_hot[:, i % 4, k, :], pos_no, spos[:, k, i:i + 1], None,
                                                  ALU.is_equal)
                ins.then_inc(pos_hot_ready, 1)
                if i == 3:
                    take_shared(1)
            take_shared(2)
            link(nc.vector.tensor_tensor(past[:], tile_no[0:1, :].unsqueeze(2).to_broadcast([1, RT, E1]),
                                         cnt[0:1, 2, :].unsqueeze(1).to_broadcast([1, RT, E1]), ALU.is_ge))
            link(nc.vector.tensor_reduce(expert_f[:], past[:], AX.X, ALU.add))
            link(nc.vector.tensor_scalar(expert_of[:], expert_f[:], float(E1 - 1), None, ALU.min))
            tr.taken(dve, ("list",))
            link(nc.vector.tensor_scalar(unused[:], list_f[:], 0.0, spare1, ALU.is_equal, ALU.mult))
            link(nc.vector.scalar_tensor_tensor(out=list_f[:], in0=list_f[:], scalar=-1.0, in1=unused[:],
                                                op0=ALU.add, op1=ALU.add))
            nc.vector.tensor_copy(slot_list[:], list_f[:]).then_inc(slot_ready, 1)
            dve.wait_ge(slot_ready, 1)
            loaded = {}

            def expert(n, k):
                if (n, id(k)) not in loaded:
                    loaded[n, id(k)] = dve.value_load(expert_of[0:1, bass.ds(n + k * XRING, 1)],
                                                      min_val=0, max_val=E1 - 1)
                return loaded[n, id(k)]

            def step(s, k):
                n = s + LEAD
                if 0 <= n < RT:
                    e = expert(n, k)
                    if n >= 2 or not isinstance(k, int):
                        dve.wait_ge(rt_filled, n - 1 + k * XRING)
                    nc.vector.tensor_copy(w1_in[:, n % 2, :], w_e1_all[:, bass.ds(e * FH, FH)])
                    dve.wait_ge(rx_filled, n + 1 + k * XRING)
                    nc.vector.tensor_copy(xinT[:, n % 2, :], bank[n % 2][:, 0:P]).then_inc(rx_emptied, 1)
                n = s
                if n >= 0:
                    a = n % NACC
                    e = expert(n, k)
                    dve.wait_ge(ry_filled, n + 1 + k * XRING)
                    if n >= NACC or not isinstance(k, int):
                        dve.wait_ge(summed[a], 16 * (n // NACC + k * (XRING // NACC)))
                    nc.vector.tensor_scalar(yout[:, a, :], bank[6 + n % 2][:, 0:P],
                                            xin[:, n % XRING, bass.ds(e + R_COMB, 1)], None,
                                            ALU.mult).then_inc(ry_emptied, 1)
                n = s + GLEAD + 1
                if n < RT:
                    if n >= BODY or not isinstance(k, int):
                        dve.wait_ge(summed[n % NACC], 16 * (n // NACC + 1 + (k - 2) * (XRING // NACC)))
                    nc.vector.tensor_copy(ids_in[:, n % BODY:n % BODY + 1],
                                          slot_list[:, bass.ds(n + k * XRING, 1)]).then_inc(ids_ready, 1)

            for s in range(-GLEAD - 1, -LEAD):
                step(s, 0)
            take_shared(3)
            for g in G:
                s = slice(g * GT, (g + 1) * GT)
                src = tm.full(dve, ("b2", g)).rearrange("p (i f) -> p i f", i=GT)
                nc.vector.tensor_tensor(h[:, s, :], src, h[:, s, :], ALU.add).then_inc(tm.emptied, 1)
            tm.taken(dve, ("b2", NG - 1))
            dve.wait_ge(ld_w1, 16)
            routed_steps(dve, step)
            total = h[:].rearrange("p i d -> p (i d)")
            for a in sums_order:
                for n, half in enumerate(halves):
                    dve.wait_ge(ld_sum[a][n], 16)
                    ins = nc.vector.tensor_tensor(total[:, half], total[:, half], sum_in[a][:, half], ALU.add)
                    if a != sums_order[-1]:
                        link(ins)
                    else:
                        ins.then_inc(total_ready, 1)

        @block.tensor
        def _(pe):
            def mm(out_, lhsT, rhs, start=True, stop=True):
                return nc.tensor.matmul(out_, lhsT, rhs, start=start, stop=stop)

            def transpose_group(key, g, first):
                pe.wait_ge(x_ready, first + g + 1)
                dst = tr.fill(pe, (key, g))
                for j in range(GT):
                    ins = nc.tensor.transpose(dst[:, j * P:(j + 1) * P], xn[:, g * GT + j, :], ident[:])
                ins.then_inc(tr.filled, 1)

            pe.wait_ge(ld_const, 64)
            for g in G:
                transpose_group("xT_a", g, X_A)
            pe.wait_ge(ld_attn, 32)
            for g in G:
                tr.taken(pe, ("xT_a", g))
                x = xT[:, g * GC:(g + 1) * GC]
                mm(mq.fill(pe, ("l1", g)), w_attn[:, 0, :], x).then_inc(mq.filled, 1)
                mm(ma.fill(pe, ("l2", g)), w_attn[:, 1, :], x).then_inc(ma.filled, 1)
            for n in range(3):
                dst = mq.fill(pe, ("taps", n))
                for k in range(4 * n, min(4 * n + 4, K)):
                    ins = mm(dst[:, (k - 4 * n) * P:(k - 4 * n + 1) * P], w_dw[:, k, :], w_attn[:, 2, :])
                if n == 2:
                    ins = mm(dst[:, P:P + 1], w_attn[:, 2, :], column("dw_b"))
                ins.then_inc(mq.filled, 1)
            mq.taken(pe, ("taps", 2))
            pe.wait_ge(ld_ssm, 96)
            A, AT = w_a[:, 0:NS], w_a[:, NS:2 * NS]
            dst = tm.fill(pe, ("woC",))
            mm(dst[0:NS, 0:P], w_c[:], w_oT[:]).then_inc(tm.filled, 1)
            dst = tm.fill(pe, ("woD",))
            mm(dst[:, 0:P], w_d[:], w_oT[:]).then_inc(tm.filled, 1)
            def ssm_products(lo, hi):
                for i in range(lo, hi):
                    tm.taken(pe, ("q", i - 1) if i else ("woC",))
                    dst = tm.fill(pe, ("q", i))
                    mm(dst[0:NS, 0:P], A, qT[:, i - 1, :] if i else woC[:]).then_inc(tm.filled, 1)
                    if i < POW_LEVELS:
                        if i:
                            tm.taken(pe, ("pow", i - 1))
                        N, NT_ = (A, AT) if i == 0 else (powers[:, i, 0:NS], powers[:, i, NS:2 * NS])
                        dst = tm.fill(pe, ("pow", i))
                        mm(dst[0:NS, 0:NS], NT_, N)
                        mm(dst[0:NS, NS:2 * NS], N, NT_).then_inc(tm.filled, 1)

            for c in range(NG + 1):
                for k in range(K):
                    if c in SSM_AT and k % 2 == 1:
                        i = 4 * SSM_AT.index(c) + k // 2
                        ssm_products(i, i + 1)
                    if c < NG:
                        dst = mq.fill(pe, ("lx", c)) if k == 0 else dst
                        ins = mm(dst, w_conv[:, k, :], lpad[:, c * GC + k:c * GC + k + GC], k == 0, k == K - 1)
                    if c >= 1 and k == 2:
                        mq.taken(pe, ("lx", c - 1))
                        x = lx[:, (c - 1) * GC:c * GC]
                        mm(ma.fill(pe, ("r", c - 1)), w_attn[:, 4, :], x).then_inc(ma.filled, 1)
                        mm(ma.fill(pe, ("i", c - 1)), w_attn[:, 3, :], x).then_inc(ma.filled, 1)
                if c < NG:
                    ins.then_inc(mq.filled, 1)
            ssm_products(4 * len(SSM_AT), NT)
            for g in G:
                pe.wait_ge(prod_ready, g + 1)
                dst = tm.fill(pe, ("pT", g))
                for j in range(GT):
                    i = g * GT + j
                    ins = nc.tensor.transpose(dst[:, j * P:(j + 1) * P], rg[:, i * P:(i + 1) * P], ident[:])
                ins.then_inc(tm.filled, 1)
            for g in G:
                transpose_group("xT_b", g, X_B)
            pe.wait_ge(ld_ff, 32)
            for g in range(NG + 1):
                if g < NG:
                    tr.taken(pe, ("xT_b", g))
                if g >= 1:
                    dst = tm.fill(pe, ("out0", g - 1))
                for j in range(MULT):
                    if g < NG:
                        mm(mq.fill(pe, ("wm1", g, j)), w_m1[:, j * P:(j + 1) * P],
                           xT[:, g * GC:(g + 1) * GC]).then_inc(mq.filled, 1)
                    if g >= 1:
                        mq.taken(pe, ("wm1", g - 1, MULT - 1))
                        for m in range(MULT):
                            ins = mm(dst[:, j * P:(j + 1) * P], hidm[:, (g - 1) % 2, m, j * P:(j + 1) * P],
                                     w_m2[:, m, :], m == 0, m == MULT - 1)
                if g >= 1:
                    ins.then_inc(tm.filled, 1)
            for g in G:
                transpose_group("xT_c", g, X_C)
            pe.wait_ge(ld_moe, 96)
            for g in G:
                tr.taken(pe, ("xT_c", g))
                dst = tm.fill(pe, ("logit0", g))
                for j in range(GT):
                    i = g * GT + j
                    ins = mm(dst[:, j * E0:(j + 1) * E0], xT[:, i * P:(i + 1) * P], w_g0[:])
                ins.then_inc(tm.filled, 1)

            def combine_transposed(key, n, ready):
                pe.wait_ge(ready, 1)
                for g in G:
                    dst = tr.fill(pe, (key, g))
                    for j in range(GT):
                        ins = nc.tensor.transpose(dst[0:n, j * P:(j + 1) * P], comb[:, g * GT + j, 0:n], ident[:])
                    ins.then_inc(tr.filled, 1)

            def weighted_rows(key, ckey, n, w):
                for g in G:
                    tr.taken(pe, (ckey, g))
                    dst = tm.fill(pe, (key, g))
                    for j in range(GT):
                        i = g * GT + j
                        ins = mm(dst[:, j * P:(j + 1) * P], combT[0:n, i * P:(i + 1) * P], w[:])
                    ins.then_inc(tm.filled, 1)

            def hidden0(g, e):
                mm(ma.fill(pe, ("hid0", g, e)), w_e1[:, e, :], xT[:, g * GC:(g + 1) * GC]).then_inc(ma.filled, 1)

            def outputs0(i):
                for half in range(2):
                    dst = tm.fill(pe, ("y0", i, half))
                    for q in range(4):
                        e = 4 * half + q
                        ins = mm(dst[:, q * P:(q + 1) * P],
                                 hid0[:, (i // GT) % 2, e, (i % GT) * P:(i % GT + 1) * P], w_e2[:, e, :])
                    ins.then_inc(tm.filled, 1)

            for e in range(E0):
                hidden0(0, e)
            pe.wait_ge(centered, 1)
            for g in G:
                ma.taken(pe, ("hid0", g, E0 - 1))
                for j in range(GT):
                    outputs0(g * GT + j)
                    if g + 1 < NG:
                        hidden0(g + 1, 2 * j)
                        hidden0(g + 1, 2 * j + 1)
                    if g * GT + j == 1:
                        combine_transposed("combT0", E0, comb0_ready)
                        weighted_rows("beta0", "combT0", E0, w_beta)
            def project(g):
                tr.taken(pe, ("xT_d", g))
                dst = tm.fill(pe, ("hm", g))
                for j in range(GT):
                    i = g * GT + j
                    ins = mm(dst[:, j * P:(j + 1) * P], xT[:, i * P:(i + 1) * P], w_iT[:])
                ins.then_inc(tm.filled, 1)

            transpose_group("xT_d", 0, X_D)
            transpose_group("xT_d", 1, X_D)
            project(0)
            transpose_group("xT_d", 2, X_D)
            project(1)
            project(2)
            transpose_group("xT_d", 3, X_D)
            project(3)
            transpose_group("uT", 0, X_U)
            for i in I:
                if i % GT == 0:
                    if i // GT + 1 < NG:
                        transpose_group("uT", i // GT + 1, X_U)
                    tr.taken(pe, ("uT", i // GT))
                dst = mq.fill(pe, ("state", i))[0:NS, 0:P]
                ins = mm(dst, w_bT[:], xT[:, i * P:(i + 1) * P], True, i == 0)
                if i:
                    mq.taken(pe, ("state", i - 1))
                    ins = mm(dst, AT, st[:, i - 1, :], False, True)
                ins.then_inc(mq.filled, 1)

            out_bank = {}

            def local_outputs(i):
                g, j = i // GT, i % GT
                if j == 0:
                    out_bank[g] = tm.fill(pe, ("y_ssm", g))
                d = out_bank[g][:, j * P:(j + 1) * P]
                nc.tensor.matmul(d, xT[:, i * P:(i + 1) * P], woD[:], start=(j == 0), stop=False,
                                 skip_group_check=True)
                nc.tensor.matmul(d, st[:, i, :], woC[:], start=False, stop=False, skip_group_check=True)

            def carried_outputs(g):
                for j in range(GT):
                    ins = nc.tensor.matmul(out_bank[g][:, j * P:(j + 1) * P], carry[:, 0:P],
                                           qT[:, g * GT + j, :], start=False, stop=(j == GT - 1),
                                           skip_group_check=True)
                ins.then_inc(tm.filled, 1)

            mq.taken(pe, ("state", NT - 1))
            pe.wait_ge(carry_ready, 1)
            for k in range(SCAN_LEVELS):
                if k:
                    mq.taken(pe, ("carry", k - 1))
                w = P - 2 ** k
                mm(mq.fill(pe, ("carry", k))[0:NS, 0:w], powers[:, 4 + k, NS:2 * NS],
                   carry[:, 1:1 + w]).then_inc(mq.filled, 1)
                local_outputs(k)
            local_outputs(SCAN_LEVELS)
            mq.taken(pe, ("carry", SCAN_LEVELS - 1))
            for g in G:
                if g >= 2:
                    for i in range(g * GT, (g + 1) * GT):
                        local_outputs(i)
                carried_outputs(g)
            for g in range(NG + 1):
                if g < NG:
                    transpose_group("xT_e", g, X_E)
                if g >= 1:
                    tr.taken(pe, ("xT_e", g - 1))
                    dst = tm.fill(pe, ("logit1", g - 1))
                    for j in range(GT):
                        i = (g - 1) * GT + j
                        ins = mm(dst[:, j * E1:(j + 1) * E1], xT[:, i * P:(i + 1) * P], w_g1[:])
                    ins.then_inc(tm.filled, 1)
            def hidden1(g, e):
                for f in range(FC):
                    mm(ma.fill(pe, ("hid1", g, e, f)), w_sh1[:, e, f * P:(f + 1) * P],
                       xT[:, g * GC:(g + 1) * GC]).then_inc(ma.filled, 1)

            def ranks():
                pe.wait_ge(chosen_ready, 1)
                dst = tm.fill(pe, ("rank",))
                mm(dst[:, 0:NT * E1], tri[:], chosen[:].rearrange("p i e -> p (i e)"), True, False)
                for d in range(1, NT):
                    mm(dst[:, d * E1:NT * E1], ones[:], chosen[:, 0:NT - d, :].rearrange("p i e -> p (i e)"),
                       False, d == NT - 1)
                for i in I:
                    ins = mm(dst[:, NT * E1:(NT + 1) * E1], ones[:], chosen[:, i, :], i == 0, i == NT - 1)
                ins.then_inc(tm.filled, 1)

            def list_tiles(lo, hi):
                for i in range(lo, hi):
                    dst = tr.fill(pe, ("list",)) if i == 0 else tr.banks[tr.at[("list",)] % 2]
                    pe.wait_ge(pos_hot_ready, i + 1)
                    pe.wait_ge(tile_hot_ready, i + 1)
                    for k in range(TOP1):
                        ins = mm(dst[:, 0:RT], pos_hot[:, i % 4, k, :], tile_hot[:, i % 4, k, :],
                                 i == 0 and k == 0, i == NT - 1 and k == TOP1 - 1)
                    ins.then_inc(tr.filled if i == NT - 1 else list_done, 1)

            pe.wait_ge(ld_shared, 80)
            hidden1(0, 0)
            for g in G:
                dst = tm.fill(pe, ("y1", g))
                for e in range(SHARED):
                    n = g * SHARED + e
                    if n + 1 < SHARED * NG:
                        hidden1((n + 1) // SHARED, (n + 1) % SHARED)
                    ma.taken(pe, ("hid1", g, e, FC - 1))
                    for j in range(GT):
                        for f in range(FC):
                            ins = nc.tensor.matmul(
                                dst[:, j * P:(j + 1) * P], hid1[:, n % 2, f, j * P:(j + 1) * P],
                                w_sh2[:, e, f * P:(f + 1) * P], start=(e == 0 and j == 0 and f == 0),
                                stop=(e == SHARED - 1 and j == GT - 1 and f == FC - 1), skip_group_check=True)
                    if e < SHARED - 1:
                        ins.then_inc(hid1_used, 1)
                        if g == 2:
                            list_tiles(6, 12)
                ins.then_inc(tm.filled, 1)
                if g == 0:
                    ranks()
                if g == 1:
                    list_tiles(0, 6)
                if g == 2:
                    list_tiles(12, NT)
            combine_transposed("combT1", ES, comb1_ready)
            weighted_rows("b2", "combT1", ES, w_b2)
            pe.wait_ge(slot_ready, 1)
            pe.wait_ge(tr.emptied, len(tr.at))

            def free(emptied, n, k):
                if n >= 2 or not isinstance(k, int):
                    pe.wait_ge(emptied, n - 1 + k * XRING)

            def step(s, k):
                n = s + LEAD
                if n < RT:
                    pe.wait_ge(gathered_in[n % XRING], 16 * (n // XRING + 1 + k))
                    free(rx_emptied, n, k)
                    nc.tensor.transpose(bank[n % 2][:, 0:P], xin[:, n % XRING, 0:P],
                                        ident[:]).then_inc(rx_filled, 1)
                n = s + 1
                if 0 <= n < RT:
                    pe.wait_ge(rx_emptied, n + 1 + k * XRING)
                    free(rt_emptied, n, k)
                    for f in range(FC):
                        ins = mm(bank[4 + n % 2][:, f * P:(f + 1) * P], w1_in[:, n % 2, f * P:(f + 1) * P],
                                 xinT[:, n % 2, :])
                    ins.then_inc(rt_filled, 1)
                if s == 0 and isinstance(k, int):
                    pe.wait_ge(ld_w2, 16)
                    pe.wait_ge(tm.emptied, len(tm.at))
                n = s
                if n >= 0:
                    e = pe.value_load(expert_of[0:1, bass.ds(n + k * XRING, 1)], min_val=0, max_val=E1 - 1)
                    pe.wait_ge(rt_emptied, n + 1 + k * XRING)
                    free(ry_emptied, n, k)
                    for f in range(FC):
                        ins = mm(bank[6 + n % 2][:, 0:P], hT[:, n % 2, f, :],
                                 w_e2_all[:, bass.ds(e * FH + f * P, P)], f == 0, f == FC - 1)
                    ins.then_inc(ry_filled, 1)

            routed_steps(pe, step)


def kernel(**inputs):
    import ml_dtypes
    import numpy as np
    import concourse.bacc as bacc
    from concourse.bass_utils import run_bass_kernel_spmd

    x = {k: np.asarray(v) for k, v in inputs.items()}
    c = np.ascontiguousarray
    consts = np.zeros((P, P + E1), np.float32)
    consts[:, :P] = np.eye(P)
    consts[:, P:] = np.arange(E1)
    vec = ["g", "b1", "b2", "dw_b", "pw_b", "bi", "br", "lam"]
    cols = [x[f"L0_attn_{v}"] for v in vec] + list(x["L0_attn_bm1"].reshape(MULT, P))
    cols += [x["L1_attn_gamma"], x["L1_attn_beta"]] + list(x["L0_ffn_b1"])
    rows = [x["L0_attn_bm2"], x["L1_attn_bi"], x["L1_attn_bo"], *x["L0_ffn_b2"], *x["L0_ffn_gamma"]]
    w1 = np.concatenate([x["L1_ffn_re_w1"], x["L1_ffn_se_w1"]])
    w2 = np.concatenate([x["L1_ffn_re_w2"], x["L1_ffn_se_w2"]])
    b1 = np.concatenate([x["L1_ffn_re_b1"], x["L1_ffn_se_b1"]])
    numbers = np.concatenate([np.arange(T).reshape(P, NT) + 1, T + 1 + np.arange(P)[:, None],
                              np.tile(np.arange(P), (P, 1)), np.tile(np.arange(RT), (P, 1))], axis=1)
    ids = np.zeros((P, NT + 2), x["x"].dtype)
    ids[:, 1:NT + 1] = x["x"].reshape(P, NT)
    ids[1:, 0] = ids[:-1, NT]
    ids[:-1, NT + 1] = ids[1:, 1]
    arrays = {
        "ids": ids,
        "table": c(x["L0_tok_conv_w"].transpose(1, 2, 0).reshape(-1, TAPS0 * P)),
        "consts": consts,
        "cols": c(np.stack(cols, axis=1)),
        "rows": c(np.concatenate(rows)),
        "attn_w": c(np.stack([x["L0_attn_W1"], x["L0_attn_W2"], x["L0_attn_pw_w"][:, :, 0].T,
                              x["L0_attn_Wi"], x["L0_attn_Wr"]], axis=1)),
        "dw_w": c(x["L0_attn_dw_w"].transpose(0, 2, 1)),
        "wm1": x["L0_attn_Wm1"],
        "wm2": c(x["L0_attn_Wm2"].reshape(MULT, P, P).transpose(1, 0, 2)),
        "moe_wg": x["L0_ffn_Wg"],
        "moe_w1": c(x["L0_ffn_W1"].transpose(1, 0, 2)),
        "moe_w2": c(x["L0_ffn_W2"].transpose(1, 0, 2)),
        "moe_beta": x["L0_ffn_beta"],
        "ssm_a": c(np.concatenate([x["L1_attn_A"], x["L1_attn_A"].T], axis=1)),
        "ssm_bT": c(x["L1_attn_Bm"].T),
        "ssm_c": x["L1_attn_Cm"],
        "ssm_d": x["L1_attn_Dm"],
        "ssm_wiT": c(x["L1_attn_Wi"].T),
        "ssm_woT": c(x["L1_attn_Wo"].T),
        "gate_wT": c(x["L1_ffn_gate_w"].T),
        "ffn_w1": c(w1.transpose(1, 0, 2)),
        "ffn_w2": c(w2.reshape(ES, FC, P, P).transpose(2, 0, 1, 3).reshape(P, ES, FH)),
        "ffn_b1": c(b1.reshape(ES * FC, P).T),
        "ffn_b2": c(np.concatenate([x["L1_ffn_re_b2"], x["L1_ffn_se_b2"]])),
        "consts_bf": np.concatenate([np.triu(np.ones((P, P)), 1), np.ones((P, P))], axis=1).astype(ml_dtypes.bfloat16),
        "slot_consts": numbers.astype(np.float32),
    }
    nc = bacc.Bacc("TRN2", target_bir_lowering=False, num_devices=1)
    args = [nc.dram_tensor(f"in_{k}", a.shape, mybir.dt.from_np(a.dtype), kind="ExternalInput").ap()
            for k, a in arrays.items()]
    args.append(nc.dram_tensor("rows", (T + P, RW), F32, kind="Internal").ap())
    args.append([nc.dram_tensor(f"sums{a}", (T + P, P), F32, kind="Internal").ap() for a in range(NACC)])
    args.append(nc.dram_tensor("out", (1, T, P), F32, kind="ExternalOutput").ap())
    lm_tower_kernel(nc, *args)
    r = run_bass_kernel_spmd(nc, [{f"in_{k}": a for k, a in arrays.items()}], core_ids=[0])
    return r.results[0]["out"]
```
